# Optimizing a Trainium2 kernel written in Bass

```python
import numpy as np
import jax
import jax.numpy as jnp

def _softmax(x, axis=-1):
    return jax.nn.softmax(x, axis=axis)

def _gelu(x):
    return jax.nn.gelu(x, approximate=True)

def _silu(x):
    return jax.nn.silu(x)

def _sigmoid(x):
    return jax.nn.sigmoid(x)

def _layernorm(x, axis=-1, eps=1e-05):
    m = jnp.mean(x, axis=axis, keepdims=True)
    v = jnp.var(x, axis=axis, keepdims=True)
    return (x - m) / jnp.sqrt(v + eps)

def _scatter_add(tgt, idx, src, axis=0):
    return tgt.at[idx].add(src)

def _segment_sum(src, seg, n):
    return jax.ops.segment_sum(src, seg, n)
kernel_name = 'mk_xattn_ffn_d2_seqx_r8_b73f66'

def setup_inputs(seed: int=0):
    np.random.seed(seed)
    _w = jnp.asarray

    def _rec_inputs():
        import jax
        import jax.numpy as jnp
        _rk = jax.random.key(seed)
        x = 0.002226 + 0.9996 * jax.random.normal(jax.random.fold_in(_rk, 1), (4, 512, 128), jnp.float32)
        _lenS = 512 - jax.random.randint(jax.random.fold_in(_rk, 7), (4,), 0, max(1, 512 // 4) + 1, jnp.int32)
        _lenS2 = 154 - jax.random.randint(jax.random.fold_in(_rk, 8), (4,), 0, max(1, 154 // 4) + 1, jnp.int32)
        _ctx_1024P = jax.random.normal(jax.random.fold_in(_rk, 11), (4, 16, 128), jnp.float32)
        _ctx_1024c = jax.random.dirichlet(jax.random.fold_in(_rk, 511), 0.3 * jnp.ones((16,), jnp.float32), (4, 154))
        _ctx_1024t = jnp.einsum('bsk,bkd->bsd', _ctx_1024c, _ctx_1024P)
        _ctx_1024t = _ctx_1024t * jax.lax.rsqrt(jnp.mean(jnp.square(_ctx_1024t)) + 1e-12) * 0.953939
        ctx_1024 = -0.000125008 + 0.999885 * (_ctx_1024t + 0.3 * jax.random.normal(jax.random.fold_in(_rk, 611), (4, 154, 128), jnp.float32))
        _validS = jnp.arange(512)[None, :] < _lenS[:, None]
        _validS2 = jnp.arange(154)[None, :] < _lenS2[:, None]
        _causal = jnp.tril(jnp.ones((512, 512), dtype=bool))
        mask_Bx1x1xS2_ik0 = jnp.where(jnp.broadcast_to(_validS2[:, None, None, :], (4, 1, 1, 154)), 0, 1).astype(jnp.int32)
        return (x, ctx_1024, mask_Bx1x1xS2_ik0)
    x, ctx_1024, mask_Bx1x1xS2_ik0 = _rec_inputs()

    def _L0_xattn_setup():
        import jax, jax.numpy as jnp
        import numpy as np
        DIM = 128
        HEADS = 16
        DIM_HEAD = 64
        INNER = HEADS * DIM_HEAD
        EPS = 1e-05

        def _layernorm(t, w, b):
            mu = jnp.mean(t, axis=-1, keepdims=True)
            var = jnp.mean(jnp.square(t - mu), axis=-1, keepdims=True)
            return (t - mu) * jax.lax.rsqrt(var + EPS) * w + b
        key = jax.random.key(seed)
        ks = jax.random.split(key, 8)
        b, n, l = (8, 512, 64)
        x = jax.random.normal(ks[0], (b, n, DIM), dtype=jnp.float32)
        latents = jax.random.normal(ks[1], (b, l, DIM), dtype=jnp.float32)
        ln1_w = jnp.ones((DIM,), jnp.float32)
        ln1_b = jnp.zeros((DIM,), jnp.float32)
        ln2_w = jnp.ones((DIM,), jnp.float32)
        ln2_b = jnp.zeros((DIM,), jnp.float32)
        Wq = jax.random.normal(ks[2], (DIM, INNER), dtype=jnp.float32) / np.sqrt(DIM)
        Wkv = jax.random.normal(ks[3], (DIM, 2 * INNER), dtype=jnp.float32) / np.sqrt(DIM)
        Wo = jax.random.normal(ks[4], (INNER, DIM), dtype=jnp.float32) / np.sqrt(INNER)
        return {'x': x, 'latents': latents, 'ln1_w': ln1_w, 'ln1_b': ln1_b, 'ln2_w': ln2_w, 'ln2_b': ln2_b, 'Wq': Wq, 'Wkv': Wkv, 'Wo': Wo}
    _L0_xattn_all = _L0_xattn_setup()
    _L0_xattn_in = {k: v for k, v in _L0_xattn_all.items() if k in ('ln1_w', 'ln1_b', 'ln2_w', 'ln2_b', 'Wq', 'Wkv', 'Wo')}
    del _L0_xattn_all

    def _L0_ffn_setup():
        import jax, jax.numpy as jnp
        import numpy as np
        B, S, D, E, R, TOP_K = (8, 512, 128, 8, 16, 2)
        key = jax.random.key(seed)
        ks = jax.random.split(key, 4)
        scale = 0.02
        return {'x': jax.random.normal(ks[0], (B, S, D), dtype=jnp.float32), 'Wr': jax.random.normal(ks[1], (D, E), dtype=jnp.float32) * scale, 'br': jnp.zeros((E,), dtype=jnp.float32), 'Wd': jax.random.normal(ks[2], (E, D, R), dtype=jnp.float32) * scale, 'bd': jnp.zeros((E, R), dtype=jnp.float32), 'Wu': jax.random.normal(ks[3], (E, R, D), dtype=jnp.float32) * scale, 'bu': jnp.zeros((E, D), dtype=jnp.float32)}
    _L0_ffn_all = _L0_ffn_setup()
    _L0_ffn_in = {k: v for k, v in _L0_ffn_all.items() if k in ('Wr', 'br', 'Wd', 'bd', 'Wu', 'bu')}
    del _L0_ffn_all

    def _L1_xattn_setup():
        import jax, jax.numpy as jnp
        import numpy as np
        EMBED_DIM = 128
        NUM_HEADS = 16
        HEAD_DIM = EMBED_DIM // NUM_HEADS
        NEG = -1000000000.0

        def _split_heads(x):
            B, S, D = x.shape
            return x.reshape(B, S, NUM_HEADS, HEAD_DIM).transpose(0, 2, 1, 3)
        key = jax.random.key(seed)
        ks = jax.random.split(key, 13)
        B, S, D = (4, 256, EMBED_DIM)
        scale = 1.0 / np.sqrt(D)
        inp = {'query': jax.random.normal(ks[0], (B, S, D), jnp.float32), 'key': jax.random.normal(ks[1], (B, S, D), jnp.float32), 'value': jax.random.normal(ks[2], (B, S, D), jnp.float32), 'mask': jax.random.randint(ks[3], (B, 1, 1, S), 0, 2, jnp.int32), 'Wq': jax.random.normal(ks[4], (D, D), jnp.float32) * scale, 'bq': jnp.zeros((D,), jnp.float32), 'Wk': jax.random.normal(ks[5], (D, D), jnp.float32) * scale, 'bk': jnp.zeros((D,), jnp.float32), 'Wv': jax.random.normal(ks[6], (D, D), jnp.float32) * scale, 'bv': jnp.zeros((D,), jnp.float32), 'Wo': jax.random.normal(ks[7], (D, D), jnp.float32) * scale, 'bo': jnp.zeros((D,), jnp.float32)}
        return inp
    _L1_xattn_all = _L1_xattn_setup()
    _L1_xattn_in = {k: v for k, v in _L1_xattn_all.items() if k in ('Wq', 'bq', 'Wk', 'bk', 'Wv', 'bv', 'Wo', 'bo')}
    del _L1_xattn_all

    def _L1_ffn_setup():
        import jax, jax.numpy as jnp
        import numpy as np
        D = 128
        F = 352
        E = 8
        TOP_K = 2
        key = jax.random.key(seed)
        ks = jax.random.split(key, 6)
        std = 0.02
        x = jax.random.normal(ks[0], (2, 256, D), dtype=jnp.float32)
        router_w = jax.random.normal(ks[1], (D, E), dtype=jnp.float32) * std
        w1 = jax.random.normal(ks[2], (E, D, F), dtype=jnp.float32) * std
        v1 = jax.random.normal(ks[3], (E, D, F), dtype=jnp.float32) * std
        w2 = jax.random.normal(ks[4], (E, F, D), dtype=jnp.float32) * std
        bias = jnp.zeros((D,), dtype=jnp.float32)
        return {'x': x, 'router_w': router_w, 'w1': w1, 'v1': v1, 'w2': w2, 'bias': bias}
    _L1_ffn_all = _L1_ffn_setup()
    _L1_ffn_in = {k: v for k, v in _L1_ffn_all.items() if k in ('router_w', 'w1', 'v1', 'w2', 'bias')}
    del _L1_ffn_all
    return {'x': x, 'ctx_1024': ctx_1024, 'mask_Bx1x1xS2_ik0': mask_Bx1x1xS2_ik0, 'L0_xattn_ln1_w': _L0_xattn_in['ln1_w'], 'L0_xattn_ln1_b': _L0_xattn_in['ln1_b'], 'L0_xattn_ln2_w': _L0_xattn_in['ln2_w'], 'L0_xattn_ln2_b': _L0_xattn_in['ln2_b'], 'L0_xattn_Wq': _L0_xattn_in['Wq'], 'L0_xattn_Wkv': _L0_xattn_in['Wkv'], 'L0_xattn_Wo': _L0_xattn_in['Wo'], 'L0_ffn_Wr': _L0_ffn_in['Wr'], 'L0_ffn_br': _L0_ffn_in['br'], 'L0_ffn_Wd': _L0_ffn_in['Wd'], 'L0_ffn_bd': _L0_ffn_in['bd'], 'L0_ffn_Wu': _L0_ffn_in['Wu'], 'L0_ffn_bu': _L0_ffn_in['bu'], 'L1_xattn_Wq': _L1_xattn_in['Wq'], 'L1_xattn_bq': _L1_xattn_in['bq'], 'L1_xattn_Wk': _L1_xattn_in['Wk'], 'L1_xattn_bk': _L1_xattn_in['bk'], 'L1_xattn_Wv': _L1_xattn_in['Wv'], 'L1_xattn_bv': _L1_xattn_in['bv'], 'L1_xattn_Wo': _L1_xattn_in['Wo'], 'L1_xattn_bo': _L1_xattn_in['bo'], 'L1_ffn_router_w': _L1_ffn_in['router_w'], 'L1_ffn_w1': _L1_ffn_in['w1'], 'L1_ffn_v1': _L1_ffn_in['v1'], 'L1_ffn_w2': _L1_ffn_in['w2'], 'L1_ffn_bias': _L1_ffn_in['bias']}

def reference(x, ctx_1024, mask_Bx1x1xS2_ik0, L0_xattn_ln1_w, L0_xattn_ln1_b, L0_xattn_ln2_w, L0_xattn_ln2_b, L0_xattn_Wq, L0_xattn_Wkv, L0_xattn_Wo, L0_ffn_Wr, L0_ffn_br, L0_ffn_Wd, L0_ffn_bd, L0_ffn_Wu, L0_ffn_bu, L1_xattn_Wq, L1_xattn_bq, L1_xattn_Wk, L1_xattn_bk, L1_xattn_Wv, L1_xattn_bv, L1_xattn_Wo, L1_xattn_bo, L1_ffn_router_w, L1_ffn_w1, L1_ffn_v1, L1_ffn_w2, L1_ffn_bias):
    import jax
    import jax.numpy as jnp

    def _L0_xattn_ref(x, latents, ln1_w, ln1_b, ln2_w, ln2_b, Wq, Wkv, Wo):
        import jax, jax.numpy as jnp
        import numpy as np
        DIM = 128
        HEADS = 16
        DIM_HEAD = 64
        INNER = HEADS * DIM_HEAD
        EPS = 1e-05

        def _layernorm(t, w, b):
            mu = jnp.mean(t, axis=-1, keepdims=True)
            var = jnp.mean(jnp.square(t - mu), axis=-1, keepdims=True)
            return (t - mu) * jax.lax.rsqrt(var + EPS) * w + b
        xn = _layernorm(x, ln1_w, ln1_b)
        latn = _layernorm(latents, ln2_w, ln2_b)
        b, l, _ = latn.shape
        q = latn @ Wq
        kv_input = jnp.concatenate([xn, latn], axis=1)
        kv = kv_input @ Wkv
        k, v = jnp.split(kv, 2, axis=-1)

        def heads(t):
            return t.reshape(t.shape[0], t.shape[1], HEADS, DIM_HEAD).transpose(0, 2, 1, 3)
        q, k, v = (heads(q), heads(k), heads(v))
        scale = 1.0 / np.sqrt(np.sqrt(DIM_HEAD))
        weight = jnp.einsum('bhld,bhnd->bhln', q * scale, k * scale)
        weight = jax.nn.softmax(weight.astype(jnp.float32), axis=-1).astype(weight.dtype)
        out = jnp.einsum('bhln,bhnd->bhld', weight, v)
        out = out.transpose(0, 2, 1, 3).reshape(b, l, INNER)
        return out @ Wo

    def _L0_ffn_ref(x, Wr, br, Wd, bd, Wu, bu):
        import jax, jax.numpy as jnp
        import numpy as np
        B, S, D, E, R, TOP_K = (8, 512, 128, 8, 16, 2)
        logits = jnp.einsum('bsd,de->bse', x, Wr) + br
        gates = jax.nn.softmax(logits, axis=-1)
        topk_vals, topk_idx = jax.lax.top_k(gates, TOP_K)
        topk_vals = topk_vals / jnp.sum(topk_vals, axis=-1, keepdims=True)
        out = jnp.zeros_like(x)
        num_experts = Wd.shape[0]
        for e in range(num_experts):
            w = jnp.sum(topk_vals * (topk_idx == e), axis=-1)
            h = jax.nn.gelu(jnp.einsum('bsd,dr->bsr', x, Wd[e]) + bd[e])
            expert_out = x + jnp.einsum('bsr,rd->bsd', h, Wu[e]) + bu[e]
            out = out + w[..., None] * expert_out
        return out

    def _L1_xattn_ref(query, key, value, mask, Wq, bq, Wk, bk, Wv, bv, Wo, bo):
        import jax, jax.numpy as jnp
        import numpy as np
        EMBED_DIM = 128
        NUM_HEADS = 16
        HEAD_DIM = EMBED_DIM // NUM_HEADS
        NEG = -1000000000.0

        def _split_heads(x):
            B, S, D = x.shape
            return x.reshape(B, S, NUM_HEADS, HEAD_DIM).transpose(0, 2, 1, 3)
        B, S, D = query.shape
        Q = _split_heads(query @ Wq + bq)
        K = _split_heads(key @ Wk + bk)
        V = _split_heads(value @ Wv + bv)
        scores = jnp.einsum('bhqd,bhkd->bhqk', Q, K) / jnp.sqrt(jnp.float32(HEAD_DIM))
        scores = jnp.where(mask == 0, jnp.float32(NEG), scores)
        attn = jax.nn.softmax(scores, axis=-1)
        out = jnp.einsum('bhqk,bhkd->bhqd', attn, V)
        out = out.transpose(0, 2, 1, 3).reshape(B, S, D)
        return out @ Wo + bo

    def _L1_ffn_ref(x, router_w, w1, v1, w2, bias):
        import jax, jax.numpy as jnp
        import numpy as np
        D = 128
        F = 352
        E = 8
        TOP_K = 2
        B, S, d = x.shape
        xt = x.reshape(B * S, d)
        scores = jax.nn.softmax(xt @ router_w, axis=-1)
        expert_weights, expert_idx = jax.lax.top_k(scores, TOP_K)
        h = jax.nn.gelu(jnp.einsum('td,edf->tef', xt, w1), approximate=False) * jnp.einsum('td,edf->tef', xt, v1)
        y = jnp.einsum('tef,efd->ted', h, w2)
        yk = jnp.take_along_axis(y, expert_idx[:, :, None], axis=1)
        out = jnp.sum(expert_weights[:, :, None] * yk, axis=1) + bias
        return out.reshape(B, S, d)
    x = x + _L0_xattn_ref(ctx_1024, _layernorm(x, axis=-1), L0_xattn_ln1_w, L0_xattn_ln1_b, L0_xattn_ln2_w, L0_xattn_ln2_b, L0_xattn_Wq, L0_xattn_Wkv, L0_xattn_Wo)
    x = x + _L0_ffn_ref(_layernorm(x, axis=-1), L0_ffn_Wr, L0_ffn_br, L0_ffn_Wd, L0_ffn_bd, L0_ffn_Wu, L0_ffn_bu)
    x = x + _L1_xattn_ref(_layernorm(x, axis=-1), ctx_1024, ctx_1024, mask_Bx1x1xS2_ik0, L1_xattn_Wq, L1_xattn_bq, L1_xattn_Wk, L1_xattn_bk, L1_xattn_Wv, L1_xattn_bv, L1_xattn_Wo, L1_xattn_bo)
    x = x + _L1_ffn_ref(_layernorm(x, axis=-1), L1_ffn_router_w, L1_ffn_w1, L1_ffn_v1, L1_ffn_w2, L1_ffn_bias)
    return x

_drawn_inputs = setup_inputs


def setup_inputs(seed=0):
    import zlib

    import numpy as np

    out = dict(_drawn_inputs(seed))
    spreads = {'L0_xattn_ln1_w': (1.0, 0.2),
     'L0_xattn_ln1_b': (0.0, 0.301),
     'L0_xattn_ln2_w': (1.0, 0.2),
     'L0_xattn_ln2_b': (0.0, 0.1),
     'L0_ffn_br': (0.0, 0.298),
     'L0_ffn_bd': (0.0, 0.8),
     'L0_ffn_bu': (0.0, 0.1),
     'L1_xattn_bq': (0.0, 0.579),
     'L1_xattn_bk': (0.0, 2.0),
     'L1_xattn_bv': (0.0, 0.1),
     'L1_xattn_bo': (0.0, 0.1),
     'L1_ffn_bias': (0.0, 0.389)}
    factors = {'L0_ffn_Wd': 8.0,
     'L0_ffn_Wu': 8.0,
     'L1_ffn_router_w': 8.0,
     'L1_ffn_w1': 8.0,
     'L1_ffn_v1': 8.0,
     'L1_ffn_w2': 8.0}
    for name, (base, spread) in spreads.items():
        noise = np.random.default_rng([zlib.crc32(name.encode()), seed]).standard_normal(out[name].shape)
        drawn = base * np.exp(spread * noise) if base else spread * noise
        out[name] = jnp.asarray(drawn.astype(out[name].dtype))
    for name, factor in factors.items():
        out[name] = (out[name] * factor).astype(out[name].dtype)
    return out
```

```python
from contextlib import ExitStack

import numpy as np

import concourse.bass as bass
from concourse import mybir

F32 = mybir.dt.float32
F32R = mybir.dt.float32r
BF16 = mybir.dt.bfloat16
I32 = mybir.dt.int32
ALU = mybir.AluOpType
ACT = mybir.ActivationFunctionType
AX = mybir.AxisListType

P = 128
B, S, D = 4, 512, 128
C = 154
CT = C - P
TOK = B * S
NT = TOK // P
QT = S // P
H0, DH0 = 16, 64
PAIRS = H0 // 2
KV0 = C + S
NK = -(-KV0 // P)
KTAIL = KV0 - (NK - 1) * P
KC = 334
E = 8
R = 16
F = 352
H1, DH1 = 16, 8
G1 = 4
F_TILES = [(j * P, min(P, F - j * P)) for j in range(-(-F // P))]
NF = len(F_TILES)
EPS = 1e-5
NEG = -1.0e9
UNITS = 2 * B
N_PARAMS = 22
DVE_CONSTS = 2


def constants():
    p = np.arange(P)
    ident = np.eye(P, dtype=np.float32)
    head_of_dim = (p[:, None] // DH1 == np.arange(H1)[None, :]).astype(np.float32)
    dim_in_group = np.broadcast_to((np.arange(32)[None, :] // DH1 == np.arange(4)[:, None]).reshape(1, 128), (P, 128))
    expert_less_8 = np.broadcast_to(np.arange(E)[None, :] - float(E), (P, E))
    expert_of_row = np.zeros((P, P), np.float32)
    expert_of_row[:E] = np.arange(P)[None, :] // R == np.arange(E)[:, None]
    return np.concatenate([ident, head_of_dim, dim_in_group, expert_less_8, expert_of_row], 1).astype(np.float32)


C_IDENT, C_HEAD, C_DIM, C_EXP, C_SEL = 0, P, P + H1, P + H1 + P, P + H1 + P + E
C_ALL = C_SEL + P


def build(nc, a, out):
    with ExitStack() as ctx:
        def sb(name, shape, dt=F32):
            return ctx.enter_context(nc.sbuf_tensor(name, shape, dt))

        def sem(name):
            return ctx.enter_context(nc.semaphore(name))

        ps = ctx.enter_context(nc.psum_tensor("ps", [P, 8, 512], F32))

        consts = sb("consts", [P, C_ALL])
        ident = consts[:, C_IDENT:C_IDENT + P]
        head_of_dim = consts[:, C_HEAD:C_HEAD + H1]
        dim_in_group = consts[:, C_DIM:C_DIM + P].rearrange("p (h d) -> p h d", h=4)
        expert_less_8 = consts[:, C_EXP:C_EXP + E]
        expert_of_row = consts[0:E, C_SEL:C_SEL + P]
        identb = sb("identb", [P, P], BF16)
        ones = sb("ones", [P, DH0])
        ones_row = sb("ones_row", [1, P], BF16)
        head_rows = sb("head_rows", [H1, H1, P], BF16)
        x = sb("x", [P, NT, D])
        stats = sb("stats", [P, NT, 6])
        mv = sb("mv", [P, NT, 2])
        sd = sb("sd", [P, NT])
        rstd = sb("rstd", [P, NT])
        ctxT = sb("ctxT", [P, B, C])
        kvT = sb("kvT", [P, B, KV0])
        cols = sb("cols", [P, 7])
        rows = sb("rows", [P, 3, D])
        wd = sb("wd", [P, E, R])
        wu = sb("wu", [P, D])
        wr0 = sb("wr0", [P, E])
        wr1 = sb("wr1", [P, E])
        br = sb("br", [P, E])
        bu = sb("bu", [E, D])
        w1x = sb("w1x", [P, 4, D])
        wo0 = sb("wo0", [P, PAIRS, D])
        big = sb("big", [P, PAIRS, TOK])

        wqkv = sb("wqkv", [P, 2, 3, P])
        k_a = sb("k_a", [P, 2, 2, KV0], F32R)
        k_b = sb("k_b", [DH0 + 1, 2, 2, KV0], F32R)
        q_a = sb("q_a", [P, 2, 2, S], F32R)
        q_b = sb("q_b", [DH0 + 1, 2, 2, S], F32R)
        v0 = sb("v0", [P, 2, NK, P])
        prob = sb("prob", [P, 2, NK, S])
        psums = sb("psums", [P, 2, S])
        nmax = sb("nmax", [P, 2, QT], BF16)
        rden = sb("rden", [P, S])

        lg = sb("lg", [P, NT, E])
        gate = sb("gate", [P, NT, E])
        g2 = sb("g2", [P, NT, E])
        eq = sb("eq", [P, NT, E])
        hot = sb("hot", [P, NT, E])
        wgt = sb("wgt", [P, NT, E])
        red = sb("red", [P, NT])
        wsum = sb("wsum", [P, NT])

        flat_big = big[:].rearrange("p a t -> p (a t)")
        flat_prob = prob[:].rearrange("p h k q -> p (h k q)")
        used = {"big": 0, "prob": 0}

        def carve(*shape, of="big"):
            flat, n = {"big": flat_big, "prob": flat_prob}[of], int(np.prod(shape))
            v = flat[:, used[of]:used[of] + n]
            used[of] += n
            names = "abcd"[:len(shape)]
            if len(shape) == 1:
                return v
            return v.rearrange(f"p ({' '.join(names)}) -> p {' '.join(names)}", **dict(zip(names, shape)))

        qT = carve(TOK)
        probm = carve(2, G1, S)
        probt = carve(2, S)
        vm = carve(H1, 32)
        vt = carve(4, 32)
        k_mask = carve(H1, C)
        k_tail = carve(H1, 32)
        qr = q_a[:].rearrange("p s h q -> p (s h q)")[:, 0:S]
        kr = k_a[:].rearrange("p s h k -> p (s h k)")[:, 0:H1 * C].rearrange("p (h c) -> p h c", h=H1)
        nmq = sb("nmq", [P, QT, H1], BF16)
        nm = sb("nm", [H1, S], BF16)
        mask_i = sb("mask_i", [P, B], I32)
        mask_t = sb("mask_t", [P, B], I32)
        qb = carve(S)
        cT = carve(C)
        kTb = carve(C)
        vb = carve(2, D)
        oT = carve(S)
        we1 = carve(2, F)
        wv1 = carve(2, F)
        we2 = carve(2, NF, D)
        wT = flat_big[0:E, 0:TOK]
        xn = carve(NT, D, of="prob")
        xnT = carve(TOK, of="prob")
        acc = carve(NT, D, of="prob")
        hidden = flat_big[:, TOK:2 * TOK]
        used["big"] = 0
        gg = carve(NF, S)
        hid = carve(2, NF, S)
        used["prob"] = NT * D
        ctx_in = carve(B, 2, D, of="prob")
        ctxn = carve(B, 2, D, of="prob")
        mask_r = carve(B, C, of="prob").bitcast(I32)
        valid_r = carve(B, C, of="prob")
        valid_m = sb("valid_m", [P, 2, B])
        any_valid = sb("any_valid", [P, B])
        mcol = sb("mcol", [P, B, 4])
        mcol_b = sb("mcol_b", [P, 4])
        neg_row = sb("neg_row", [1, B, C], BF16)

        wcol = sb("wcol", [P, 2, NT])

        names = """x_loaded ctx_loaded params_loaded mask_loaded pair_even pair_odd
            expert_even expert_odd dve_step pool_step var_ready sd_ready lat_ready ctxn_ready
            tr_done kvT_done ctxT_done q_proj k_proj v_proj q_hi q_lo q_dup k_hi k_lo k_dup v_dve v_act
            max_scores max_done row_proj row_copied scores scores_taken sum_step pv_done den_done
            den_read recip head_done wo_done x1_done ln_ready xt_done xnT_done logits_done logit_ready gate_exp hT_done h_gelu
            wT_tr wT_done wb_done hw_done up_done x2_done q1_done qT_done ctx_b qb_done qr_done kv1_done
            k1_done kr_done v1_done mc_done max1 max1_done rows1 nm_done s1 s1_taken pv1 den1_read
            o1_done wo1 x3_done r1_done g_done v_done gelu_done h_done down_done acc_done w_done
            out_stored""".split()
        s = {n: sem(n) for n in names}

        dve_n = [0]

        from_one = {"pe": ["s1", "kv1_done"], "act": ["s1_taken", "gelu_done", "den_read"],
                    "dve": ["head_done", "x3_done", "max1_done", "o1_done", "h_done", "acc_done"]}

        def link(eng, ins):
            dve_n[0] += 1
            ins.then_inc(s["dve_step"], 1)
            eng.wait_ge(s["dve_step"], dve_n[0])

        block = ctx.enter_context(nc.Block())

        @block.sync
        def _(sp):
            sp.dma_start(x[:], a["x"].rearrange("b (t p) d -> p (b t) d", p=P)).then_inc(s["x_loaded"], 16)
            c = a["ctx_1024"]
            sp.dma_start(ctx_in[:, :, 0, :], c[:, 0:P, :].rearrange("b p d -> p b d")).then_inc(s["ctx_loaded"], 16)
            sp.dma_start(ctx_in[0:CT, :, 1, :], c[:, P:C, :].rearrange("b p d -> p b d")).then_inc(s["ctx_loaded"], 16)
            params = [(consts[:], a["shape_consts"])]
            for n, name in enumerate(["L0_xattn_ln1_w", "L0_xattn_ln1_b", "L0_xattn_ln2_w", "L0_xattn_ln2_b",
                                      "L0_ffn_bd", "L1_xattn_bq", "L1_xattn_bk"]):
                src = a[name] if len(a[name].shape) == 1 else a[name].rearrange("e r -> (e r)")
                params.append((cols[:, n:n + 1], src.rearrange("(p o) -> p o", o=1)))
            for n, name in enumerate(["L1_xattn_bv", "L1_xattn_bo", "L1_ffn_bias"]):
                params.append((rows[:, n, :], a[name].partition_broadcast(P)))
            params.append((wd[:], a["L0_ffn_Wd"].rearrange("e d r -> d e r")))
            params.append((wu[:], a["L0_ffn_Wu"].rearrange("e r d -> (e r) d")))
            params.append((wr0[:], a["L0_ffn_Wr"]))
            params.append((wr1[:], a["L1_ffn_router_w"]))
            params.append((br[:], a["L0_ffn_br"].partition_broadcast(P)))
            params.append((bu[:], a["L0_ffn_bu"]))
            for n, name in enumerate(["Wq", "Wk", "Wv", "Wo"]):
                params.append((w1x[:, n, :], a["L1_xattn_" + name]))
            params.append((wo0[:], a["L0_xattn_Wo"].rearrange("(j p) d -> p j d", p=P)))
            for dst, src in params:
                sp.dma_start(dst, src).then_inc(s["params_loaded"], 16)
            assert len(params) == N_PARAMS
            wq, wkv = a["L0_xattn_Wq"], a["L0_xattn_Wkv"]

            def load_pair(pair, par, name):
                sp.dma_start(wqkv[:, par, 0, :], wq[:, bass.ds(pair * P, P)]).then_inc(s[name], 16)
                sp.dma_start(wqkv[:, par, 1, :], wkv[:, bass.ds(pair * P, P)]).then_inc(s[name], 16)
                sp.dma_start(wqkv[:, par, 2, :], wkv[:, bass.ds(pair * P + H0 * DH0, P)]).then_inc(s[name], 16)

            load_pair(0, 0, "pair_even")
            load_pair(1, 1, "pair_odd")
            m = a["mask_Bx1x1xS2_ik0"].rearrange("b o u c -> (b o u) c")
            sp.dma_start(mask_i[:], a["mask_by_key"][0:P, :]).then_inc(s["mask_loaded"], 16)
            sp.wait_ge(s["pool_step"], 1)
            for g in range(G1):
                sp.dma_start(mask_t[32 * g:32 * g + CT, :], a["mask_by_key"][P:C, :]).then_inc(s["mask_loaded"], 16)
            sp.dma_start(mask_r, m.rearrange("b c -> (b c)").partition_broadcast(P)
                         .rearrange("p (b c) -> p b c", b=B)).then_inc(s["mask_loaded"], 16)

            def dups(w, st):
                for h in range(2):
                    sp.wait_ge(s["q_hi"], 2 * w + h + 1)
                    sp.dma_start(q_a[DH0:P, st, h, :].bitcast(F32),
                                 q_a[0:DH0, st, h, :].bitcast(F32)).then_inc(s["q_dup"], 16)
                for h in range(2):
                    sp.wait_ge(s["k_hi"], 4 * w + 3 + h)
                    sp.dma_start(k_b[0:DH0, st, h, :].bitcast(F32),
                                 k_a[0:DH0, st, h, :].bitcast(F32)).then_inc(s["k_dup"], 16)

            def turn(u0, last_turn):
                for i in range(UNITS - last_turn):
                    w = u0 + i + 1
                    dups(w, (i + 1) % 2)
                    if i % B == B - 2 and not last_turn:
                        sp.wait_ge(s["v_proj"], 2 * w + 2)
                        pair = it * 2 + 2 + i // B
                        load_pair(pair, i // B, ["pair_even", "pair_odd"][i // B])

            dups(0, 0)
            with sp.Fori(0, PAIRS // 2 - 1) as it:
                turn(it * UNITS, False)
            turn(PAIRS * B - UNITS, True)

            w1, v1, w2 = a["L1_ffn_w1"], a["L1_ffn_v1"], a["L1_ffn_w2"]

            def load_expert(e, par, name):
                sp.dma_start(we1[:, par, :], w1[bass.ds(e, 1), :, :].rearrange("e d f -> d (e f)")).then_inc(s[name], 16)
                sp.dma_start(wv1[:, par, :], v1[bass.ds(e, 1), :, :].rearrange("e d f -> d (e f)")).then_inc(s[name], 16)
                for j, (f0, fn) in enumerate(F_TILES):
                    sp.dma_start(we2[0:fn, par, j, :],
                                 w2[bass.ds(e, 1), f0:f0 + fn, :].rearrange("e f d -> f (e d)")).then_inc(s[name], 16)

            sp.wait_ge(s["wo_done"], B)
            load_expert(0, 0, "expert_even")
            load_expert(1, 1, "expert_odd")
            with sp.Fori(1, E // 2) as it:
                sp.wait_ge(s["down_done"], it * (2 * B) - B)
                load_expert(it * 2, 0, "expert_even")
                sp.wait_ge(s["down_done"], it * (2 * B))
                load_expert(it * 2 + 1, 1, "expert_odd")

            o = out.rearrange("b (t p) d -> p (b t) d", p=P)
            for c in range(B):
                sp.wait_ge(s["acc_done"], 1 + (E - 1) * B + c + 1)
                sp.dma_start(o[:, QT * c:QT * (c + 1), :], acc[:, QT * c:QT * (c + 1), :]).then_inc(s["out_stored"], 16)
            sp.wait_ge(s["out_stored"], 16 * B)

        @block.tensor
        def _(pe):
            mm = nc.tensor.matmul
            for n in from_one["pe"]:
                pe.sem_inc(s[n], 1)

            pe.wait_ge(s["params_loaded"], 16 * N_PARAMS)
            pe.wait_ge(s["ctx_loaded"], 32)
            for b in range(B):
                nc.tensor.transpose(ps[:, B + b, 160:160 + P], ctx_in[:, b, 0, :], ident)
                nc.tensor.transpose(ps[:, B + b, 160 + P:160 + C], ctx_in[0:CT, b, 1, :], ident[0:CT, 0:CT])
            pe.wait_ge(s["ctxn_ready"], 1)
            for b in range(B):
                nc.tensor.transpose(ps[:, B + b, 0:P], ctxn[:, b, 0, :], ident)
                last = nc.tensor.transpose(ps[:, B + b, P:C], ctxn[0:CT, b, 1, :], ident[0:CT, 0:CT])
            last.then_inc(s["tr_done"], 1)
            pe.wait_ge(s["lat_ready"], 1)
            for b in range(B):
                for t in range(QT):
                    last = nc.tensor.transpose(ps[:, b, t * P:(t + 1) * P], xn[:, QT * b + t, :], ident)
                last.then_inc(s["tr_done"], 1)

            SC, PV, PR = 2, 5, 7

            def q_proj(w, b, wp):
                if not (isinstance(w, int) and w == 0):
                    pe.wait_ge(s["v_act"], 2 * w)
                mm(ps[:, PR, :], wqkv[:, wp, 0, :], kvT[:, b, C:KV0], start=True, stop=True).then_inc(s["q_proj"], 1)

            def k_proj(w, b, wp, c):
                if c == 0:
                    pe.wait_ge(s["q_hi"], 2 * w + 2)
                    pe.wait_ge(s["q_lo"], 2 * w + 2)
                else:
                    pe.wait_ge(s["k_hi"], 4 * w + 2)
                    pe.wait_ge(s["k_lo"], 4 * w + 2)
                n = KV0 // 2
                mm(ps[:, PR, 0:n], wqkv[:, wp, 1, :], kvT[:, b, c * n:(c + 1) * n],
                   start=True, stop=True).then_inc(s["k_proj"], 1)

            def v_proj(w, b, wp, c):
                if c == 0:
                    pe.wait_ge(s["k_hi"], 4 * w + 4)
                    pe.wait_ge(s["k_lo"], 4 * w + 4)
                else:
                    pe.wait_ge(s["v_dve"], w + 1)
                for t in (range(4) if c == 0 else range(4, NK)):
                    n = min(P, KV0 - t * P)
                    last = mm(ps[0:n, PR, (t % 4) * P:(t % 4 + 1) * P], kvT[:, b, t * P:t * P + n],
                              wqkv[:, wp, 2, :], start=True, stop=True)
                last.then_inc(s["v_proj"], 1)

            def max_scores(w, st, j):
                h, t = divmod(j, QT)
                if j == 0:
                    pe.wait_ge(s["q_hi"], 2 * w + 2)
                    pe.wait_ge(s["k_hi"], 4 * w + 4)
                    if not (isinstance(w, int) and w == 0):
                        pe.wait_ge(s["den_read"], 1 + w - 1)
                pe.wait_ge(s["max_done"], 8 * w + j)
                for c in range(2):
                    k0 = c * (KV0 - KC)
                    last = mm(ps[:, c, 0:KC], q_a[0:DH0, st, h, t * P:(t + 1) * P], k_a[0:DH0, st, h, k0:k0 + KC],
                              start=True, stop=True)
                last.then_inc(s["max_scores"], 1)

            def max_rows(w):
                pe.wait_ge(s["max_done"], 8 * w + 8)
                for t in range(QT):
                    for h in range(2):
                        last = mm(ps[32 * h:32 * h + 1, 0, t * P:(t + 1) * P], nmax[:, h, t:t + 1], identb[:],
                                  start=True, stop=True)
                last.then_inc(s["row_proj"], 1)

            def scores(u, st, kt, heads=(0, 1)):
                n = min(P, KV0 - kt * P)
                for h in heads:
                    j = 2 * kt + h
                    if kt == 0 and h == 0:
                        pe.wait_ge(s["row_copied"], 2 * u + 2)
                        pe.wait_ge(s["q_lo"], 2 * u + 2)
                        pe.wait_ge(s["q_dup"], 32 * u + 32)
                        pe.wait_ge(s["k_lo"], 4 * u + 4)
                        pe.wait_ge(s["k_dup"], 32 * u + 32)
                    pe.wait_ge(s["scores_taken"], 2 * NK * u + j + 1)
                    o = ps[0:n, SC + j % 3, :]
                    mm(o, k_a[:, st, h, kt * P:kt * P + n], q_a[:, st, h, :], start=True, stop=False)
                    mm(o, k_b[:, st, h, kt * P:kt * P + n], q_b[:, st, h, :],
                       start=False, stop=True).then_inc(s["scores"], 1)

            def pv(u, st, kt):
                n = min(P, KV0 - kt * P)
                if kt == 0:
                    pe.wait_ge(s["v_dve"], u + 1)
                    pe.wait_ge(s["v_act"], 2 * u + 2)
                pe.wait_ge(s["scores_taken"], 3 + 2 * NK * u + 2 * kt + 2)
                for h in range(2):
                    last = mm(ps[DH0 * h:DH0 * h + DH0, PV + st, :], v0[0:n, st, kt, DH0 * h:DH0 * h + DH0],
                              prob[0:n, h, kt, :], start=(kt == 0), stop=(kt == NK - 1))
                if kt == NK - 1:
                    last.then_inc(s["pv_done"], 1)

            def den(u, more):
                if more == 0:
                    pe.wait_ge(s["den_read"], 1 + u)
                pe.wait_ge(s["sum_step"], 2 * (NK - 1) * (u + 1))
                for h in range(2):
                    last = mm(ps[DH0 * h:DH0 * h + DH0, 1, :], ones[:], psums[:, h, :], start=True, stop=True)
                last.then_inc(s["den_done"], 1)

            def unit(u, i, more):
                st, nst, b1, wp1 = i % 2, (i + 1) % 2, (i + 1) % B, ((i + 1) // B) % 2
                b2, wp2 = (i + 2) % B, ((i + 2) // B) % 2
                w, z = u + 1, u + 2
                steps = max_scores if more > 0 else (lambda *a: None)
                scores(u, st, 1)
                if more > 0:
                    k_proj(w, b1, wp1, 1)
                pv(u, st, 0)
                scores(u, st, 2, [0])
                steps(w, nst, 0)
                scores(u, st, 2, [1])
                if more > 0:
                    v_proj(w, b1, wp1, 0)
                steps(w, nst, 1)
                pv(u, st, 1)
                scores(u, st, 3, [0])
                steps(w, nst, 2)
                scores(u, st, 3, [1])
                pv(u, st, 2)
                steps(w, nst, 3)
                if more > 0:
                    v_proj(w, b1, wp1, 1)
                scores(u, st, 4)
                steps(w, nst, 4)
                pv(u, st, 3)
                scores(u, st, 5, [0])
                steps(w, nst, 5)
                scores(u, st, 5, [1])
                if more > 1:
                    q_proj(z, b2, wp2)
                steps(w, nst, 6)
                pv(u, st, 4)
                steps(w, nst, 7)
                pv(u, st, 5)
                if more > 0:
                    max_rows(w)
                den(u, more)
                if more > 1:
                    k_proj(z, b2, wp2, 0)
                if more > 0:
                    scores(w, nst, 0)

            def turn(u0, last_turn):
                for i in range(UNITS):
                    if i == UNITS - 2 and not last_turn:
                        pe.wait_ge(s["pair_even"], pair_count(u0) + 48)
                    if i == B - 2:
                        pe.wait_ge(s["pair_odd"], pair_count(u0))
                    unit(u0 + i, i, min(2, UNITS - 1 - i) if last_turn else 2)

            def pair_count(u0):
                return u0 * (48 // UNITS) + 48

            pe.wait_ge(s["pair_even"], 48)
            pe.wait_ge(s["kvT_done"], B + 1)
            q_proj(0, 0, 0)
            k_proj(0, 0, 0, 0)
            k_proj(0, 0, 0, 1)
            v_proj(0, 0, 0, 0)
            v_proj(0, 0, 0, 1)
            for j in range(8):
                max_scores(0, 0, j)
            q_proj(1, 1, 0)
            max_rows(0)
            k_proj(1, 1, 0, 0)
            scores(0, 0, 0)
            with pe.Fori(0, PAIRS * B - UNITS, UNITS) as u0:
                turn(u0, False)
            turn(PAIRS * B - UNITS, True)

            pe.wait_ge(s["head_done"], 1 + PAIRS * B)
            for t in range(NT):
                for j in range(PAIRS):
                    last = mm(ps[:, t // QT, (t % QT) * P:(t % QT + 1) * P], big[:, j, t * P:(t + 1) * P],
                              wo0[:, j, :], start=(j == 0), stop=(j == PAIRS - 1))
                if t % QT == QT - 1:
                    last.then_inc(s["wo_done"], 1)

            def transpose_xn(stage):
                for c in range(B):
                    pe.wait_ge(s["ln_ready"], B * stage + c + 1)
                    for t in range(QT):
                        last = nc.tensor.transpose(ps[:, 4 + c, t * P:(t + 1) * P], xn[:, QT * c + t, :], ident)
                    last.then_inc(s["xt_done"], 1)

            def router(stage, w):
                pe.wait_ge(s["xnT_done"], B * (2 * stage + 1))
                for t in range(NT):
                    last = mm(ps[:, 0, t * E:(t + 1) * E], xnT[:, t * P:(t + 1) * P], w[:], start=True, stop=True)
                last.then_inc(s["logits_done"], 1)

            pe.wait_ge(s["x1_done"], B)
            transpose_xn(0)
            router(0, wr0)
            for c in range(B):
                mm(ps[:, 4 + c, :], wd[:].rearrange("p e r -> p (e r)"), xnT[:, c * S:(c + 1) * S],
                   start=True, stop=True).then_inc(s["hT_done"], 1)
            pe.wait_ge(s["w_done"], 1)
            for t in range(NT):
                last = nc.tensor.transpose(ps[0:E, t // QT, (t % QT) * P:(t % QT + 1) * P], wgt[:, t, :], ident)
            last.then_inc(s["wT_tr"], 1)
            pe.wait_ge(s["wT_done"], 1)
            for c in range(B):
                mm(ps[:, c, :], expert_of_row, wT[:, c * S:(c + 1) * S], start=True, stop=True).then_inc(s["wb_done"], 1)
            for t in range(NT):
                if t % QT == 0:
                    pe.wait_ge(s["hw_done"], t // QT + 1)
                    pe.wait_ge(s["h_gelu"], B)
                o = ps[:, 4 + t // QT, (t % QT) * P:(t % QT + 1) * P]
                mm(o, hidden[:, t * P:(t + 1) * P], wu[:], start=True, stop=False)
                last = mm(o, wT[:, t * P:(t + 1) * P], bu[:], start=False, stop=True)
                if t % QT == QT - 1:
                    last.then_inc(s["up_done"], 1)

            pe.wait_ge(s["x2_done"], B)
            transpose_xn(1)
            for c in range(B):
                pe.wait_ge(s["xnT_done"], B + c + 1)
                mm(ps[:, c, :], w1x[:, 0, :], xnT[:, c * S:(c + 1) * S], start=True, stop=True).then_inc(s["q1_done"], 1)
            pe.wait_ge(s["qT_done"], B)
            with pe.Fori(0, B) as b:
                pe.wait_ge(s["ctx_b"], b + 1)
                pe.wait_ge(s["x3_done"], 1 + b)
                mm(ps[:, 0, 0:C], w1x[:, 1, :], cT, start=True, stop=True)
                mm(ps[:, 1, 0:D], cT[:, 0:P], w1x[:, 2, :], start=True, stop=True)
                mm(ps[0:CT, 1, D:2 * D], cT[:, P:C], w1x[:, 2, :], start=True, stop=True).then_inc(s["kv1_done"], 1)
                pe.wait_ge(s["qr_done"], b + 1)
                pe.wait_ge(s["kr_done"], b + 1)
                for n in range(QT * 6):
                    t, j = divmod(n, 6)
                    hn = min(3, H1 - 3 * j)
                    pe.wait_ge(s["max1_done"], 1 + b * (QT * 6) + max(n - 3, 0))
                    mm(ps[:, 2 + n % 4, 0:hn * C], qr[:, t * P:(t + 1) * P],
                       kr[:, 3 * j:3 * j + hn, :], start=True, stop=False)
                    mm(ps[:, 2 + n % 4, 0:hn * C], ones_row[:],
                       neg_row[:, bass.ds(b, 1), :].broadcast_to([1, hn, C]),
                       start=False, stop=True).then_inc(s["max1"], 1)
                pe.wait_ge(s["max1_done"], 1 + b * (QT * 6) + QT * 6)
                for t in range(QT):
                    last = mm(ps[0:H1, 6, t * P:(t + 1) * P], nmq[:, t, :], identb[:], start=True, stop=True)
                last.then_inc(s["rows1"], 1)
                pe.wait_ge(s["nm_done"], b + 1)
                pe.wait_ge(s["qb_done"], b + 1)

                pe.wait_ge(s["v1_done"], b + 1)

                def scores1(hh):
                    for g in range(G1):
                        n, h = 5 * hh + g, 4 * g + hh
                        pe.wait_ge(s["s1_taken"], 1 + b * 20 + max(n - 3, 0))
                        mm(ps[:, 2 + n % 4, :], k_mask[:, h, 0:P], qb, start=True, stop=False)
                        mm(ps[:, 2 + n % 4, :], head_rows[:, h, :], nm[:], start=False, stop=True).then_inc(s["s1"], 1)
                    n = 5 * hh + 4
                    pe.wait_ge(s["s1_taken"], 1 + b * 20 + n - 3)
                    for g in range(G1):
                        mm(ps[32 * g:32 * g + 32, 2 + n % 4, :], k_tail[:, 4 * g + hh, :], qb, start=True, stop=False)
                    for g in range(G1):
                        last = mm(ps[32 * g:32 * g + 32, 2 + n % 4, :], head_rows[:, 4 * g + hh, 0:32], nm[:],
                                  start=False, stop=True)
                    last.then_inc(s["s1"], 1)

                def pv1(hh):
                    pe.wait_ge(s["s1_taken"], 1 + b * 20 + 5 * hh + 5)
                    for dst, lm, lt in ((6, lambda g: vm[:, 4 * g + hh, :], lambda g: vt[32 * g:32 * g + CT, hh, :]),
                                        (7, lambda g: dim_in_group[:, hh, :],
                                         lambda g: dim_in_group[32 * g:32 * g + CT, hh, :])):
                        for g in range(G1):
                            mm(ps[32 * g:32 * g + 32, dst, :], lm(g), probm[:, hh % 2, g, :],
                               start=(hh == 0), stop=False)
                        for g in range(G1):
                            last = mm(ps[32 * g:32 * g + 32, dst, :], lt(g), probt[32 * g:32 * g + CT, hh % 2, :],
                                      start=False, stop=(hh == 3))
                    if hh == 3:
                        last.then_inc(s["pv1"], 1)

                scores1(0)
                for hh in range(1, 4):
                    scores1(hh)
                    pv1(hh - 1)
                pv1(3)
                pe.wait_ge(s["o1_done"], 1 + b + 1)
                for t in range(QT):
                    last = mm(ps[:, 0, t * P:(t + 1) * P], oT[:, t * P:(t + 1) * P], w1x[:, 3, :], start=True, stop=True)
                last.then_inc(s["wo1"], 1)

            pe.wait_ge(s["x3_done"], 1 + B)
            transpose_xn(2)
            router(1, wr1)
            pe.wait_ge(s["logit_ready"], 2)

            def up(m, c, par, j, dist):
                f0, fn = F_TILES[j]
                if not (isinstance(m, int) and m == 0):
                    pe.wait_ge(s["gelu_done"], 1 + NF * m - dist)
                    pe.wait_ge(s["h_done"], 1 + NF * m - dist)
                r = xnT[:, c * S:(c + 1) * S]
                mm(ps[0:fn, j, :], we1[:, par, f0:f0 + fn], r, start=True, stop=True).then_inc(s["g_done"], 1)
                mm(ps[0:fn, 3 + j, :], wv1[:, par, f0:f0 + fn], r, start=True, stop=True).then_inc(s["v_done"], 1)

            def down(m, i):
                pe.wait_ge(s["h_done"], 1 + NF * m + NF)
                for t in range(QT):
                    for j, (f0, fn) in enumerate(F_TILES):
                        last = mm(ps[:, 6 + i % 2, t * P:(t + 1) * P], hid[0:fn, i % 2, j, t * P:(t + 1) * P],
                                  we2[0:fn, (i // B) % 2, j, :], start=(j == 0), stop=(j == NF - 1))
                last.then_inc(s["down_done"], 1)

            def turn1(m0, last_turn):
                for i in range(UNITS):
                    m, c, par = m0 + i, i % B, i // B
                    up(m, c, par, 1, 0)
                    up(m, c, par, 2, 0)
                    if not (last_turn and i == UNITS - 1):
                        if i == UNITS - 1:
                            pe.wait_ge(s["expert_even"], m0 * (80 // UNITS) + 160)
                        if i == B - 1:
                            pe.wait_ge(s["expert_odd"], m0 * (80 // UNITS) + 80)
                        up(m + 1, (i + 1) % B, ((i + 1) // B) % 2, 0, NF - 1)
                    down(m, i)

            pe.wait_ge(s["expert_even"], 80)
            up(0, 0, 0, 0, 0)
            with pe.Fori(0, E * B - UNITS, UNITS) as m0:
                turn1(m0, False)
            turn1(E * B - UNITS, True)

        @block.scalar
        def _(act):
            cp = nc.scalar.copy
            af = nc.scalar.activation
            for n in from_one["act"]:
                act.sem_inc(s[n], 1)

            def roots(n):
                act.wait_ge(s["var_ready"], n + 1)
                af(sd[:], mv[:, :, 1], ACT.Sqrt).then_inc(s["sd_ready"], 1)

            roots(0)
            roots(1)
            roots(2)
            act.wait_ge(s["tr_done"], 1)
            for b in range(B):
                last = cp(ctxT[:, b, :], ps[:, B + b, 160:160 + C])
            last.then_inc(s["ctxT_done"], 1)

            SC, PR = 2, 7
            s_taken = s["scores_taken"]

            def q_hi(w, st):
                act.wait_ge(s["q_proj"], w + 1)
                for h in range(2):
                    cp(q_a[0:DH0, st, h, :], ps[DH0 * h:DH0 * h + DH0, PR, :]).then_inc(s["q_hi"], 1)

            def k_hi(w, st, c):
                n = KV0 // 2
                act.wait_ge(s["k_proj"], 2 * w + c + 1)
                for h in range(2):
                    cp(k_a[0:DH0, st, h, c * n:(c + 1) * n],
                       ps[DH0 * h:DH0 * h + DH0, PR, 0:n]).then_inc(s["k_hi"], 1)

            def v_last(w, st):
                act.wait_ge(s["v_proj"], 2 * w + 2)
                cp(v0[:, st, 4, :], ps[:, PR, 0:P]).then_inc(s["v_act"], 1)
                cp(v0[0:KTAIL, st, 5, :], ps[0:KTAIL, PR, P:2 * P]).then_inc(s["v_act"], 1)

            def max_row(w, st):
                act.wait_ge(s["row_proj"], w + 1)
                for h in range(2):
                    cp(q_b[DH0:DH0 + 1, st, h, :], ps[32 * h:32 * h + 1, 0, :]).then_inc(s["row_copied"], 1)

            def sums_copy(u):
                act.wait_ge(s["den_done"], u + 1)
                act.wait_ge(s["head_done"], 1 + u)
                cp(rden[:], ps[:, 1, :]).then_inc(s["den_read"], 1)

            def exps(u, st, kt):
                n = min(P, KV0 - kt * P)
                if kt == 0 and not (isinstance(u, int) and u == 0):
                    act.wait_ge(s["sum_step"], 2 * (NK - 1) * (u - 1) + 2)
                for h in range(2):
                    j = 2 * kt + h
                    act.wait_ge(s["scores"], 2 * NK * u + j + 1)
                    af(prob[0:n, h, kt, :], ps[0:n, SC + j % 3, :], ACT.Exp,
                       scale=1.0 / DH0 ** 0.5).then_inc(s_taken, 1)

            def unit(u, i, more):
                st, nst, w, z = i % 2, (i + 1) % 2, u + 1, u + 2
                exps(u, st, 1)
                if more > 0:
                    k_hi(w, nst, 1)
                exps(u, st, 2)
                exps(u, st, 3)
                if more > 0:
                    v_last(w, nst)
                exps(u, st, 4)
                exps(u, st, 5)
                if more > 1:
                    q_hi(z, st)
                if more > 0:
                    max_row(w, nst)
                sums_copy(u)
                if more > 1:
                    k_hi(z, st, 0)
                if more > 0:
                    exps(w, nst, 0)

            act.sem_inc(s_taken, 3)
            act.wait_ge(s["dve_step"], DVE_CONSTS)
            q_hi(0, 0)
            k_hi(0, 0, 0)
            k_hi(0, 0, 1)
            v_last(0, 0)
            q_hi(1, 1)
            max_row(0, 0)
            k_hi(1, 1, 0)
            exps(0, 0, 0)
            with act.Fori(0, PAIRS * B - UNITS, UNITS) as u0:
                for i in range(UNITS):
                    unit(u0 + i, i, 2)
            for i in range(UNITS):
                unit(PAIRS * B - UNITS + i, i, min(2, UNITS - 1 - i))

            def copy_xnT(stage):
                for c in range(B):
                    act.wait_ge(s["xt_done"], B * stage + c + 1)
                    cp(xnT[:, c * S:(c + 1) * S], ps[:, 4 + c, :]).then_inc(s["xnT_done"], 1)

            def gate_exp(stage):
                act.wait_ge(s["logit_ready"], stage + 1)
                af(gate[:], lg[:], ACT.Exp).then_inc(s["gate_exp"], 1)

            roots(3)
            copy_xnT(0)
            gate_exp(0)
            for c in range(B):
                act.wait_ge(s["hT_done"], c + 1)
                af(hidden[:, c * S:(c + 1) * S], ps[:, 4 + c, :], ACT.Gelu_apprx_tanh, bias=cols[:, 4:5]).then_inc(s["h_gelu"], 1)
            act.wait_ge(s["wT_tr"], 1)
            for c in range(B):
                last = cp(wT[:, c * S:(c + 1) * S], ps[0:E, c, :])
            last.then_inc(s["wT_done"], 1)

            roots(4)
            copy_xnT(1)
            for c in range(B):
                act.wait_ge(s["q1_done"], c + 1)
                af(qT[:, c * S:(c + 1) * S], ps[:, c, :], ACT.Identity, bias=cols[:, 5:6]).then_inc(s["qT_done"], 1)
            act.wait_ge(s["qT_done"], B)
            with act.Fori(0, B) as b:
                act.wait_ge(s["s1"], 1 + b * 20)
                act.wait_ge(s["kv1_done"], 1 + b)
                cp(cT, ctxT[:, bass.ds(b, 1), :].rearrange("p b c -> p (b c)")).then_inc(s["ctx_b"], 1)
                cp(qb, qT[:, bass.ds(b * S, S)]).then_inc(s["qb_done"], 1)
                cp(qr, qT[:, bass.ds(b * S, S)]).then_inc(s["qr_done"], 1)
                act.wait_ge(s["rows1"], b + 1)
                cp(nm[:], ps[0:H1, 6, :]).then_inc(s["nm_done"], 1)
                act.wait_ge(s["mc_done"], b + 1)
                for hh in range(4):
                    for g in range(G1 + 1):
                        n = 5 * hh + g
                        act.wait_ge(s["s1"], 1 + b * 20 + n + 1)
                        if g < G1:
                            af(probm[:, hh % 2, g, :], ps[:, 2 + n % 4, :], ACT.Exp, bias=mcol_b[:, 1:2],
                               scale=mcol_b[:, 0:1]).then_inc(s["s1_taken"], 1)
                        else:
                            af(probt[:, hh % 2, :], ps[:, 2 + n % 4, :], ACT.Exp, bias=mcol_b[:, 3:4],
                               scale=mcol_b[:, 2:3]).then_inc(s["s1_taken"], 1)

            roots(5)
            copy_xnT(2)
            gate_exp(1)

            def gelu(m, j):
                fn = F_TILES[j][1]
                act.wait_ge(s["g_done"], NF * m + j + 1)
                if not (isinstance(m, int) and m == 0):
                    act.wait_ge(s["h_done"], 1 + NF * m + j + 1 - NF)
                af(gg[0:fn, j, :], ps[0:fn, j, :], ACT.Gelu).then_inc(s["gelu_done"], 1)

            def gelus(m, first, last_one):
                for j in (1, 2):
                    fn = F_TILES[j][1]
                    act.wait_ge(s["g_done"], NF * m + j + 1)
                    act.wait_ge(s["h_done"], 1 + NF * m)
                    af(gg[0:fn, j, :], ps[0:fn, j, :], ACT.Gelu).then_inc(s["gelu_done"], 1)
                if not last_one:
                    gelu(m + 1, 0)

            gelu(0, 0)
            with act.Fori(0, E * B - UNITS, UNITS) as m0:
                for i in range(UNITS):
                    gelus(m0 + i, False, False)
            for i in range(UNITS):
                gelus(E * B - UNITS + i, False, i == UNITS - 1)

        @block.vector
        def _(dve):
            v = nc.vector
            tt, ts, tc, rd, stt = v.tensor_tensor, v.tensor_scalar, v.tensor_copy, v.tensor_reduce, v.scalar_tensor_tensor
            ln_n = [0]

            def norm(src, dst, n, parts=None, per_chunk=None):
                parts = parts or [P] * n
                for t in range(n):
                    ins = v.bn_stats(stats[0:parts[t], t, :], src(t))
                link(dve, ins)
                for t in range(n):
                    ins = v.bn_aggr(mv[0:parts[t], t, :], stats[0:parts[t], t, :])
                link(dve, ins)
                ts(mv[:, 0:n, 1], mv[:, 0:n, 1], EPS, None, ALU.add).then_inc(s["var_ready"], 1)
                dve.wait_ge(s["sd_ready"], ln_n[0] + 1)
                ln_n[0] += 1
                link(dve, v.reciprocal(rstd[:, 0:n], sd[:, 0:n]))
                for t in range(n):
                    ins = ts(dst(t), src(t), mv[0:parts[t], t, 0:1], rstd[0:parts[t], t:t + 1], ALU.subtract, ALU.mult)
                    if per_chunk is not None and t % QT == QT - 1:
                        ins.then_inc(per_chunk, 1)
                return ins

            for n in from_one["dve"]:
                dve.sem_inc(s[n], 1)

            dve.wait_ge(s["params_loaded"], 16 * N_PARAMS)
            v.memset(ones[:], 1.0)
            v.memset(ones_row[:], 1.0)
            v.memset(k_b[DH0:DH0 + 1, :, :, :].bitcast(F32), 1.0)
            tc(identb[:], ident)
            link(dve, v.memset(mv[:], 0.0))
            link(dve, tc(head_rows[:], ident[0:H1, 0:H1].unsqueeze(2).broadcast_to([H1, H1, P])))
            assert dve_n[0] == DVE_CONSTS

            dve.wait_ge(s["ctx_loaded"], 32)
            parts = [P, CT] * B
            norm(lambda t: ctx_in[0:parts[t], t // 2, t % 2, :], lambda t: ctxn[0:parts[t], t // 2, t % 2, :],
                 2 * B, parts).then_inc(s["ctxn_ready"], 1)
            dve.wait_ge(s["x_loaded"], 16)
            link(dve, norm(lambda t: x[:, t, :], lambda t: xn[:, t, :], NT))
            norm(lambda t: xn[:, t, :], lambda t: xn[:, t, :], NT).then_inc(s["lat_ready"], 1)
            dve.wait_ge(s["ctxT_done"], 1)
            for b in range(B):
                ins = ts(kvT[:, b, 0:C], ps[:, B + b, 0:C], cols[:, 0:1], cols[:, 1:2], ALU.mult, ALU.add)
            ins.then_inc(s["kvT_done"], 1)
            for b in range(B):
                dve.wait_ge(s["tr_done"], b + 2)
                ts(kvT[:, b, C:KV0], ps[:, b, :], cols[:, 2:3], cols[:, 3:4], ALU.mult, ALU.add).then_inc(s["kvT_done"], 1)

            dve.wait_ge(s["mask_loaded"], 16 * 6)
            tc(valid_m[:, 0, :], mask_i[:])
            tc(valid_m[:, 1, :], mask_t[:])
            link(dve, tc(valid_r, mask_r))
            ts(valid_m[:], valid_m[:], 0.0, None, ALU.not_equal)
            link(dve, ts(valid_r, valid_r, 0.0, None, ALU.not_equal))
            link(dve, rd(any_valid[:], valid_r, AX.X, ALU.max))
            for k in range(2):
                ts(mcol[:, :, 2 * k], valid_m[:, k, :], 1.0 / DH1 ** 0.5, None, ALU.mult)
                ts(mcol[:, :, 2 * k + 1], valid_m[:, k, :], -NEG, NEG, ALU.mult, ALU.add)
            link(dve, ts(valid_r[0:1], valid_r[0:1], -NEG, NEG, ALU.mult, ALU.add))
            for k in range(2):
                tt(mcol[:, :, 2 * k + 1], mcol[:, :, 2 * k + 1], any_valid[:], ALU.mult)
            link(dve, tc(neg_row[:], valid_r[0:1]))

            PV, PR = 5, 7

            def q_lo(w, st):
                for h in range(2):
                    dve.wait_ge(s["q_hi"], 2 * w + h + 1)
                    tt(q_b[0:DH0, st, h, :], ps[DH0 * h:DH0 * h + DH0, PR, :], q_a[0:DH0, st, h, :].bitcast(F32),
                       ALU.subtract).then_inc(s["q_lo"], 1)

            def k_lo(w, st, c):
                n = KV0 // 2
                for h in range(2):
                    dve.wait_ge(s["k_hi"], 4 * w + 2 * c + h + 1)
                    tt(k_a[DH0:P, st, h, c * n:(c + 1) * n], ps[DH0 * h:DH0 * h + DH0, PR, 0:n],
                       k_a[0:DH0, st, h, c * n:(c + 1) * n].bitcast(F32), ALU.subtract).then_inc(s["k_lo"], 1)

            def take_max(w, j):
                h, t = divmod(j, QT)
                dve.wait_ge(s["max_scores"], 8 * w + j + 1)
                rd(nmax[:, h, t:t + 1], ps[:, 0:2, 0:KC], AX.XY, ALU.max, negate=True).then_inc(s["max_done"], 1)

            def v_first(w, st):
                dve.wait_ge(s["v_proj"], 2 * w + 1)
                tc(v0[:, st, 0:4, :], ps[:, PR, :].rearrange("p (t d) -> p t d", t=4)).then_inc(s["v_dve"], 1)

            def invert(u, half):
                c = slice(half * (S // 2), (half + 1) * (S // 2))
                dve.wait_ge(s["den_read"], 1 + u + 1)
                v.reciprocal(rden[:, c], rden[:, c]).then_inc(s["recip"], 1)

            def head_out(u, st, pair, b):
                dve.wait_ge(s["recip"], 2 * u + 2)
                dve.wait_ge(s["pv_done"], u + 1)
                o = big[:, bass.ds(pair, 1), b * S:(b + 1) * S].rearrange("p a t -> p (a t)")
                tt(o, ps[:, PV + st, :], rden[:], ALU.mult).then_inc(s["head_done"], 1)

            def unit(u, i, pair, more):
                st, nst, w, z = i % 2, (i + 1) % 2, u + 1, u + 2
                if more > 0:
                    for j in range(1, 8):
                        take_max(w, j)
                if more > 1:
                    q_lo(z, st)
                    k_lo(z, st, 0)
                invert(u, 0)
                invert(u, 1)
                if more > 1:
                    k_lo(z, st, 1)
                    take_max(z, 0)
                head_out(u, st, pair, i % B)
                if more > 1:
                    v_first(z, st)

            q_lo(0, 0)
            k_lo(0, 0, 0)
            k_lo(0, 0, 1)
            v_first(0, 0)
            for j in range(8):
                take_max(0, j)
            q_lo(1, 1)
            k_lo(1, 1, 0)
            k_lo(1, 1, 1)
            take_max(1, 0)
            v_first(1, 1)
            with dve.Fori(0, PAIRS - 2, 2) as p0:
                for i in range(UNITS):
                    unit(p0 * B + i, i, p0 + i // B, 2)
            for i in range(UNITS):
                unit(PAIRS * B - UNITS + i, i, PAIRS - 2 + i // B, min(2, UNITS - 1 - i))

            for c in range(B):
                dve.wait_ge(s["wo_done"], c + 1)
                tt(x[:, QT * c:QT * (c + 1), :], x[:, QT * c:QT * (c + 1), :],
                   ps[:, c, :].rearrange("p (t d) -> p t d", t=QT), ALU.add).then_inc(s["x1_done"], 1)
            dve.wait_ge(s["x1_done"], B)

            def wide(col):
                return col[:].unsqueeze(2).broadcast_to([P, NT, E])

            def elements(row):
                return row.unsqueeze(1).broadcast_to([P, NT, E])

            def top2(stage, bias, renormalise):
                dve.wait_ge(s["logits_done"], stage + 1)
                z = ps[:, 0, 0:NT * E].rearrange("p (t e) -> p t e", e=E)
                if bias is not None:
                    link(dve, tt(lg[:], z, elements(bias), ALU.add))
                else:
                    link(dve, tc(lg[:], z))
                link(dve, rd(red[:], lg[:], AX.X, ALU.max))
                tt(lg[:], lg[:], wide(red), ALU.subtract).then_inc(s["logit_ready"], 1)
                dve.wait_ge(s["gate_exp"], stage + 1)
                link(dve, rd(red[:], gate[:], AX.X, ALU.add))
                link(dve, v.reciprocal(red[:], red[:]))
                link(dve, tt(gate[:], gate[:], wide(red), ALU.mult))
                link(dve, tc(g2[:], gate[:]))
                for k in range(2):
                    link(dve, rd(red[:], g2[:], AX.X, ALU.max))
                    link(dve, tt(eq[:], g2[:], wide(red), ALU.is_equal))
                    link(dve, tt(eq[:], eq[:], elements(expert_less_8), ALU.mult))
                    link(dve, rd(red[:], eq[:], AX.X, ALU.min))
                    link(dve, tt(eq[:], elements(expert_less_8), wide(red), ALU.is_equal))
                    if k == 0:
                        link(dve, tc(hot[:], eq[:]))
                        link(dve, stt(g2[:], eq[:], -2.0, g2[:], ALU.mult, ALU.add))
                    else:
                        link(dve, tt(hot[:], hot[:], eq[:], ALU.add))
                if renormalise:
                    link(dve, tt(hot[:], gate[:], hot[:], ALU.mult))
                    link(dve, rd(red[:], hot[:], AX.X, ALU.add))
                    link(dve, v.reciprocal(red[:], red[:]))
                    ins = tt(wgt[:], hot[:], wide(red), ALU.mult)
                else:
                    ins = tt(wgt[:], gate[:], hot[:], ALU.mult)
                ins.then_inc(s["w_done"], 1)
                dve.wait_ge(s["w_done"], stage + 1)

            norm(lambda t: x[:, t, :], lambda t: xn[:, t, :], NT, per_chunk=s["ln_ready"])
            top2(0, br[:], True)
            link(dve, rd(wsum[:], wgt[:], AX.X, ALU.add))
            for t in range(NT):
                ins = stt(x[:, t, :], xn[:, t, :], wsum[:, t:t + 1], x[:, t, :], ALU.mult, ALU.add)
            link(dve, ins)
            for c in range(B):
                dve.wait_ge(s["wb_done"], c + 1)
                dve.wait_ge(s["h_gelu"], c + 1)
                tt(hidden[:, c * S:(c + 1) * S], hidden[:, c * S:(c + 1) * S], ps[:, c, :], ALU.mult).then_inc(s["hw_done"], 1)
            for c in range(B):
                dve.wait_ge(s["up_done"], c + 1)
                tt(x[:, QT * c:QT * (c + 1), :], x[:, QT * c:QT * (c + 1), :],
                   ps[:, 4 + c, :].rearrange("p (t d) -> p t d", t=QT), ALU.add).then_inc(s["x2_done"], 1)
            dve.wait_ge(s["x2_done"], B)

            norm(lambda t: x[:, t, :], lambda t: xn[:, t, :], NT, per_chunk=s["ln_ready"])
            dve.wait_ge(s["ln_ready"], 2 * B)
            for c in range(B):
                ins = tt(x[:, QT * c:QT * (c + 1), :], x[:, QT * c:QT * (c + 1), :],
                         rows[:, 1:2, :].broadcast_to([P, QT, D]), ALU.add)
            link(dve, ins)
            link(dve, v.memset(k_tail, 0.0))
            with dve.Fori(0, B) as b:
                dve.wait_ge(s["kv1_done"], 1 + b + 1)
                dve.wait_ge(s["s1_taken"], 1 + b * 20)
                dve.wait_ge(s["x3_done"], 1 + b)
                ts(kTb, ps[:, 0, 0:C], cols[:, 6:7], None, ALU.add).then_inc(s["k1_done"], 1)
                tt(vb[:, 0, :], ps[:, 1, 0:D], rows[:, 0, :], ALU.add)
                tt(vb[0:CT, 1, :], ps[0:CT, 1, D:2 * D], rows[0:CT, 0, :], ALU.add).then_inc(s["k1_done"], 1)
                tc(mcol_b[:], mcol[:, bass.ds(b, 1), :].rearrange("p b c -> p (b c)")).then_inc(s["mc_done"], 1)
                dve.wait_ge(s["k1_done"], 3 * b + 2)
                tt(k_mask, kTb.unsqueeze(1).broadcast_to([P, H1, C]),
                   head_of_dim.unsqueeze(2).broadcast_to([P, H1, C]), ALU.mult).then_inc(s["k1_done"], 1)
                dve.wait_ge(s["k1_done"], 3 * b + 3)
                tc(kr, k_mask).then_inc(s["kr_done"], 1)
                tc(k_tail[:, :, 0:CT], k_mask[:, :, P:C])
                tt(vm.rearrange("p (g h) d -> p g h d", g=G1),
                   vb[:, 0, :].rearrange("p (g d) -> p g d", g=G1).unsqueeze(2).broadcast_to([P, G1, 4, 32]),
                   dim_in_group.unsqueeze(1).broadcast_to([P, G1, 4, 32]), ALU.mult)
                for g in range(G1):
                    ins = tt(vt[32 * g:32 * g + CT, :, :],
                             vb[0:CT, 1, 32 * g:32 * g + 32].unsqueeze(1).broadcast_to([CT, 4, 32]),
                             dim_in_group[0:CT, :, :], ALU.mult)
                ins.then_inc(s["v1_done"], 1)
                for n in range(QT * 6):
                    t, j = divmod(n, 6)
                    hn = min(3, H1 - 3 * j)
                    dve.wait_ge(s["max1"], b * (QT * 6) + n + 1)
                    rd(nmq[:, t, 3 * j:3 * j + hn], ps[:, 2 + n % 4, 0:hn * C].rearrange("p (h c) -> p h c", h=hn),
                       AX.X, ALU.max, negate=True).then_inc(s["max1_done"], 1)
                dve.wait_ge(s["pv1"], b + 1)
                dve.wait_ge(s["o1_done"], 1 + b)
                v.reciprocal(rden[:], ps[:, 7, :]).then_inc(s["den1_read"], 1)
                dve.wait_ge(s["den1_read"], b + 1)
                tt(oT, ps[:, 6, :], rden[:], ALU.mult).then_inc(s["o1_done"], 1)
                dve.wait_ge(s["wo1"], b + 1)
                xb = x[:, bass.ds(b * QT, QT), :]
                tt(xb, xb, ps[:, 0, :].rearrange("p (t d) -> p t d", t=QT), ALU.add).then_inc(s["x3_done"], 1)

            dve.wait_ge(s["x3_done"], 1 + B)
            norm(lambda t: x[:, t, :], lambda t: xn[:, t, :], NT, per_chunk=s["ln_ready"])
            link(dve, tt(acc, x[:], rows[:, 2:3, :].broadcast_to([P, NT, D]), ALU.add))
            top2(1, None, False)

            def h_prod(m, i, j):
                fn = F_TILES[j][1]
                dve.wait_ge(s["v_done"], NF * m + j + 1)
                dve.wait_ge(s["gelu_done"], 1 + NF * m + j + 1)
                tt(hid[0:fn, i % 2, j, :], gg[0:fn, j, :], ps[0:fn, 3 + j, :], ALU.mult).then_inc(s["h_done"], 1)

            def turn(m0, e0, last_turn):
                for i in range(UNITS):
                    m, c, par = m0 + i, i % B, i // B
                    h_prod(m, i, 1)
                    h_prod(m, i, 2)
                    if not (last_turn and i == UNITS - 1):
                        h_prod(m + 1, i + 1, 0)
                    if c == 0:
                        tc(wcol[:, par, :], wgt[:, :, bass.ds(e0 + par, 1)].rearrange("p t e -> p (t e)")).then_inc(s["r1_done"], 1)
                        dve.wait_ge(s["r1_done"], e0 + par + 1)
                    dve.wait_ge(s["down_done"], m + 1)
                    dve.wait_ge(s["acc_done"], 1 + m)
                    for t in range(QT):
                        o = acc[:, QT * c + t, :]
                        ins = stt(o, ps[:, 6 + i % 2, t * P:(t + 1) * P], wcol[:, par, QT * c + t:QT * c + t + 1], o,
                                  ALU.mult, ALU.add)
                    ins.then_inc(s["acc_done"], 1)

            h_prod(0, 0, 0)
            with dve.Fori(0, E - 2, 2) as e0:
                turn(e0 * B, e0, False)
            turn(E * B - UNITS, E - 2, True)

        @block.gpsimd
        def _(pool):
            g = nc.gpsimd
            g.memset(mask_t[:], 0).then_inc(s["pool_step"], 1)

            def sums(u, st, kt):
                n = min(P, KV0 - kt * P)
                for h in range(2):
                    pool.wait_ge(s["scores_taken"], 3 + 2 * NK * u + 2 * kt + h + 1)
                    if kt > 1:
                        pool.wait_ge(s["sum_step"], 2 * (NK - 1) * u + 2 * (kt - 2) + h + 1)
                    first = prob[0:n, h, 0, :] if kt == 1 else psums[0:n, h, :]
                    ins = g.tensor_tensor(psums[0:n, h, :], first, prob[0:n, h, kt, :], ALU.add)
                    ins.then_inc(s["sum_step"], 1)

            def unit(u, i):
                for kt in range(1, NK):
                    sums(u, i % 2, kt)

            with pool.Fori(0, PAIRS * B, UNITS) as u0:
                for i in range(UNITS):
                    unit(u0 + i, i)


_INS = ["x", "ctx_1024", "mask_Bx1x1xS2_ik0", "L0_xattn_ln1_w", "L0_xattn_ln1_b", "L0_xattn_ln2_w", "L0_xattn_ln2_b",
        "L0_xattn_Wq", "L0_xattn_Wkv", "L0_xattn_Wo", "L0_ffn_Wr", "L0_ffn_br", "L0_ffn_Wd", "L0_ffn_bd", "L0_ffn_Wu",
        "L0_ffn_bu", "L1_xattn_Wq", "L1_xattn_bq", "L1_xattn_Wk", "L1_xattn_bk", "L1_xattn_Wv", "L1_xattn_bv",
        "L1_xattn_Wo", "L1_xattn_bo", "L1_ffn_router_w", "L1_ffn_w1", "L1_ffn_v1", "L1_ffn_w2", "L1_ffn_bias"]


def kernel(**inputs):
    import concourse.bacc as _bacc
    from concourse.bass_utils import run_bass_kernel_spmd as _run

    nc = _bacc.Bacc("TRN2", target_bir_lowering=False, num_devices=1)
    arrays = {f"in_{n}_dram": np.ascontiguousarray(inputs[n]) for n in _INS}
    arrays["in_shape_consts_dram"] = constants()
    arrays["in_mask_by_key_dram"] = np.ascontiguousarray(np.asarray(inputs["mask_Bx1x1xS2_ik0"]).reshape(B, C).T)
    args = {n[3:-5]: nc.dram_tensor(n, v.shape, mybir.dt.from_np(v.dtype), kind="ExternalInput").ap()
            for n, v in arrays.items()}
    out = nc.dram_tensor("out_0_dram", (B, S, D), F32, kind="ExternalOutput").ap()
    build(nc, args, out)
    r = _run(nc, [arrays], core_ids=[0])
    return r.results[0]["out_0_dram"]
```

```python
from contextlib import ExitStack

import numpy as np

import concourse.bass as bass
from concourse import mybir

F32 = mybir.dt.float32
F32R = mybir.dt.float32r
BF16 = mybir.dt.bfloat16
I32 = mybir.dt.int32
ALU = mybir.AluOpType
ACT = mybir.ActivationFunctionType
AX = mybir.AxisListType

P = 128
B, S, D = 4, 512, 128
C = 154
CT = C - P
TOK = B * S
NT = TOK // P
QT = S // P
H0, DH0 = 16, 64
PAIRS = H0 // 2
KV0 = C + S
NK = -(-KV0 // P)
KTAIL = KV0 - (NK - 1) * P
KC = 334
E = 8
R = 16
F = 352
H1, DH1 = 16, 8
G1 = 4
F_TILES = [(j * P, min(P, F - j * P)) for j in range(-(-F // P))]
NF = len(F_TILES)
EPS = 1e-5
NEG = -1.0e9
UNITS = 2 * B
N_PARAMS = 17
GH = 4
UNITS1 = B * GH
TAILS = G1 * CT
DVE_CONSTS = 1


def constants():
    p = np.arange(P)
    ident = np.eye(P, dtype=np.float32)
    dim_in_group = np.broadcast_to((np.arange(32)[None, :] // DH1 == np.arange(4)[:, None]).reshape(1, 128), (P, 128))
    expert_less_8 = np.broadcast_to(np.arange(E)[None, :] - float(E), (P, E))
    expert_of_row = np.zeros((P, P), np.float32)
    expert_of_row[:E] = np.arange(P)[None, :] // R == np.arange(E)[:, None]
    group_of_row = p[:, None] // 32 == np.arange(G1)[None, :]
    slot = p % 32 // DH1
    low_slots = -np.stack([slot == 3, slot == 2], 1).astype(np.float32)
    fixed_rows = np.stack([p % 32 == 1, p % 32 == 0], 1)
    neg_place = np.zeros((P, P), np.float32)
    neg_place[0] = p % 32 == 1
    return np.concatenate([ident, dim_in_group, expert_less_8, expert_of_row, group_of_row, low_slots, fixed_rows,
                           neg_place], 1).astype(np.float32)


def tail_constants():
    p = np.arange(P)
    own = (p[:, None] // CT == p[None, :] // 32) & (p[:, None] < TAILS)
    head = p[None, :] % 32 // DH1 == np.arange(GH)[:, None]
    return np.concatenate([own[:, None, :], own[:, None, :] & head[None]], 1).reshape(P, -1).astype(np.float32)


C_IDENT, C_DIM, C_EXP, C_SEL, C_GROUP = 0, P, 2 * P, 2 * P + E, 3 * P + E
C_LOW, C_FIXED, C_PLACE = C_GROUP + G1, C_GROUP + G1 + 2, C_GROUP + G1 + 4
C_ALL = C_PLACE + P


def build(nc, a, out):
    with ExitStack() as ctx:
        def sb(name, shape, dt=F32):
            return ctx.enter_context(nc.sbuf_tensor(name, shape, dt))

        def sem(name):
            return ctx.enter_context(nc.semaphore(name))

        ps = ctx.enter_context(nc.psum_tensor("ps", [P, 8, 512], F32))

        consts = sb("consts", [P, C_ALL])
        ident = consts[:, C_IDENT:C_IDENT + P]
        dim_in_group = consts[:, C_DIM:C_DIM + P].rearrange("p (h d) -> p h d", h=4)
        expert_less_8 = consts[:, C_EXP:C_EXP + E]
        expert_of_row = consts[0:E, C_SEL:C_SEL + P]
        group_of_row = consts[:, C_GROUP:C_GROUP + G1]
        low_slots = consts[:, C_LOW:C_LOW + 2]
        fixed_rows = consts[:, C_FIXED:C_FIXED + 2]
        identb = sb("identb", [P, P], BF16)
        ones = sb("ones", [P, DH0])
        neg_place = sb("neg_place", [1, P], BF16)
        x = sb("x", [P, NT, D])
        stats = sb("stats", [P, NT, 6])
        mv = sb("mv", [P, NT, 2])
        sd = sb("sd", [P, NT])
        rstd = sb("rstd", [P, NT])
        ctxT = sb("ctxT", [P, B, C])
        kvT = sb("kvT", [P, B, KV0])
        cols = sb("cols", [P, 5])
        rows = sb("rows", [P, 2, D])
        wd = sb("wd", [P, E, R])
        wu = sb("wu", [P, D])
        wr0 = sb("wr0", [P, E])
        wr1 = sb("wr1", [P, E])
        br = sb("br", [P, E])
        bu = sb("bu", [E, D])
        wo1 = sb("wo1", [P, D])
        wo0 = sb("wo0", [P, PAIRS, D])
        big = sb("big", [P, PAIRS, TOK])

        wqkv = sb("wqkv", [P, 2, 3, P])
        k_a = sb("k_a", [P, 2, 2, KV0], F32R)
        k_b = sb("k_b", [DH0 + 1, 2, 2, KV0], F32R)
        q_a = sb("q_a", [P, 2, 2, S], F32R)
        q_b = sb("q_b", [DH0 + 1, 2, 2, S], F32R)
        v0 = sb("v0", [P, 2, NK, P])
        prob = sb("prob", [P, 2, NK, S])
        psums = sb("psums", [P, 2, S])
        nmax = sb("nmax", [P, 2, QT], BF16)
        rden = sb("rden", [P, S])

        lg = sb("lg", [P, NT, E])
        gate = sb("gate", [P, NT, E])
        g2 = sb("g2", [P, NT, E])
        eq = sb("eq", [P, NT, E])
        hot = sb("hot", [P, NT, E])
        wgt = sb("wgt", [P, NT, E])
        red = sb("red", [P, NT])
        wsum = sb("wsum", [P, NT])

        flat_big = big[:].rearrange("p a t -> p (a t)")
        flat_prob = prob[:].rearrange("p h k q -> p (h k q)")
        used = {"big": 0, "prob": 0}

        def carve(*shape, of="big"):
            flat, n = {"big": flat_big, "prob": flat_prob}[of], int(np.prod(shape))
            v = flat[:, used[of]:used[of] + n]
            used[of] += n
            names = "abcd"[:len(shape)]
            if len(shape) == 1:
                return v
            return v.rearrange(f"p ({' '.join(names)}) -> p {' '.join(names)}", **dict(zip(names, shape)))

        probm = carve(2, G1, S)
        probt = carve(2, S)
        vm = carve(GH, D)
        vt = carve(GH, D)
        q_full = carve(S)
        q_high = carve(S)
        k_full = carve(C)
        k_high = carve(C)
        k_slots = carve(C)
        cT = carve(P + TAILS)
        o_raw = carve(S)
        oT = carve(S)
        q_slots = q_a[:].rearrange("p s h q -> p (s h) q")
        k_diag = k_a[:].rearrange("p s h k -> p (s h k)")[:, 0:GH * G1 * C].rearrange(
            "p (h g c) -> p h g c", h=GH, g=G1)
        flat_kvT = kvT[:].rearrange("p b k -> p (b k)")
        wq1 = flat_kvT[:, 0:4 * D].rearrange("p (h m) -> p h m", h=GH)
        wk1 = flat_kvT[:, 4 * D:8 * D].rearrange("p (h m) -> p h m", h=GH)
        wv1h = flat_kvT[:, 8 * D:12 * D].rearrange("p (h m) -> p h m", h=GH)
        bv1 = flat_kvT[:, 12 * D:16 * D].rearrange("p (h m) -> p h m", h=GH)
        tails = psums[:].rearrange("p h q -> p (h q)")[:, 0:(GH + 1) * D].rearrange("p (h m) -> p h m", h=GH + 1)
        k_tails = sb("k_tails", [P, GH, TAILS], F32R)
        b_slots = sb("b_slots", [P, 2, GH])
        nmax1 = sb("nmax1", [P, QT, P], BF16)
        mask_i = sb("mask_i", [P, B], I32)
        mask_t = sb("mask_t", [P, B], I32)
        we1 = carve(2, 2, F)
        we1_split = sb("we1_split", [P, 2, 2, 2, F], F32R)
        xnT_low = k_a[:].rearrange("p s h k -> p (s h k)")[:, 0:TOK]
        xnT_high = q_a[:].rearrange("p s h q -> p (s h q)")
        we2 = carve(2, NF, D)
        wT = flat_big[0:E, 0:TOK]
        xn = carve(NT, D, of="prob")
        xnT = carve(TOK, of="prob")
        acc = carve(NT, D, of="prob")
        hidden = flat_big[:, TOK:2 * TOK]
        used["big"] = 0
        gg = carve(NF, S)
        hid = carve(2, NF, S)
        used["prob"] = NT * D
        ctx_in = carve(B, 2, D, of="prob")
        ctxn = carve(B, 2, D, of="prob")
        mask_r = carve(B, C, of="prob").bitcast(I32)
        valid_r = carve(B, C, of="prob")
        valid_m = sb("valid_m", [P, 2, B])
        any_valid = sb("any_valid", [P, B])
        mcol = sb("mcol", [P, B, 4])
        mcol_b = sb("mcol_b", [P, 4])
        neg_row = sb("neg_row", [1, B, C], BF16)

        wcol = sb("wcol", [P, 2, NT])

        names = """x_loaded ctx_loaded params_loaded mask_loaded pair_even pair_odd
            expert_even expert_odd dve_step pool_step var_ready sd_ready lat_ready ctxn_ready
            tr_done kvT_done ctxT_done q_proj k_proj v_proj q_hi q_lo q_dup k_hi k_lo k_dup v_dve v_act
            max_scores max_done row_proj row_copied scores scores_taken sum_step pv_done den_done
            den_read recip head_done wo_done x1_done ln_ready xt_done xnT_done logits_done logit_ready gate_exp hT_done h_gelu
            wT_tr wT_done wb_done hw_done up_done x2_done second_loaded b_slots_done ctx1_ready
            q1_proj q1_split q1_slots kv1_proj k1_split k1_slots k1_diag v1_dve v1_pool
            max1 max1_taken rows1 q1_max s1 s1_taken pv1 o1_copied recip1 o1_done wo1 x3_done mc_done
            xnT_low_done w_split
            r1_done g_done v_done gelu_done h_done down_done acc_done w_done
            out_stored""".split()
        s = {n: sem(n) for n in names}

        dve_n = [0]

        from_one = {"act": ["gelu_done", "den_read"],
                    "dve": ["head_done", "x3_done", "o1_done", "h_done", "acc_done"]}

        def link(eng, ins):
            dve_n[0] += 1
            ins.then_inc(s["dve_step"], 1)
            eng.wait_ge(s["dve_step"], dve_n[0])

        block = ctx.enter_context(nc.Block())

        @block.sync
        def _(sp):
            sp.dma_start(x[:], a["x"].rearrange("b (t p) d -> p (b t) d", p=P)).then_inc(s["x_loaded"], 16)
            c = a["ctx_1024"]
            sp.dma_start(ctx_in[:, :, 0, :], c[:, 0:P, :].rearrange("b p d -> p b d")).then_inc(s["ctx_loaded"], 16)
            sp.dma_start(ctx_in[0:CT, :, 1, :], c[:, P:C, :].rearrange("b p d -> p b d")).then_inc(s["ctx_loaded"], 16)
            params = [(consts[:], a["shape_consts"])]
            for n, name in enumerate(["L0_xattn_ln1_w", "L0_xattn_ln1_b", "L0_xattn_ln2_w", "L0_xattn_ln2_b",
                                      "L0_ffn_bd"]):
                src = a[name] if len(a[name].shape) == 1 else a[name].rearrange("e r -> (e r)")
                params.append((cols[:, n:n + 1], src.rearrange("(p o) -> p o", o=1)))
            for n, name in enumerate(["L1_xattn_bo", "L1_ffn_bias"]):
                params.append((rows[:, n, :], a[name].partition_broadcast(P)))
            params.append((wd[:], a["L0_ffn_Wd"].rearrange("e d r -> d e r")))
            params.append((wu[:], a["L0_ffn_Wu"].rearrange("e r d -> (e r) d")))
            params.append((wr0[:], a["L0_ffn_Wr"]))
            params.append((wr1[:], a["L1_ffn_router_w"]))
            params.append((br[:], a["L0_ffn_br"].partition_broadcast(P)))
            params.append((bu[:], a["L0_ffn_bu"]))
            params.append((wo1[:], a["L1_xattn_Wo"]))
            params.append((b_slots[:], a["b_slots"]))
            params.append((wo0[:], a["L0_xattn_Wo"].rearrange("(j p) d -> p j d", p=P)))
            for dst, src in params:
                sp.dma_start(dst, src).then_inc(s["params_loaded"], 16)
            assert len(params) == N_PARAMS
            wq, wkv = a["L0_xattn_Wq"], a["L0_xattn_Wkv"]

            def load_pair(pair, par, name):
                sp.dma_start(wqkv[:, par, 0, :], wq[:, bass.ds(pair * P, P)]).then_inc(s[name], 16)
                sp.dma_start(wqkv[:, par, 1, :], wkv[:, bass.ds(pair * P, P)]).then_inc(s[name], 16)
                sp.dma_start(wqkv[:, par, 2, :], wkv[:, bass.ds(pair * P + H0 * DH0, P)]).then_inc(s[name], 16)

            load_pair(0, 0, "pair_even")
            load_pair(1, 1, "pair_odd")
            m = a["mask_Bx1x1xS2_ik0"].rearrange("b o u c -> (b o u) c")
            sp.dma_start(mask_i[:], a["mask_by_key"][0:P, :]).then_inc(s["mask_loaded"], 16)
            sp.wait_ge(s["pool_step"], 1)
            for g in range(G1):
                sp.dma_start(mask_t[CT * g:CT * (g + 1), :], a["mask_by_key"][P:C, :]).then_inc(s["mask_loaded"], 16)
            sp.dma_start(mask_r, m.rearrange("b c -> (b c)").partition_broadcast(P)
                         .rearrange("p (b c) -> p b c", b=B)).then_inc(s["mask_loaded"], 16)

            def dups(w, st):
                for h in range(2):
                    sp.wait_ge(s["q_hi"], 2 * w + h + 1)
                    sp.dma_start(q_a[DH0:P, st, h, :].bitcast(F32),
                                 q_a[0:DH0, st, h, :].bitcast(F32)).then_inc(s["q_dup"], 16)
                for h in range(2):
                    sp.wait_ge(s["k_hi"], 4 * w + 3 + h)
                    sp.dma_start(k_b[0:DH0, st, h, :].bitcast(F32),
                                 k_a[0:DH0, st, h, :].bitcast(F32)).then_inc(s["k_dup"], 16)

            def turn(u0, last_turn):
                for i in range(UNITS - last_turn):
                    w = u0 + i + 1
                    dups(w, (i + 1) % 2)
                    if i % B == B - 2 and not last_turn:
                        sp.wait_ge(s["v_proj"], 2 * w + 2)
                        pair = it * 2 + 2 + i // B
                        load_pair(pair, i // B, ["pair_even", "pair_odd"][i // B])

            dups(0, 0)
            with sp.Fori(0, PAIRS // 2 - 1) as it:
                turn(it * UNITS, False)
            turn(PAIRS * B - UNITS, True)

            w1, v1, w2 = a["L1_ffn_w1"], a["L1_ffn_v1"], a["L1_ffn_w2"]

            def load_expert(e, par, name):
                sp.dma_start(we1[:, par, 0, :], w1[bass.ds(e, 1), :, :].rearrange("e d f -> d (e f)")).then_inc(s[name], 16)
                sp.dma_start(we1[:, par, 1, :], v1[bass.ds(e, 1), :, :].rearrange("e d f -> d (e f)")).then_inc(s[name], 16)
                for j, (f0, fn) in enumerate(F_TILES):
                    sp.dma_start(we2[0:fn, par, j, :],
                                 w2[bass.ds(e, 1), f0:f0 + fn, :].rearrange("e f d -> f (e d)")).then_inc(s[name], 16)

            sp.wait_ge(s["wo_done"], B)
            for dst, src in ((wq1, a["Wq_slots"]), (wk1, a["Wk_slots"]), (wv1h, a["Wv_heads"]),
                             (tails, a["tail_consts"].rearrange("p (h m) -> p h m", h=GH + 1)),
                             (bv1, a["bv_heads"].partition_broadcast(P).rearrange("p (h m) -> p h m", h=GH))):
                sp.dma_start(dst, src).then_inc(s["second_loaded"], 16)
            load_expert(0, 0, "expert_even")
            load_expert(1, 1, "expert_odd")
            with sp.Fori(1, E // 2) as it:
                sp.wait_ge(s["down_done"], it * (2 * B) - B)
                load_expert(it * 2, 0, "expert_even")
                sp.wait_ge(s["down_done"], it * (2 * B))
                load_expert(it * 2 + 1, 1, "expert_odd")

            o = out.rearrange("b (t p) d -> p (b t) d", p=P)
            for c in range(B):
                sp.wait_ge(s["acc_done"], 1 + (E - 1) * B + c + 1)
                sp.dma_start(o[:, QT * c:QT * (c + 1), :], acc[:, QT * c:QT * (c + 1), :]).then_inc(s["out_stored"], 16)
            sp.wait_ge(s["out_stored"], 16 * B)

        @block.tensor
        def _(pe):
            mm = nc.tensor.matmul
            pe.wait_ge(s["params_loaded"], 16 * N_PARAMS)
            pe.wait_ge(s["ctx_loaded"], 32)
            for b in range(B):
                nc.tensor.transpose(ps[:, B + b, 160:160 + P], ctx_in[:, b, 0, :], ident)
                nc.tensor.transpose(ps[:, B + b, 160 + P:160 + C], ctx_in[0:CT, b, 1, :], ident[0:CT, 0:CT])
            pe.wait_ge(s["ctxn_ready"], 1)
            for b in range(B):
                nc.tensor.transpose(ps[:, B + b, 0:P], ctxn[:, b, 0, :], ident)
                last = nc.tensor.transpose(ps[:, B + b, P:C], ctxn[0:CT, b, 1, :], ident[0:CT, 0:CT])
            last.then_inc(s["tr_done"], 1)
            pe.wait_ge(s["lat_ready"], 1)
            for b in range(B):
                for t in range(QT):
                    last = nc.tensor.transpose(ps[:, b, t * P:(t + 1) * P], xn[:, QT * b + t, :], ident)
                last.then_inc(s["tr_done"], 1)

            SC, PV, PR = 2, 5, 7

            def q_proj(w, b, wp):
                if not (isinstance(w, int) and w == 0):
                    pe.wait_ge(s["v_act"], 2 * w)
                mm(ps[:, PR, :], wqkv[:, wp, 0, :], kvT[:, b, C:KV0], start=True, stop=True).then_inc(s["q_proj"], 1)

            def k_proj(w, b, wp, c):
                if c == 0:
                    pe.wait_ge(s["q_hi"], 2 * w + 2)
                    pe.wait_ge(s["q_lo"], 2 * w + 2)
                else:
                    pe.wait_ge(s["k_hi"], 4 * w + 2)
                    pe.wait_ge(s["k_lo"], 4 * w + 2)
                n = KV0 // 2
                mm(ps[:, PR, 0:n], wqkv[:, wp, 1, :], kvT[:, b, c * n:(c + 1) * n],
                   start=True, stop=True).then_inc(s["k_proj"], 1)

            def v_proj(w, b, wp, c):
                if c == 0:
                    pe.wait_ge(s["k_hi"], 4 * w + 4)
                    pe.wait_ge(s["k_lo"], 4 * w + 4)
                else:
                    pe.wait_ge(s["v_dve"], w + 1)
                for t in (range(4) if c == 0 else range(4, NK)):
                    n = min(P, KV0 - t * P)
                    last = mm(ps[0:n, PR, (t % 4) * P:(t % 4 + 1) * P], kvT[:, b, t * P:t * P + n],
                              wqkv[:, wp, 2, :], start=True, stop=True)
                last.then_inc(s["v_proj"], 1)

            def max_scores(w, st, j):
                h, t = divmod(j, QT)
                if j == 0:
                    pe.wait_ge(s["q_hi"], 2 * w + 2)
                    pe.wait_ge(s["k_hi"], 4 * w + 4)
                    if not (isinstance(w, int) and w == 0):
                        pe.wait_ge(s["den_read"], 1 + w - 1)
                pe.wait_ge(s["max_done"], 8 * w + j)
                for c in range(2):
                    k0 = c * (KV0 - KC)
                    last = mm(ps[:, c, 0:KC], q_a[0:DH0, st, h, t * P:(t + 1) * P], k_a[0:DH0, st, h, k0:k0 + KC],
                              start=True, stop=True)
                last.then_inc(s["max_scores"], 1)

            def max_rows(w):
                pe.wait_ge(s["max_done"], 8 * w + 8)
                for t in range(QT):
                    for h in range(2):
                        last = mm(ps[32 * h:32 * h + 1, 0, t * P:(t + 1) * P], nmax[:, h, t:t + 1], identb[:],
                                  start=True, stop=True)
                last.then_inc(s["row_proj"], 1)

            def scores(u, st, kt, heads=(0, 1)):
                n = min(P, KV0 - kt * P)
                for h in heads:
                    j = 2 * kt + h
                    if kt == 0 and h == 0:
                        pe.wait_ge(s["row_copied"], 2 * u + 2)
                        pe.wait_ge(s["q_lo"], 2 * u + 2)
                        pe.wait_ge(s["q_dup"], 32 * u + 32)
                        pe.wait_ge(s["k_lo"], 4 * u + 4)
                        pe.wait_ge(s["k_dup"], 32 * u + 32)
                    pe.wait_ge(s["scores_taken"], 2 * NK * u + j + 1)
                    o = ps[0:n, SC + j % 3, :]
                    mm(o, k_a[:, st, h, kt * P:kt * P + n], q_a[:, st, h, :], start=True, stop=False)
                    mm(o, k_b[:, st, h, kt * P:kt * P + n], q_b[:, st, h, :],
                       start=False, stop=True).then_inc(s["scores"], 1)

            def pv(u, st, kt):
                n = min(P, KV0 - kt * P)
                if kt == 0:
                    pe.wait_ge(s["v_dve"], u + 1)
                    pe.wait_ge(s["v_act"], 2 * u + 2)
                pe.wait_ge(s["scores_taken"], 3 + 2 * NK * u + 2 * kt + 2)
                for h in range(2):
                    last = mm(ps[DH0 * h:DH0 * h + DH0, PV + st, :], v0[0:n, st, kt, DH0 * h:DH0 * h + DH0],
                              prob[0:n, h, kt, :], start=(kt == 0), stop=(kt == NK - 1))
                if kt == NK - 1:
                    last.then_inc(s["pv_done"], 1)

            def den(u, more):
                if more == 0:
                    pe.wait_ge(s["den_read"], 1 + u)
                pe.wait_ge(s["sum_step"], 2 * (NK - 1) * (u + 1))
                for h in range(2):
                    last = mm(ps[DH0 * h:DH0 * h + DH0, 1, :], ones[:], psums[:, h, :], start=True, stop=True)
                last.then_inc(s["den_done"], 1)

            def unit(u, i, more):
                st, nst, b1, wp1 = i % 2, (i + 1) % 2, (i + 1) % B, ((i + 1) // B) % 2
                b2, wp2 = (i + 2) % B, ((i + 2) // B) % 2
                w, z = u + 1, u + 2
                steps = max_scores if more > 0 else (lambda *a: None)
                scores(u, st, 1)
                if more > 0:
                    k_proj(w, b1, wp1, 1)
                pv(u, st, 0)
                steps(w, nst, 0)
                scores(u, st, 2, [0])
                if more > 0:
                    v_proj(w, b1, wp1, 0)
                steps(w, nst, 1)
                scores(u, st, 2, [1])
                pv(u, st, 1)
                steps(w, nst, 2)
                scores(u, st, 3)
                if more > 0:
                    v_proj(w, b1, wp1, 1)
                steps(w, nst, 3)
                pv(u, st, 2)
                scores(u, st, 4, [0])
                steps(w, nst, 4)
                scores(u, st, 4, [1])
                pv(u, st, 3)
                steps(w, nst, 5)
                scores(u, st, 5, [0])
                pv(u, st, 4)
                steps(w, nst, 6)
                scores(u, st, 5, [1])
                if more > 1:
                    q_proj(z, b2, wp2)
                steps(w, nst, 7)
                pv(u, st, 5)
                if more > 0:
                    max_rows(w)
                den(u, more)
                if more > 1:
                    k_proj(z, b2, wp2, 0)
                if more > 0:
                    scores(w, nst, 0)

            def turn(u0, last_turn):
                for i in range(UNITS):
                    if i == UNITS - 2 and not last_turn:
                        pe.wait_ge(s["pair_even"], pair_count(u0) + 48)
                    if i == B - 2:
                        pe.wait_ge(s["pair_odd"], pair_count(u0))
                    unit(u0 + i, i, min(2, UNITS - 1 - i) if last_turn else 2)

            def pair_count(u0):
                return u0 * (48 // UNITS) + 48

            pe.wait_ge(s["pair_even"], 48)
            pe.wait_ge(s["kvT_done"], B + 1)
            q_proj(0, 0, 0)
            k_proj(0, 0, 0, 0)
            k_proj(0, 0, 0, 1)
            v_proj(0, 0, 0, 0)
            v_proj(0, 0, 0, 1)
            for j in range(8):
                max_scores(0, 0, j)
            q_proj(1, 1, 0)
            max_rows(0)
            k_proj(1, 1, 0, 0)
            scores(0, 0, 0)
            with pe.Fori(0, PAIRS * B - UNITS, UNITS) as u0:
                turn(u0, False)
            turn(PAIRS * B - UNITS, True)

            pe.wait_ge(s["head_done"], 1 + PAIRS * B)
            for t in range(NT):
                for j in range(PAIRS):
                    last = mm(ps[:, t // QT, (t % QT) * P:(t % QT + 1) * P], big[:, j, t * P:(t + 1) * P],
                              wo0[:, j, :], start=(j == 0), stop=(j == PAIRS - 1))
                if t % QT == QT - 1:
                    last.then_inc(s["wo_done"], 1)

            def transpose_xn(stage):
                for c in range(B):
                    pe.wait_ge(s["ln_ready"], B * stage + c + 1)
                    for t in range(QT):
                        last = nc.tensor.transpose(ps[:, 4 + c, t * P:(t + 1) * P], xn[:, QT * c + t, :], ident)
                    last.then_inc(s["xt_done"], 1)

            def router(stage, w):
                pe.wait_ge(s["xnT_done"], B * (3 * stage + 1))
                for t in range(NT):
                    last = mm(ps[:, 0, t * E:(t + 1) * E], xnT[:, t * P:(t + 1) * P], w[:], start=True, stop=True)
                last.then_inc(s["logits_done"], 1)

            pe.wait_ge(s["x1_done"], B)
            transpose_xn(0)
            router(0, wr0)
            for c in range(B):
                mm(ps[:, 4 + c, :], wd[:].rearrange("p e r -> p (e r)"), xnT[:, c * S:(c + 1) * S],
                   start=True, stop=True).then_inc(s["hT_done"], 1)
            pe.wait_ge(s["w_done"], 1)
            for t in range(NT):
                last = nc.tensor.transpose(ps[0:E, t // QT, (t % QT) * P:(t % QT + 1) * P], wgt[:, t, :], ident)
            last.then_inc(s["wT_tr"], 1)
            pe.wait_ge(s["wT_done"], 1)
            for c in range(B):
                mm(ps[:, c, :], expert_of_row, wT[:, c * S:(c + 1) * S], start=True, stop=True).then_inc(s["wb_done"], 1)
            for t in range(NT):
                if t % QT == 0:
                    pe.wait_ge(s["hw_done"], t // QT + 1)
                    pe.wait_ge(s["h_gelu"], B)
                o = ps[:, 4 + t // QT, (t % QT) * P:(t % QT + 1) * P]
                mm(o, hidden[:, t * P:(t + 1) * P], wu[:], start=True, stop=False)
                last = mm(o, wT[:, t * P:(t + 1) * P], bu[:], start=False, stop=True)
                if t % QT == QT - 1:
                    last.then_inc(s["up_done"], 1)

            pe.wait_ge(s["x2_done"], B)
            transpose_xn(1)
            def q1_proj(z, hz, bz):
                if not (isinstance(z, int) and z < 2):
                    pe.wait_ge(s["q1_max"], z - 1)
                mm(ps[:, 4, :], wq1[:, hz, :], xnT[:, bass.ds(bz * S, S)],
                   start=True, stop=True).then_inc(s["q1_proj"], 1)

            def kv1_proj(z, hz, bz):
                if not (isinstance(z, int) and z == 0):
                    pe.wait_ge(s["k1_split"], 2 * z)
                    pe.wait_ge(s["v1_dve"], 2 * z)
                pe.wait_ge(s["ctx1_ready"], bz + 1)
                mm(ps[:, 5, 0:C], wk1[:, hz, :], ctxT[:, bass.ds(bz, 1), :].rearrange("p b c -> p (b c)"),
                   start=True, stop=False)
                mm(ps[:, 5, 0:C], neg_place[:], neg_row[:, bass.ds(bz, 1), :].rearrange("p b c -> p (b c)"),
                   start=False, stop=True)
                mm(ps[:, 5, 160:160 + D], cT[:, 0:P], wv1h[:, hz, :], start=True, stop=True)
                mm(ps[0:TAILS, 5, 160 + D:160 + 2 * D], cT[:, P:P + TAILS], wv1h[:, hz, :],
                   start=True, stop=True).then_inc(s["kv1_proj"], 1)

            def max1(w, hw, t, bw=None):
                if t == 0:
                    pe.wait_ge(s["q1_slots"], w + 1)
                    pe.wait_ge(s["k1_diag"], 2 * w + 2)
                    if bw is not None:
                        pe.wait_ge(s["x3_done"], 1 + bw)
                if not (isinstance(w, int) and w == 0 and t == 0):
                    pe.wait_ge(s["max1_taken"], QT * w + t)
                for c in range(2):
                    last = mm(ps[:, c, 0:2 * C], q_slots[:, hw, t * P:(t + 1) * P], k_diag[:, hw, 2 * c:2 * c + 2, :],
                              start=True, stop=True)
                last.then_inc(s["max1"], 1)

            def rows1(w, splits):
                pe.wait_ge(s["max1_taken"], QT * w + QT)
                pe.wait_ge(s["q1_split"], 2 * splits)
                for t in range(QT):
                    last = mm(ps[:, 4, t * P:(t + 1) * P], nmax1[:, t, :], identb[:], start=True, stop=True)
                last.then_inc(s["rows1"], 1)

            def scores1(u, h, j):
                if j == 0:
                    pe.wait_ge(s["q1_max"], u + 1)
                pe.wait_ge(s["s1_taken"], 5 * u + j + 1)
                n = (5 * h + j) % 2
                k = k_diag[:, h, j, 0:P] if j < G1 else k_tails[:, h, :]
                mm(ps[0:P if j < G1 else TAILS, 2 + n, :], k, q_slots[:, h, :],
                   start=True, stop=True).then_inc(s["s1"], 1)

            def pv1(u, h, bu=None):
                if bu is not None:
                    pe.wait_ge(s["o1_copied"], 2 * bu)
                pe.wait_ge(s["v1_dve"], 2 * u + 2)
                pe.wait_ge(s["s1_taken"], 2 + 5 * u + G1)
                for g in range(G1):
                    mm(ps[32 * g:32 * g + 32, 6, :], vm[:, h, 32 * g:32 * g + 32], probm[:, h % 2, g, :],
                       start=(h == 0), stop=False)

            def den1(h):
                for g in range(G1):
                    mm(ps[32 * g:32 * g + 32, 7, :], dim_in_group[:, h, :], probm[:, h % 2, g, :],
                       start=(h == 0), stop=False)

            def pv1_tail(u, h):
                pe.wait_ge(s["v1_pool"], u + 1)
                pe.wait_ge(s["s1_taken"], 2 + 5 * u + G1 + 1)
                mm(ps[:, 6, :], vt[0:TAILS, h, :], probt[0:TAILS, h % 2, :], start=False, stop=(h == GH - 1))

            def den1_tail(h):
                mm(ps[:, 7, :], tails[0:TAILS, 1 + h, :], probt[0:TAILS, h % 2, :],
                   start=False, stop=(h == GH - 1)).then_inc(s["pv1"], 1)

            def wo1_proj(b):
                pe.wait_ge(s["o1_done"], 1 + b + 1)
                for t in range(QT):
                    last = mm(ps[:, 0, t * P:(t + 1) * P], oT[:, t * P:(t + 1) * P], wo1[:], start=True, stop=True)
                last.then_inc(s["wo1"], 1)

            def unit1(b, i, more):
                u, w, z = GH * b + i, GH * b + i + 1, GH * b + i + 2
                hw, hz, bz = (i + 1) % GH, (i + 2) % GH, b + (i + 2) // GH
                first = isinstance(u, int) and u == 0
                scores1(u, i, 0)
                scores1(u, i, 1)
                if more > 0:
                    max1(w, hw, 0, b if i == 2 and not (isinstance(b, int) and b == 0) else None)
                if more > 1:
                    q1_proj(z, hz, bz)
                scores1(u, i, 2)
                if more > 0:
                    max1(w, hw, 1)
                scores1(u, i, 3)
                if more > 1:
                    kv1_proj(z, hz, bz)
                scores1(u, i, 4)
                if more > 0:
                    max1(w, hw, 2)
                pv1(u, i, b if i == 0 and not first else None)
                if more > 0:
                    max1(w, hw, 3)
                den1(i)
                if i == 1 and not (isinstance(b, int) and b == 0):
                    pe.wait_ge(s["max1_taken"], QT * w + QT)
                    wo1_proj(b - 1)
                pv1_tail(u, i)
                if more > 0:
                    rows1(w, z + 1 if more > 1 else z)
                den1_tail(i)

            pe.wait_ge(s["second_loaded"], 16 * 5)
            pe.wait_ge(s["xnT_done"], 2 * B)
            q1_proj(0, 0, 0)
            kv1_proj(0, 0, 0)
            for t in range(QT):
                max1(0, 0, t)
            pe.wait_ge(s["q1_split"], 2)
            q1_proj(1, 1, 0)
            kv1_proj(1, 1, 0)
            rows1(0, 2)
            unit1(0, 0, 2)
            unit1(0, 1, 2)
            with pe.Fori(0, B - 1) as b:
                unit1(b, 2, 2)
                unit1(b, 3, 2)
                unit1(b + 1, 0, 2)
                unit1(b + 1, 1, 2)
            unit1(B - 1, 2, 1)
            unit1(B - 1, 3, 0)
            wo1_proj(B - 1)

            pe.wait_ge(s["x3_done"], 1 + B)
            transpose_xn(2)
            router(1, wr1)
            pe.wait_ge(s["logit_ready"], 2)

            def up(m, c, par, j, dist):
                f0, fn = F_TILES[j]
                if not (isinstance(m, int) and m == 0):
                    pe.wait_ge(s["gelu_done"], 1 + NF * m - dist)
                    pe.wait_ge(s["h_done"], 1 + NF * m - dist)
                high, low = xnT_high[:, c * S:(c + 1) * S], xnT_low[:, c * S:(c + 1) * S]
                for k, done in enumerate(["g_done", "v_done"]):
                    o, w = ps[0:fn, NF * k + j, :], we1_split[:, par, :, k, f0:f0 + fn]
                    mm(o, w[:, 0, :], high, start=True, stop=False)
                    mm(o, w[:, 0, :], low, start=False, stop=False)
                    mm(o, w[:, 1, :], high, start=False, stop=True).then_inc(s[done], 1)

            def down(m, i):
                pe.wait_ge(s["h_done"], 1 + NF * m + NF)
                for t in range(QT):
                    for j, (f0, fn) in enumerate(F_TILES):
                        last = mm(ps[:, 6 + i % 2, t * P:(t + 1) * P], hid[0:fn, i % 2, j, t * P:(t + 1) * P],
                                  we2[0:fn, (i // B) % 2, j, :], start=(j == 0), stop=(j == NF - 1))
                last.then_inc(s["down_done"], 1)

            def turn1(m0, last_turn):
                for i in range(UNITS):
                    m, c, par = m0 + i, i % B, i // B
                    up(m, c, par, 1, 0)
                    up(m, c, par, 2, 0)
                    if not (last_turn and i == UNITS - 1):
                        if i == UNITS - 1:
                            pe.wait_ge(s["w_split"], m0 + 12)
                        if i == B - 1:
                            pe.wait_ge(s["w_split"], m0 + 8)
                        up(m + 1, (i + 1) % B, ((i + 1) // B) % 2, 0, NF - 1)
                    down(m, i)

            pe.wait_ge(s["w_split"], 4)
            pe.wait_ge(s["xnT_low_done"], B)
            up(0, 0, 0, 0, 0)
            with pe.Fori(0, E * B - UNITS, UNITS) as m0:
                turn1(m0, False)
            turn1(E * B - UNITS, True)

        @block.scalar
        def _(act):
            cp = nc.scalar.copy
            af = nc.scalar.activation
            for n in from_one["act"]:
                act.sem_inc(s[n], 1)

            def roots(n):
                act.wait_ge(s["var_ready"], n + 1)
                af(sd[:], mv[:, :, 1], ACT.Sqrt).then_inc(s["sd_ready"], 1)

            roots(0)
            roots(1)
            roots(2)
            act.wait_ge(s["tr_done"], 1)
            for b in range(B):
                last = cp(ctxT[:, b, :], ps[:, B + b, 160:160 + C])
            last.then_inc(s["ctxT_done"], 1)

            SC, PR = 2, 7
            s_taken = s["scores_taken"]

            def q_hi(w, st):
                act.wait_ge(s["q_proj"], w + 1)
                for h in range(2):
                    cp(q_a[0:DH0, st, h, :], ps[DH0 * h:DH0 * h + DH0, PR, :]).then_inc(s["q_hi"], 1)

            def k_hi(w, st, c):
                n = KV0 // 2
                act.wait_ge(s["k_proj"], 2 * w + c + 1)
                for h in range(2):
                    cp(k_a[0:DH0, st, h, c * n:(c + 1) * n],
                       ps[DH0 * h:DH0 * h + DH0, PR, 0:n]).then_inc(s["k_hi"], 1)

            def v_last(w, st):
                act.wait_ge(s["v_proj"], 2 * w + 2)
                cp(v0[:, st, 4, :], ps[:, PR, 0:P]).then_inc(s["v_act"], 1)
                cp(v0[0:KTAIL, st, 5, :], ps[0:KTAIL, PR, P:2 * P]).then_inc(s["v_act"], 1)

            def max_row(w, st):
                act.wait_ge(s["row_proj"], w + 1)
                for h in range(2):
                    cp(q_b[DH0:DH0 + 1, st, h, :], ps[32 * h:32 * h + 1, 0, :]).then_inc(s["row_copied"], 1)

            def sums_copy(u):
                act.wait_ge(s["den_done"], u + 1)
                act.wait_ge(s["head_done"], 1 + u)
                cp(rden[:], ps[:, 1, :]).then_inc(s["den_read"], 1)

            def exps(u, st, kt):
                n = min(P, KV0 - kt * P)
                if kt == 0 and not (isinstance(u, int) and u == 0):
                    act.wait_ge(s["sum_step"], 2 * (NK - 1) * (u - 1) + 2)
                for h in range(2):
                    j = 2 * kt + h
                    act.wait_ge(s["scores"], 2 * NK * u + j + 1)
                    af(prob[0:n, h, kt, :], ps[0:n, SC + j % 3, :], ACT.Exp,
                       scale=1.0 / DH0 ** 0.5).then_inc(s_taken, 1)

            def unit(u, i, more):
                st, nst, w, z = i % 2, (i + 1) % 2, u + 1, u + 2
                exps(u, st, 1)
                if more > 0:
                    k_hi(w, nst, 1)
                exps(u, st, 2)
                exps(u, st, 3)
                if more > 0:
                    v_last(w, nst)
                exps(u, st, 4)
                exps(u, st, 5)
                if more > 1:
                    q_hi(z, st)
                if more > 0:
                    max_row(w, nst)
                sums_copy(u)
                if more > 1:
                    k_hi(z, st, 0)
                if more > 0:
                    exps(w, nst, 0)

            act.sem_inc(s_taken, 3)
            act.wait_ge(s["dve_step"], DVE_CONSTS)
            q_hi(0, 0)
            k_hi(0, 0, 0)
            k_hi(0, 0, 1)
            v_last(0, 0)
            q_hi(1, 1)
            max_row(0, 0)
            k_hi(1, 1, 0)
            exps(0, 0, 0)
            with act.Fori(0, PAIRS * B - UNITS, UNITS) as u0:
                for i in range(UNITS):
                    unit(u0 + i, i, 2)
            for i in range(UNITS):
                unit(PAIRS * B - UNITS + i, i, min(2, UNITS - 1 - i))

            def copy_xnT(stage):
                for c in range(B):
                    act.wait_ge(s["xt_done"], B * stage + c + 1)
                    cp(xnT[:, c * S:(c + 1) * S], ps[:, 4 + c, :]).then_inc(s["xnT_done"], 1)

            def gate_exp(stage):
                act.wait_ge(s["logit_ready"], stage + 1)
                af(gate[:], lg[:], ACT.Exp).then_inc(s["gate_exp"], 1)

            roots(3)
            copy_xnT(0)
            gate_exp(0)
            for c in range(B):
                act.wait_ge(s["hT_done"], c + 1)
                af(hidden[:, c * S:(c + 1) * S], ps[:, 4 + c, :], ACT.Gelu_apprx_tanh, bias=cols[:, 4:5]).then_inc(s["h_gelu"], 1)
            act.wait_ge(s["wT_tr"], 1)
            for c in range(B):
                last = cp(wT[:, c * S:(c + 1) * S], ps[0:E, c, :])
            last.then_inc(s["wT_done"], 1)

            roots(4)
            copy_xnT(1)
            def q1_split(z, h):
                act.wait_ge(s["q1_proj"], z + 1)
                if not (isinstance(z, int) and z == 0):
                    act.wait_ge(s["q1_slots"], z)
                for o in (q_full, q_high.bitcast(F32R)):
                    af(o, ps[:, 4, :], ACT.Identity, bias=b_slots[:, 0, h:h + 1]).then_inc(s["q1_split"], 1)

            def k1_split(z, h):
                act.wait_ge(s["kv1_proj"], z + 1)
                if not (isinstance(z, int) and z == 0):
                    act.wait_ge(s["k1_slots"], z)
                for o in (k_full, k_high.bitcast(F32R)):
                    af(o, ps[:, 5, 0:C], ACT.Identity, bias=b_slots[:, 1, h:h + 1]).then_inc(s["k1_split"], 1)

            def exps1(u, h, j):
                if j == 0 and not (isinstance(u, int) and u < 2):
                    act.wait_ge(s["pv1"], u - 1)
                act.wait_ge(s["s1"], 5 * u + j + 1)
                n = (5 * h + j) % 2
                if j < G1:
                    af(probm[:, h % 2, j, :], ps[:, 2 + n, :], ACT.Exp, bias=mcol_b[:, 1:2],
                       scale=mcol_b[:, 0:1]).then_inc(s["s1_taken"], 1)
                else:
                    af(probt[0:TAILS, h % 2, :], ps[0:TAILS, 2 + n, :], ACT.Exp, bias=mcol_b[0:TAILS, 3:4],
                       scale=mcol_b[0:TAILS, 2:3]).then_inc(s["s1_taken"], 1)

            def mask_cols(b):
                if not (isinstance(b, int) and b == 0):
                    act.wait_ge(s["s1_taken"], 2 + 5 * GH * b)
                cp(mcol_b[:], mcol[:, bass.ds(b, 1), :].rearrange("p b c -> p (b c)")).then_inc(s["mc_done"], 1)
                act.wait_ge(s["mc_done"], b + 1)

            def results(b):
                act.wait_ge(s["pv1"], GH * b + GH)
                act.wait_ge(s["o1_done"], 1 + b)
                cp(o_raw, ps[:, 6, :]).then_inc(s["o1_copied"], 1)
                cp(rden[:], ps[:, 7, :]).then_inc(s["o1_copied"], 1)

            def unit1(b, i, more):
                u, z, hz = GH * b + i, GH * b + i + 2, (i + 2) % GH
                if i == 0:
                    mask_cols(b)
                exps1(u, i, 0)
                if i == 0 and not (isinstance(b, int) and b == 0):
                    results(b - 1)
                exps1(u, i, 1)
                exps1(u, i, 2)
                exps1(u, i, 3)
                if more > 1:
                    k1_split(z, hz)
                exps1(u, i, 4)
                if more > 1:
                    q1_split(z, hz)

            act.sem_inc(s["s1_taken"], 2)
            act.wait_ge(s["b_slots_done"], 1)
            q1_split(0, 0)
            k1_split(0, 0)
            q1_split(1, 1)
            k1_split(1, 1)
            unit1(0, 0, 2)
            unit1(0, 1, 2)
            with act.Fori(0, B - 1) as b:
                unit1(b, 2, 2)
                unit1(b, 3, 2)
                unit1(b + 1, 0, 2)
                unit1(b + 1, 1, 2)
            unit1(B - 1, 2, 1)
            unit1(B - 1, 3, 0)
            results(B - 1)

            roots(5)
            for c in range(B):
                act.wait_ge(s["xt_done"], 2 * B + c + 1)
                cp(xnT_high[:, c * S:(c + 1) * S], ps[:, 4 + c, :]).then_inc(s["xnT_done"], 1)
                cp(xnT[:, c * S:(c + 1) * S], ps[:, 4 + c, :]).then_inc(s["xnT_done"], 1)
            gate_exp(1)

            def gelu(m, j):
                fn = F_TILES[j][1]
                act.wait_ge(s["g_done"], NF * m + j + 1)
                if not (isinstance(m, int) and m == 0):
                    act.wait_ge(s["h_done"], 1 + NF * m + j + 1 - NF)
                af(gg[0:fn, j, :], ps[0:fn, j, :], ACT.Gelu).then_inc(s["gelu_done"], 1)

            def gelus(m, first, last_one):
                for j in (1, 2):
                    fn = F_TILES[j][1]
                    act.wait_ge(s["g_done"], NF * m + j + 1)
                    act.wait_ge(s["h_done"], 1 + NF * m)
                    af(gg[0:fn, j, :], ps[0:fn, j, :], ACT.Gelu).then_inc(s["gelu_done"], 1)
                if not last_one:
                    gelu(m + 1, 0)

            gelu(0, 0)
            with act.Fori(0, E * B - UNITS, UNITS) as m0:
                for i in range(UNITS):
                    gelus(m0 + i, False, False)
            for i in range(UNITS):
                gelus(E * B - UNITS + i, False, i == UNITS - 1)

        @block.vector
        def _(dve):
            v = nc.vector
            tt, ts, tc, rd, stt = v.tensor_tensor, v.tensor_scalar, v.tensor_copy, v.tensor_reduce, v.scalar_tensor_tensor
            ln_n = [0]

            def norm(src, dst, n, parts=None, per_chunk=None):
                parts = parts or [P] * n
                for t in range(n):
                    ins = v.bn_stats(stats[0:parts[t], t, :], src(t))
                link(dve, ins)
                for t in range(n):
                    ins = v.bn_aggr(mv[0:parts[t], t, :], stats[0:parts[t], t, :])
                link(dve, ins)
                ts(mv[:, 0:n, 1], mv[:, 0:n, 1], EPS, None, ALU.add).then_inc(s["var_ready"], 1)
                dve.wait_ge(s["sd_ready"], ln_n[0] + 1)
                ln_n[0] += 1
                link(dve, v.reciprocal(rstd[:, 0:n], sd[:, 0:n]))
                for t in range(n):
                    ins = ts(dst(t), src(t), mv[0:parts[t], t, 0:1], rstd[0:parts[t], t:t + 1], ALU.subtract, ALU.mult)
                    if per_chunk is not None and t % QT == QT - 1:
                        ins.then_inc(per_chunk, 1)
                return ins

            for n in from_one["dve"]:
                dve.sem_inc(s[n], 1)

            dve.wait_ge(s["params_loaded"], 16 * N_PARAMS)
            v.memset(ones[:], 1.0)
            tc(neg_place[:], consts[0:1, C_PLACE:C_PLACE + P])
            v.memset(nmax1[:], 0.0)
            tt(b_slots[:], b_slots[:], fixed_rows.unsqueeze(2).broadcast_to([P, 2, GH]), ALU.add).then_inc(s["b_slots_done"], 1)
            v.memset(k_b[DH0:DH0 + 1, :, :, :].bitcast(F32), 1.0)
            tc(identb[:], ident)
            link(dve, v.memset(mv[:], 0.0))
            assert dve_n[0] == DVE_CONSTS

            dve.wait_ge(s["ctx_loaded"], 32)
            parts = [P, CT] * B
            norm(lambda t: ctx_in[0:parts[t], t // 2, t % 2, :], lambda t: ctxn[0:parts[t], t // 2, t % 2, :],
                 2 * B, parts).then_inc(s["ctxn_ready"], 1)
            dve.wait_ge(s["x_loaded"], 16)
            link(dve, norm(lambda t: x[:, t, :], lambda t: xn[:, t, :], NT))
            norm(lambda t: xn[:, t, :], lambda t: xn[:, t, :], NT).then_inc(s["lat_ready"], 1)
            dve.wait_ge(s["ctxT_done"], 1)
            for b in range(B):
                ins = ts(kvT[:, b, 0:C], ps[:, B + b, 0:C], cols[:, 0:1], cols[:, 1:2], ALU.mult, ALU.add)
            ins.then_inc(s["kvT_done"], 1)
            for b in range(B):
                dve.wait_ge(s["tr_done"], b + 2)
                ts(kvT[:, b, C:KV0], ps[:, b, :], cols[:, 2:3], cols[:, 3:4], ALU.mult, ALU.add).then_inc(s["kvT_done"], 1)

            dve.wait_ge(s["mask_loaded"], 16 * 6)
            tc(valid_m[:, 0, :], mask_i[:])
            tc(valid_m[:, 1, :], mask_t[:])
            link(dve, tc(valid_r, mask_r))
            ts(valid_m[:], valid_m[:], 0.0, None, ALU.not_equal)
            link(dve, ts(valid_r, valid_r, 0.0, None, ALU.not_equal))
            link(dve, rd(any_valid[:], valid_r, AX.X, ALU.max))
            for k in range(2):
                ts(mcol[:, :, 2 * k], valid_m[:, k, :], 1.0 / DH1 ** 0.5, None, ALU.mult)
                ts(mcol[:, :, 2 * k + 1], valid_m[:, k, :], -NEG, NEG, ALU.mult, ALU.add)
            link(dve, ts(valid_r[0:1], valid_r[0:1], -NEG, NEG, ALU.mult, ALU.add))
            for k in range(2):
                tt(mcol[:, :, 2 * k + 1], mcol[:, :, 2 * k + 1], any_valid[:], ALU.mult)
            link(dve, tc(neg_row[:], valid_r[0:1]))

            PV, PR = 5, 7

            def q_lo(w, st):
                for h in range(2):
                    dve.wait_ge(s["q_hi"], 2 * w + h + 1)
                    tt(q_b[0:DH0, st, h, :], ps[DH0 * h:DH0 * h + DH0, PR, :], q_a[0:DH0, st, h, :].bitcast(F32),
                       ALU.subtract).then_inc(s["q_lo"], 1)

            def k_lo(w, st, c):
                n = KV0 // 2
                for h in range(2):
                    dve.wait_ge(s["k_hi"], 4 * w + 2 * c + h + 1)
                    tt(k_a[DH0:P, st, h, c * n:(c + 1) * n], ps[DH0 * h:DH0 * h + DH0, PR, 0:n],
                       k_a[0:DH0, st, h, c * n:(c + 1) * n].bitcast(F32), ALU.subtract).then_inc(s["k_lo"], 1)

            def take_max(w, j):
                h, t = divmod(j, QT)
                dve.wait_ge(s["max_scores"], 8 * w + j + 1)
                rd(nmax[:, h, t:t + 1], ps[:, 0:2, 0:KC], AX.XY, ALU.max, negate=True).then_inc(s["max_done"], 1)

            def v_first(w, st):
                dve.wait_ge(s["v_proj"], 2 * w + 1)
                tc(v0[:, st, 0:4, :], ps[:, PR, :].rearrange("p (t d) -> p t d", t=4)).then_inc(s["v_dve"], 1)

            def invert(u, part):
                c = slice(part * P, (part + 1) * P)
                dve.wait_ge(s["den_read"], 1 + u + 1)
                v.reciprocal(rden[:, c], rden[:, c]).then_inc(s["recip"], 1)

            def head_out(u, st, pair, b):
                dve.wait_ge(s["recip"], QT * u + QT)
                dve.wait_ge(s["pv_done"], u + 1)
                o = big[:, bass.ds(pair, 1), b * S:(b + 1) * S].rearrange("p a t -> p (a t)")
                tt(o, ps[:, PV + st, :], rden[:], ALU.mult).then_inc(s["head_done"], 1)

            def unit(u, i, pair, more):
                st, nst, w, z = i % 2, (i + 1) % 2, u + 1, u + 2
                if more > 0:
                    take_max(w, 7)
                if more > 1:
                    q_lo(z, st)
                invert(u, 0)
                if more > 1:
                    k_lo(z, st, 0)
                invert(u, 1)
                if more > 1:
                    k_lo(z, st, 1)
                    take_max(z, 0)
                    v_first(z, st)
                    take_max(z, 1)
                invert(u, 2)
                if more > 1:
                    take_max(z, 2)
                invert(u, 3)
                if more > 1:
                    take_max(z, 3)
                if more > 1:
                    take_max(z, 4)
                head_out(u, st, pair, i % B)
                if more > 1:
                    take_max(z, 5)
                    take_max(z, 6)

            q_lo(0, 0)
            k_lo(0, 0, 0)
            k_lo(0, 0, 1)
            v_first(0, 0)
            for j in range(8):
                take_max(0, j)
            q_lo(1, 1)
            k_lo(1, 1, 0)
            k_lo(1, 1, 1)
            take_max(1, 0)
            v_first(1, 1)
            for j in range(1, 7):
                take_max(1, j)
            with dve.Fori(0, PAIRS - 2, 2) as p0:
                for i in range(UNITS):
                    unit(p0 * B + i, i, p0 + i // B, 2)
            for i in range(UNITS):
                unit(PAIRS * B - UNITS + i, i, PAIRS - 2 + i // B, min(2, UNITS - 1 - i))

            for c in range(B):
                dve.wait_ge(s["wo_done"], c + 1)
                tt(x[:, QT * c:QT * (c + 1), :], x[:, QT * c:QT * (c + 1), :],
                   ps[:, c, :].rearrange("p (t d) -> p t d", t=QT), ALU.add).then_inc(s["x1_done"], 1)
            dve.wait_ge(s["x1_done"], B)

            def wide(col):
                return col[:].unsqueeze(2).broadcast_to([P, NT, E])

            def elements(row):
                return row.unsqueeze(1).broadcast_to([P, NT, E])

            def top2(stage, bias, renormalise):
                dve.wait_ge(s["logits_done"], stage + 1)
                z = ps[:, 0, 0:NT * E].rearrange("p (t e) -> p t e", e=E)
                if bias is not None:
                    link(dve, tt(lg[:], z, elements(bias), ALU.add))
                else:
                    link(dve, tc(lg[:], z))
                link(dve, rd(red[:], lg[:], AX.X, ALU.max))
                tt(lg[:], lg[:], wide(red), ALU.subtract).then_inc(s["logit_ready"], 1)
                dve.wait_ge(s["gate_exp"], stage + 1)
                link(dve, rd(red[:], gate[:], AX.X, ALU.add))
                link(dve, v.reciprocal(red[:], red[:]))
                link(dve, tt(gate[:], gate[:], wide(red), ALU.mult))
                link(dve, tc(g2[:], gate[:]))
                for k in range(2):
                    link(dve, rd(red[:], g2[:], AX.X, ALU.max))
                    link(dve, tt(eq[:], g2[:], wide(red), ALU.is_equal))
                    link(dve, tt(eq[:], eq[:], elements(expert_less_8), ALU.mult))
                    link(dve, rd(red[:], eq[:], AX.X, ALU.min))
                    link(dve, tt(eq[:], elements(expert_less_8), wide(red), ALU.is_equal))
                    if k == 0:
                        link(dve, tc(hot[:], eq[:]))
                        link(dve, stt(g2[:], eq[:], -2.0, g2[:], ALU.mult, ALU.add))
                    else:
                        link(dve, tt(hot[:], hot[:], eq[:], ALU.add))
                if renormalise:
                    link(dve, tt(hot[:], gate[:], hot[:], ALU.mult))
                    link(dve, rd(red[:], hot[:], AX.X, ALU.add))
                    link(dve, v.reciprocal(red[:], red[:]))
                    ins = tt(wgt[:], hot[:], wide(red), ALU.mult)
                else:
                    ins = tt(wgt[:], gate[:], hot[:], ALU.mult)
                ins.then_inc(s["w_done"], 1)
                dve.wait_ge(s["w_done"], stage + 1)

            norm(lambda t: x[:, t, :], lambda t: xn[:, t, :], NT, per_chunk=s["ln_ready"])
            top2(0, br[:], True)
            link(dve, rd(wsum[:], wgt[:], AX.X, ALU.add))
            for t in range(NT):
                ins = stt(x[:, t, :], xn[:, t, :], wsum[:, t:t + 1], x[:, t, :], ALU.mult, ALU.add)
            link(dve, ins)
            for c in range(B):
                dve.wait_ge(s["wb_done"], c + 1)
                dve.wait_ge(s["h_gelu"], c + 1)
                tt(hidden[:, c * S:(c + 1) * S], hidden[:, c * S:(c + 1) * S], ps[:, c, :], ALU.mult).then_inc(s["hw_done"], 1)
            for c in range(B):
                dve.wait_ge(s["up_done"], c + 1)
                tt(x[:, QT * c:QT * (c + 1), :], x[:, QT * c:QT * (c + 1), :],
                   ps[:, 4 + c, :].rearrange("p (t d) -> p t d", t=QT), ALU.add).then_inc(s["x2_done"], 1)
            dve.wait_ge(s["x2_done"], B)

            norm(lambda t: x[:, t, :], lambda t: xn[:, t, :], NT, per_chunk=s["ln_ready"])
            dve.wait_ge(s["ln_ready"], 2 * B)
            for c in range(B):
                ins = tt(x[:, QT * c:QT * (c + 1), :], x[:, QT * c:QT * (c + 1), :],
                         rows[:, 0:1, :].broadcast_to([P, QT, D]), ALU.add)
            link(dve, ins)

            def q1_slots(z, h):
                dve.wait_ge(s["q1_split"], 2 * z + 2)
                if not (isinstance(z, int) and z < GH):
                    dve.wait_ge(s["s1"], 5 * (z - GH) + 5)
                stt(q_slots[:, h, :], q_high, low_slots[:, 0:1], q_full, ALU.mult, ALU.add).then_inc(s["q1_slots"], 1)

            def k1_slots(z, h):
                dve.wait_ge(s["k1_split"], 2 * z + 2)
                if not (isinstance(z, int) and z == 0):
                    dve.wait_ge(s["k1_diag"], 2 * z)
                stt(k_slots.bitcast(F32R), k_high, low_slots[:, 1:2], k_full, ALU.mult, ALU.add).then_inc(s["k1_slots"], 1)

            def v1_bias(z, h):
                dve.wait_ge(s["k1_split"], 2 * z + 2)
                if not (isinstance(z, int) and z < GH):
                    dve.wait_ge(s["pv1"], z - GH + 1)
                tt(vm[:, h, :], ps[:, 5, 160:160 + D], bv1[:, h, :], ALU.add).then_inc(s["v1_dve"], 1)
                tt(vt[0:TAILS, h, :], ps[0:TAILS, 5, 160 + D:160 + 2 * D], bv1[0:TAILS, h, :],
                   ALU.add).then_inc(s["v1_dve"], 1)

            def take_max1(w, t):
                dve.wait_ge(s["max1"], QT * w + t + 1)
                rd(nmax1[:, t, :].rearrange("p (g x) -> p g x", g=G1)[:, :, 0:1].rearrange("p (c g) x -> p c (g x)", c=2),
                   ps[:, 0:2, 0:2 * C].rearrange("p c (g k) -> p c g k", g=2), AX.X, ALU.max,
                   negate=True).then_inc(s["max1_taken"], 1)

            def q1_max(w, h):
                dve.wait_ge(s["rows1"], w + 1)
                dve.wait_ge(s["q1_slots"], w + 1)
                tt(q_slots[:, h, :], q_slots[:, h, :].bitcast(F32), ps[:, 4, :], ALU.add).then_inc(s["q1_max"], 1)

            def invert1(b, part):
                c = slice(part * P, (part + 1) * P)
                dve.wait_ge(s["o1_copied"], 2 * b + 2)
                v.reciprocal(rden[:, c], rden[:, c]).then_inc(s["recip1"], 1)

            def result1(b):
                dve.wait_ge(s["recip1"], QT * b + QT)
                tt(oT, o_raw, rden[:], ALU.mult).then_inc(s["o1_done"], 1)

            def add1(b):
                dve.wait_ge(s["wo1"], b + 1)
                xb = x[:, bass.ds(b * QT, QT), :]
                tt(xb, xb, ps[:, 0, :].rearrange("p (t d) -> p t d", t=QT), ALU.add).then_inc(s["x3_done"], 1)

            def unit1(b, i, more):
                w, z, hw, hz = GH * b + i + 1, GH * b + i + 2, (i + 1) % GH, (i + 2) % GH
                ends = i < 2 and not (isinstance(b, int) and b == 0)
                for t in range(QT - 1 if more > 0 else 0):
                    take_max1(w, t)
                    if ends and t < 2:
                        invert1(b - 1, 2 * i + t)
                if more > 1:
                    v1_bias(z, hz)
                    k1_slots(z, hz)
                if ends and i == 1:
                    result1(b - 1)
                if more > 0:
                    take_max1(w, QT - 1)
                if more > 1:
                    q1_slots(z, hz)
                if ends and i == 1:
                    add1(b - 1)
                if more > 0:
                    q1_max(w, hw)

            v1_bias(0, 0)
            q1_slots(0, 0)
            k1_slots(0, 0)
            for t in range(QT):
                take_max1(0, t)
            q1_slots(1, 1)
            v1_bias(1, 1)
            q1_max(0, 0)
            k1_slots(1, 1)
            unit1(0, 0, 2)
            unit1(0, 1, 2)
            with dve.Fori(0, B - 1) as b:
                unit1(b, 2, 2)
                unit1(b, 3, 2)
                unit1(b + 1, 0, 2)
                unit1(b + 1, 1, 2)
            unit1(B - 1, 2, 1)
            for part in range(QT):
                invert1(B - 1, part)
            result1(B - 1)
            add1(B - 1)

            dve.wait_ge(s["x3_done"], 1 + B)
            norm(lambda t: x[:, t, :], lambda t: xn[:, t, :], NT, per_chunk=s["ln_ready"])
            link(dve, tt(acc, x[:], rows[:, 1:2, :].broadcast_to([P, NT, D]), ALU.add))
            for c in range(B):
                dve.wait_ge(s["xnT_done"], 2 * B + 2 * c + 2)
                tt(xnT_low[:, c * S:(c + 1) * S], ps[:, 4 + c, :], xnT_high[:, c * S:(c + 1) * S].bitcast(F32),
                   ALU.subtract).then_inc(s["xnT_low_done"], 1)
            top2(1, None, False)

            def h_prod(m, i, j):
                fn = F_TILES[j][1]
                dve.wait_ge(s["v_done"], NF * m + j + 1)
                dve.wait_ge(s["gelu_done"], 1 + NF * m + j + 1)
                tt(hid[0:fn, i % 2, j, :], gg[0:fn, j, :], ps[0:fn, 3 + j, :], ALU.mult).then_inc(s["h_done"], 1)

            def turn(m0, e0, last_turn):
                for i in range(UNITS):
                    m, c, par = m0 + i, i % B, i // B
                    h_prod(m, i, 1)
                    h_prod(m, i, 2)
                    if not (last_turn and i == UNITS - 1):
                        h_prod(m + 1, i + 1, 0)
                    if c == 0:
                        tc(wcol[:, par, :], wgt[:, :, bass.ds(e0 + par, 1)].rearrange("p t e -> p (t e)")).then_inc(s["r1_done"], 1)
                        dve.wait_ge(s["r1_done"], e0 + par + 1)
                    dve.wait_ge(s["down_done"], m + 1)
                    dve.wait_ge(s["acc_done"], 1 + m)
                    for t in range(QT):
                        o = acc[:, QT * c + t, :]
                        ins = stt(o, ps[:, 6 + i % 2, t * P:(t + 1) * P], wcol[:, par, QT * c + t:QT * c + t + 1], o,
                                  ALU.mult, ALU.add)
                    ins.then_inc(s["acc_done"], 1)

            h_prod(0, 0, 0)
            with dve.Fori(0, E - 2, 2) as e0:
                turn(e0 * B, e0, False)
            turn(E * B - UNITS, E - 2, True)

        @block.gpsimd
        def _(pool):
            g = nc.gpsimd
            g.memset(mask_t[:], 0).then_inc(s["pool_step"], 1)

            def sums(u, st, kt):
                n = min(P, KV0 - kt * P)
                for h in range(2):
                    pool.wait_ge(s["scores_taken"], 3 + 2 * NK * u + 2 * kt + h + 1)
                    if kt > 1:
                        pool.wait_ge(s["sum_step"], 2 * (NK - 1) * u + 2 * (kt - 2) + h + 1)
                    first = prob[0:n, h, 0, :] if kt == 1 else psums[0:n, h, :]
                    ins = g.tensor_tensor(psums[0:n, h, :], first, prob[0:n, h, kt, :], ALU.add)
                    ins.then_inc(s["sum_step"], 1)

            def unit(u, i):
                for kt in range(1, NK):
                    sums(u, i % 2, kt)

            with pool.Fori(0, PAIRS * B, UNITS) as u0:
                for i in range(UNITS):
                    unit(u0 + i, i)

            def context1(b):
                if not (isinstance(b, int) and b == 0):
                    pool.wait_ge(s["kv1_proj"], GH * b)
                src = ctxT[:, bass.ds(b, 1), :].rearrange("p b c -> p (b c)")
                g.tensor_copy(cT[:, 0:P], src[:, 0:P])
                g.tensor_copy(cT[:, P:P + TAILS].rearrange("p (g c) -> p g c", g=G1),
                              src[:, P:C].unsqueeze(1).broadcast_to([P, G1, CT])).then_inc(s["ctx1_ready"], 1)

            def spread(z, h):
                pool.wait_ge(s["v1_dve"], 2 * z + 2)
                g.tensor_tensor(vt[0:TAILS, h, :], vt[0:TAILS, h, :], tails[0:TAILS, 0, :],
                                ALU.mult).then_inc(s["v1_pool"], 1)
                pool.wait_ge(s["k1_slots"], z + 1)
                if not (isinstance(z, int) and z < GH):
                    pool.wait_ge(s["s1"], 5 * (z - GH) + 5)
                g.tensor_tensor(k_diag[:, h, :, :], k_slots.unsqueeze(1).broadcast_to([P, G1, C]),
                                group_of_row.unsqueeze(2).broadcast_to([P, G1, C]), ALU.mult).then_inc(s["k1_diag"], 1)
                g.tensor_tensor(k_tails[:, h, :].rearrange("p (g c) -> p g c", g=G1),
                                k_slots[:, P:C].unsqueeze(1).broadcast_to([P, G1, CT]),
                                group_of_row.unsqueeze(2).broadcast_to([P, G1, CT]), ALU.mult).then_inc(s["k1_diag"], 1)

            pool.wait_ge(s["x2_done"], B)
            pool.wait_ge(s["second_loaded"], 16 * 5)
            context1(0)
            for z in range(GH):
                spread(z, z)
            with pool.Fori(1, B) as b:
                context1(b)
                for h in range(GH):
                    spread(b * GH + h, h)

            def split(par):
                g.tensor_copy(we1_split[:, par, 0, :, :], we1[:, par, :, :]).then_inc(s["w_split"], 2)

            def split_low(e, par):
                pool.wait_ge(s["w_split"], 4 * e + 2)
                g.tensor_tensor(we1_split[:, par, 1, :, :], we1[:, par, :, :], we1_split[:, par, 0, :, :].bitcast(F32),
                                ALU.subtract).then_inc(s["w_split"], 2)

            for e, name in enumerate(["expert_even", "expert_odd"]):
                pool.wait_ge(s[name], 80)
                split(e)
                split_low(e, e)
            with pool.Fori(1, E // 2) as k:
                for par, name in enumerate(["expert_even", "expert_odd"]):
                    pool.wait_ge(s[name], k * 80 + 80)
                    pool.wait_ge(s["v_done"], k * (2 * NF * B) - (1 - par) * NF * B)
                    split(par)
                    split_low(k * 2 + par, par)


_INS = ["x", "ctx_1024", "mask_Bx1x1xS2_ik0", "L0_xattn_ln1_w", "L0_xattn_ln1_b", "L0_xattn_ln2_w", "L0_xattn_ln2_b",
        "L0_xattn_Wq", "L0_xattn_Wkv", "L0_xattn_Wo", "L0_ffn_Wr", "L0_ffn_br", "L0_ffn_Wd", "L0_ffn_bd", "L0_ffn_Wu",
        "L0_ffn_bu", "L1_xattn_Wo", "L1_xattn_bo", "L1_ffn_router_w", "L1_ffn_w1", "L1_ffn_v1", "L1_ffn_w2", "L1_ffn_bias"]


def in_slots(w):
    v = w.reshape(len(w), G1, GH, DH1).transpose(0, 2, 1, 3)[:, :, :, None, :]
    return np.concatenate([np.zeros_like(v), v, v, v], 3).reshape(len(w), GH, P)


def by_head(w):
    v = w.reshape(len(w), G1, GH, DH1)
    r = np.zeros((len(w), GH) + v.shape[1:], w.dtype)
    for h in range(GH):
        r[:, h, :, h, :] = v[:, :, h, :]
    return r.reshape(len(w), GH, P)


def kernel(**inputs):
    import concourse.bacc as _bacc
    from concourse.bass_utils import run_bass_kernel_spmd as _run

    nc = _bacc.Bacc("TRN2", target_bir_lowering=False, num_devices=1)
    arrays = {f"in_{n}_dram": np.ascontiguousarray(inputs[n]) for n in _INS}
    arrays["in_shape_consts_dram"] = constants()
    arrays["in_tail_consts_dram"] = tail_constants()
    wq, wk, wv, bq, bk, bv = (np.asarray(inputs["L1_xattn_" + n]) for n in ("Wq", "Wk", "Wv", "bq", "bk", "bv"))
    arrays["in_Wq_slots_dram"], arrays["in_Wk_slots_dram"] = in_slots(wq), in_slots(wk)
    arrays["in_b_slots_dram"] = np.ascontiguousarray(in_slots(np.stack([bq, bk])).transpose(2, 0, 1))
    arrays["in_Wv_heads_dram"] = by_head(wv)
    arrays["in_bv_heads_dram"] = by_head(bv[None]).reshape(-1)
    arrays["in_mask_by_key_dram"] = np.ascontiguousarray(np.asarray(inputs["mask_Bx1x1xS2_ik0"]).reshape(B, C).T)
    args = {n[3:-5]: nc.dram_tensor(n, v.shape, mybir.dt.from_np(v.dtype), kind="ExternalInput").ap()
            for n, v in arrays.items()}
    out = nc.dram_tensor("out_0_dram", (B, S, D), F32, kind="ExternalOutput").ap()
    build(nc, args, out)
    r = _run(nc, [arrays], core_ids=[0])
    return r.results[0]["out_0_dram"]
```

```python
from contextlib import ExitStack

import numpy as np

import concourse.bass as bass
from concourse import mybir

F32 = mybir.dt.float32
F32R = mybir.dt.float32r
BF16 = mybir.dt.bfloat16
I32 = mybir.dt.int32
ALU = mybir.AluOpType
ACT = mybir.ActivationFunctionType
AX = mybir.AxisListType

P = 128
B, S, D = 4, 512, 128
C = 154
CT = C - P
TOK = B * S
NT = TOK // P
QT = S // P
H0, DH0 = 16, 64
PAIRS = H0 // 2
KV0 = C + S
NK = -(-KV0 // P)
KTAIL = KV0 - (NK - 1) * P
KC = 334
E = 8
R = 16
F = 352
H1, DH1 = 16, 8
G1 = 4
F_TILES = [(j * P, min(P, F - j * P)) for j in range(-(-F // P))]
NF = len(F_TILES)
EPS = 1e-5
NEG = -1.0e9
UNITS = 2 * B
N_FIRST = 5
N_PARAMS = 12
GH = 4
UNITS1 = B * GH
TAILS = G1 * CT


def constants():
    p = np.arange(P)
    ident = np.eye(P, dtype=np.float32)
    dim_in_group = np.broadcast_to((np.arange(32)[None, :] // DH1 == np.arange(4)[:, None]).reshape(1, 128), (P, 128))
    expert_less_8 = np.broadcast_to(np.arange(E)[None, :] - float(E), (P, E))
    expert_of_row = np.zeros((P, P), np.float32)
    expert_of_row[:E] = np.arange(P)[None, :] // R == np.arange(E)[:, None]
    group_of_row = p[:, None] // 32 == np.arange(G1)[None, :]
    slot = p % 32 // DH1
    low_slots = -np.stack([slot == 3, slot == 2], 1).astype(np.float32)
    fixed_rows = np.stack([p % 32 == 1, p % 32 == 0], 1)
    neg_place = np.zeros((P, P), np.float32)
    neg_place[0] = p % 32 == 1
    return np.concatenate([ident, dim_in_group, expert_less_8, expert_of_row, group_of_row, low_slots, fixed_rows,
                           neg_place], 1).astype(np.float32)


def tail_constants():
    p = np.arange(P)
    own = (p[:, None] // CT == p[None, :] // 32) & (p[:, None] < TAILS)
    head = p[None, :] % 32 // DH1 == np.arange(GH)[:, None]
    return np.concatenate([own[:, None, :], own[:, None, :] & head[None]], 1).reshape(P, -1).astype(np.float32)


C_IDENT, C_DIM, C_EXP, C_SEL, C_GROUP = 0, P, 2 * P, 2 * P + E, 3 * P + E
C_LOW, C_FIXED, C_PLACE = C_GROUP + G1, C_GROUP + G1 + 2, C_GROUP + G1 + 4
C_ALL = C_PLACE + P


def build(nc, a, out):
    with ExitStack() as ctx:
        def sb(name, shape, dt=F32):
            return ctx.enter_context(nc.sbuf_tensor(name, shape, dt))

        def sem(name):
            return ctx.enter_context(nc.semaphore(name))

        ps = ctx.enter_context(nc.psum_tensor("ps", [P, 8, 512], F32))

        consts = sb("consts", [P, C_ALL])
        ident = consts[:, C_IDENT:C_IDENT + P]
        dim_in_group = consts[:, C_DIM:C_DIM + P].rearrange("p (h d) -> p h d", h=4)
        expert_less_8 = consts[:, C_EXP:C_EXP + E]
        expert_of_row = consts[0:E, C_SEL:C_SEL + P]
        group_of_row = consts[:, C_GROUP:C_GROUP + G1]
        low_slots = consts[:, C_LOW:C_LOW + 2]
        fixed_rows = consts[:, C_FIXED:C_FIXED + 2]
        identb = sb("identb", [P, P], BF16)
        ones = sb("ones", [P, DH0])
        neg_place = sb("neg_place", [1, P], BF16)
        x = sb("x", [P, NT, D])
        stats = sb("stats", [P, NT, 6])
        mv = sb("mv", [P, NT, 2])
        sd = sb("sd", [P, NT])
        rstd = sb("rstd", [P, NT])
        ctxT = sb("ctxT", [P, B, C])
        kvT = sb("kvT", [P, B, KV0])
        cols = sb("cols", [P, 5])
        rows = sb("rows", [P, 2, D])
        wd = sb("wd", [P, E, R])
        wu = sb("wu", [P, D])
        wr0 = sb("wr0", [P, E])
        wr1 = sb("wr1", [P, E])
        br = sb("br", [P, E])
        bu = sb("bu", [E, D])
        wo1 = sb("wo1", [P, D])
        wo0 = sb("wo0", [P, PAIRS, D])
        big = sb("big", [P, PAIRS, TOK])

        wqkv = sb("wqkv", [P, 2, 3, P])
        k_a = sb("k_a", [P, 2, 2, KV0], F32R)
        k_b = sb("k_b", [DH0 + 1, 2, 2, KV0], F32R)
        q_a = sb("q_a", [P, 2, 2, S], F32R)
        q_b = sb("q_b", [DH0 + 1, 2, 2, S], F32R)
        v0 = sb("v0", [P, 2, NK, P])
        prob = sb("prob", [P, 2, NK, S])
        psums = sb("psums", [P, 2, S])
        nmax = sb("nmax", [P, 2, QT], BF16)
        rden = sb("rden", [P, S])

        lg = sb("lg", [P, NT, E])
        gate = sb("gate", [P, NT, E])
        g2 = sb("g2", [P, NT, E])
        eq = sb("eq", [P, NT, E])
        hot = sb("hot", [P, NT, E])
        wgt = sb("wgt", [P, NT, E])
        red = sb("red", [P, NT])
        wsum = sb("wsum", [P, NT])

        flat_big = big[:].rearrange("p a t -> p (a t)")
        flat_prob = prob[:].rearrange("p h k q -> p (h k q)")
        used = {"big": 0, "prob": 0}

        def carve(*shape, of="big"):
            flat, n = {"big": flat_big, "prob": flat_prob}[of], int(np.prod(shape))
            v = flat[:, used[of]:used[of] + n]
            used[of] += n
            names = "abcd"[:len(shape)]
            if len(shape) == 1:
                return v
            return v.rearrange(f"p ({' '.join(names)}) -> p {' '.join(names)}", **dict(zip(names, shape)))

        probm = carve(2, G1, S)
        probt = carve(2, S)
        vm = carve(GH, D)
        vt = carve(GH, D)
        q_full = carve(S)
        q_high = carve(S)
        k_full = carve(C)
        k_high = carve(C)
        k_slots = carve(C)
        cT = carve(P + TAILS)
        o_raw = carve(S)
        oT = carve(S)
        q_slots = q_a[:].rearrange("p s h q -> p (s h) q")
        k_diag = k_a[:].rearrange("p s h k -> p (s h k)")[:, 0:GH * G1 * C].rearrange(
            "p (h g c) -> p h g c", h=GH, g=G1)
        flat_kvT = kvT[:].rearrange("p b k -> p (b k)")
        wq1 = flat_kvT[:, 0:4 * D].rearrange("p (h m) -> p h m", h=GH)
        wk1 = flat_kvT[:, 4 * D:8 * D].rearrange("p (h m) -> p h m", h=GH)
        wv1h = flat_kvT[:, 8 * D:12 * D].rearrange("p (h m) -> p h m", h=GH)
        bv1 = flat_kvT[:, 12 * D:16 * D].rearrange("p (h m) -> p h m", h=GH)
        tails = psums[:].rearrange("p h q -> p (h q)")[:, 0:(GH + 1) * D].rearrange("p (h m) -> p h m", h=GH + 1)
        k_tails = sb("k_tails", [P, GH, TAILS], F32R)
        b_slots = sb("b_slots", [P, 2, GH])
        nmax1 = sb("nmax1", [P, QT, P], BF16)
        mask_i = sb("mask_i", [P, B], I32)
        mask_t = sb("mask_t", [P, B], I32)
        we1 = carve(2, 2, F)
        we1_split = sb("we1_split", [P, 2, 2, 2, F], F32R)
        xnT_low = k_a[:].rearrange("p s h k -> p (s h k)")[:, 0:TOK]
        xnT_high = q_a[:].rearrange("p s h q -> p (s h q)")
        we2 = carve(2, NF, D)
        wT = flat_big[0:E, 0:TOK]
        xn = carve(NT, D, of="prob")
        xnT = carve(TOK, of="prob")
        acc = carve(NT, D, of="prob")
        hidden = flat_big[:, TOK:2 * TOK]
        used["big"] = 0
        gg = carve(NF, S)
        hid = carve(2, NF, S)
        used["prob"] = NT * D
        ctx_in = carve(B, 2, D, of="prob")
        ctxn = carve(B, 2, D, of="prob")
        mask_r = carve(B, C, of="prob").bitcast(I32)
        valid_r = carve(B, C, of="prob")
        valid_m = sb("valid_m", [P, 2, B])
        any_valid = sb("any_valid", [P, B])
        mcol = sb("mcol", [P, B, 4])
        mcol_b = sb("mcol_b", [P, 4])
        neg_row = sb("neg_row", [1, B, C], BF16)

        wcol = sb("wcol", [P, 2, NT])

        names = """x_first x_rest ctx_loaded first_params params_loaded mask_loaded pair_even pair_odd
            expert_even expert_odd dve_step pool_step var_ready sd_ready lat_ready
            tr_done kvT_done ctxT_done q_proj k_proj v_proj q_hi q_lo q_dup k_hi k_lo k_dup v_dve v_act
            max_scores max_done row_proj row_copied scores scores_taken sum_step pv_done den_done
            den_read recip head_done wo_done x1_done ln_ready xt_done xnT_done logits_done logit_ready gate_exp hT_done h_gelu
            wT_tr wT_done wb_done hw_done up_done x2_done second_loaded b_slots_done ctx1_ready
            q1_proj q1_split q1_slots kv1_proj k1_split k1_slots k1_diag v1_dve v1_pool
            max1 max1_taken rows1 q1_max s1 s1_taken pv1 o1_copied recip1 o1_done wo1 x3_done mc_done
            xnT_low_done w_split bo_added
            r1_done g_done v_done gelu_done h_done down_done acc_done w_done
            out_stored""".split()
        s = {n: sem(n) for n in names}

        dve_n = [0]

        from_one = {"act": ["gelu_done", "den_read"],
                    "dve": ["head_done", "x3_done", "o1_done", "h_done", "acc_done"]}

        def link(eng, ins):
            dve_n[0] += 1
            ins.then_inc(s["dve_step"], 1)
            eng.wait_ge(s["dve_step"], dve_n[0])

        block = ctx.enter_context(nc.Block())

        WO_BANKS = [7, 0, 2, 3]

        @block.sync
        def _(sp):
            m = a["mask_Bx1x1xS2_ik0"].rearrange("b o u c -> (b o u) c")
            xs = a["x"].rearrange("b (t p) d -> p (b t) d", p=P)
            c = a["ctx_1024"]
            sp.dma_start(x[:, 0:QT, :], xs[:, 0:QT, :]).then_inc(s["x_first"], 16)
            sp.dma_start(ctx_in[:, :, 0, :], c[:, 0:P, :].rearrange("b p d -> p b d")).then_inc(s["ctx_loaded"], 16)
            sp.dma_start(ctx_in[0:CT, :, 1, :], c[:, P:C, :].rearrange("b p d -> p b d")).then_inc(s["ctx_loaded"], 16)
            sp.dma_start(mask_r, m.rearrange("b c -> (b c)").partition_broadcast(P)
                         .rearrange("p (b c) -> p b c", b=B)).then_inc(s["mask_loaded"], 16)
            sp.dma_start(mask_i[:], a["mask_by_key"][0:P, :]).then_inc(s["mask_loaded"], 16)
            sp.wait_ge(s["pool_step"], 1)
            for g in range(G1):
                sp.dma_start(mask_t[CT * g:CT * (g + 1), :], a["mask_by_key"][P:C, :]).then_inc(s["mask_loaded"], 16)
            params = [(consts[:], a["shape_consts"])]
            for n, name in enumerate(["L0_xattn_ln1_w", "L0_xattn_ln1_b", "L0_xattn_ln2_w", "L0_xattn_ln2_b",
                                      "L0_ffn_bd"]):
                src = a[name] if len(a[name].shape) == 1 else a[name].rearrange("e r -> (e r)")
                params.append((cols[:, n:n + 1], src.rearrange("(p o) -> p o", o=1)))
            for n, name in enumerate(["L1_xattn_bo", "L1_ffn_bias"]):
                params.append((rows[:, n, :], a[name].partition_broadcast(P)))
            params.append((wd[:], a["L0_ffn_Wd"].rearrange("e d r -> d e r")))
            params.append((wu[:], a["L0_ffn_Wu"].rearrange("e r d -> (e r) d")))
            params.append((wr0[:], a["L0_ffn_Wr"]))
            params.append((wr1[:], a["L1_ffn_router_w"]))
            params.append((br[:], a["L0_ffn_br"].partition_broadcast(P)))
            params.append((bu[:], a["L0_ffn_bu"]))
            params.append((wo1[:], a["L1_xattn_Wo"]))
            params.append((b_slots[:], a["b_slots"]))
            params.append((wo0[:], a["L0_xattn_Wo"].rearrange("(j p) d -> p j d", p=P)))
            for dst, src in params[:N_FIRST]:
                sp.dma_start(dst, src).then_inc(s["first_params"], 16)
            assert len(params) == N_FIRST + N_PARAMS
            wq, wkv = a["L0_xattn_Wq"], a["L0_xattn_Wkv"]

            def load_pair(pair, par, name):
                sp.dma_start(wqkv[:, par, 0, :], wq[:, bass.ds(pair * P, P)]).then_inc(s[name], 16)
                sp.dma_start(wqkv[:, par, 1, :], wkv[:, bass.ds(pair * P, P)]).then_inc(s[name], 16)
                sp.dma_start(wqkv[:, par, 2, :], wkv[:, bass.ds(pair * P + H0 * DH0, P)]).then_inc(s[name], 16)

            load_pair(0, 0, "pair_even")
            sp.dma_start(x[:, QT:NT, :], xs[:, QT:NT, :]).then_inc(s["x_rest"], 16)
            load_pair(1, 1, "pair_odd")
            for dst, src in params[N_FIRST:]:
                sp.dma_start(dst, src).then_inc(s["params_loaded"], 16)

            def dups(w, st):
                for h in range(2):
                    sp.wait_ge(s["q_hi"], 2 * w + h + 1)
                    sp.dma_start(q_a[DH0:P, st, h, :].bitcast(F32),
                                 q_a[0:DH0, st, h, :].bitcast(F32)).then_inc(s["q_dup"], 16)
                for h in range(2):
                    sp.wait_ge(s["k_hi"], 4 * w + 3 + h)
                    sp.dma_start(k_b[0:DH0, st, h, :].bitcast(F32),
                                 k_a[0:DH0, st, h, :].bitcast(F32)).then_inc(s["k_dup"], 16)

            def turn(u0, last_turn):
                for i in range(UNITS - last_turn):
                    w = u0 + i + 1
                    dups(w, (i + 1) % 2)
                    if i % B == B - 2 and not last_turn:
                        sp.wait_ge(s["v_proj"], 2 * w + 2)
                        pair = it * 2 + 2 + i // B
                        load_pair(pair, i // B, ["pair_even", "pair_odd"][i // B])

            dups(0, 0)
            with sp.Fori(0, PAIRS // 2 - 1) as it:
                turn(it * UNITS, False)
            turn(PAIRS * B - UNITS, True)

            w1, v1, w2 = a["L1_ffn_w1"], a["L1_ffn_v1"], a["L1_ffn_w2"]

            def load_expert(e, par, name):
                sp.dma_start(we1[:, par, 0, :], w1[bass.ds(e, 1), :, :].rearrange("e d f -> d (e f)")).then_inc(s[name], 16)
                sp.dma_start(we1[:, par, 1, :], v1[bass.ds(e, 1), :, :].rearrange("e d f -> d (e f)")).then_inc(s[name], 16)
                for j, (f0, fn) in enumerate(F_TILES):
                    sp.dma_start(we2[0:fn, par, j, :],
                                 w2[bass.ds(e, 1), f0:f0 + fn, :].rearrange("e f d -> f (e d)")).then_inc(s[name], 16)

            sp.wait_ge(s["wo_done"], B)
            for dst, src in ((wq1, a["Wq_slots"]), (wk1, a["Wk_slots"]), (wv1h, a["Wv_heads"]),
                             (tails, a["tail_consts"].rearrange("p (h m) -> p h m", h=GH + 1)),
                             (bv1, a["bv_heads"].partition_broadcast(P).rearrange("p (h m) -> p h m", h=GH))):
                sp.dma_start(dst, src).then_inc(s["second_loaded"], 16)
            load_expert(0, 0, "expert_even")
            load_expert(1, 1, "expert_odd")
            with sp.Fori(1, E // 2) as it:
                sp.wait_ge(s["down_done"], it * (2 * B) - B)
                load_expert(it * 2, 0, "expert_even")
                sp.wait_ge(s["down_done"], it * (2 * B))
                load_expert(it * 2 + 1, 1, "expert_odd")

            o = out.rearrange("b (t p) d -> p (b t) d", p=P)
            for c in range(B):
                sp.wait_ge(s["acc_done"], 1 + (E - 1) * B + c + 1)
                sp.dma_start(o[:, QT * c:QT * (c + 1), :], acc[:, QT * c:QT * (c + 1), :]).then_inc(s["out_stored"], 16)
            sp.wait_ge(s["out_stored"], 16 * B)

        @block.tensor
        def _(pe):
            mm = nc.tensor.matmul
            def transposes(b):
                pe.wait_ge(s["lat_ready"], b + 1)
                if b > 0:
                    pe.wait_ge(s["kvT_done"], b)
                for t in range(QT):
                    nc.tensor.transpose(ps[:, 5, t * P:(t + 1) * P], xn[:, QT * b + t, :], ident)
                for k, src in enumerate((ctxn, ctx_in)):
                    nc.tensor.transpose(ps[:, 6, 160 * k:160 * k + P], src[:, b, 0, :], ident)
                    last = nc.tensor.transpose(ps[:, 6, 160 * k + P:160 * k + C], src[0:CT, b, 1, :], ident[0:CT, 0:CT])
                last.then_inc(s["tr_done"], 1)

            SC, PV, PR = 2, 5, 7

            def q_proj(w, b, wp):
                if not (isinstance(w, int) and w == 0):
                    pe.wait_ge(s["v_act"], 2 * w)
                mm(ps[:, PR, :], wqkv[:, wp, 0, :], kvT[:, b, C:KV0], start=True, stop=True).then_inc(s["q_proj"], 1)

            def k_proj(w, b, wp, c):
                if c == 0:
                    pe.wait_ge(s["q_hi"], 2 * w + 2)
                    pe.wait_ge(s["q_lo"], 2 * w + 2)
                else:
                    pe.wait_ge(s["k_hi"], 4 * w + 2)
                    pe.wait_ge(s["k_lo"], 4 * w + 2)
                n = KV0 // 2
                mm(ps[:, PR, 0:n], wqkv[:, wp, 1, :], kvT[:, b, c * n:(c + 1) * n],
                   start=True, stop=True).then_inc(s["k_proj"], 1)

            def v_proj(w, b, wp, c):
                if c == 0:
                    pe.wait_ge(s["k_hi"], 4 * w + 4)
                    pe.wait_ge(s["k_lo"], 4 * w + 4)
                else:
                    pe.wait_ge(s["v_dve"], w + 1)
                for t in (range(4) if c == 0 else range(4, NK)):
                    n = min(P, KV0 - t * P)
                    last = mm(ps[0:n, PR, (t % 4) * P:(t % 4 + 1) * P], kvT[:, b, t * P:t * P + n],
                              wqkv[:, wp, 2, :], start=True, stop=True)
                last.then_inc(s["v_proj"], 1)

            def max_scores(w, st, j):
                h, t = divmod(j, QT)
                if j == 0:
                    pe.wait_ge(s["q_hi"], 2 * w + 2)
                    pe.wait_ge(s["k_hi"], 4 * w + 4)
                    if not (isinstance(w, int) and w == 0):
                        pe.wait_ge(s["den_read"], 1 + w - 1)
                first = isinstance(w, int) and w == 0
                bank = 2 * (j % 2) if first else 0
                if not first:
                    pe.wait_ge(s["max_done"], 8 * w + j)
                elif j > 1:
                    pe.wait_ge(s["max_done"], j - 1)
                for c in range(2):
                    k0 = c * (KV0 - KC)
                    last = mm(ps[:, bank + c, 0:KC], q_a[0:DH0, st, h, t * P:(t + 1) * P], k_a[0:DH0, st, h, k0:k0 + KC],
                              start=True, stop=True)
                last.then_inc(s["max_scores"], 1)

            def max_rows(w):
                pe.wait_ge(s["max_done"], 8 * w + 8)
                for t in range(QT):
                    for h in range(2):
                        last = mm(ps[32 * h:32 * h + 1, 0, t * P:(t + 1) * P], nmax[:, h, t:t + 1], identb[:],
                                  start=True, stop=True)
                last.then_inc(s["row_proj"], 1)

            def scores(u, st, kt, heads=(0, 1)):
                n = min(P, KV0 - kt * P)
                for h in heads:
                    j = 2 * kt + h
                    if kt == 0 and h == 0:
                        pe.wait_ge(s["row_copied"], 2 * u + 2)
                        pe.wait_ge(s["q_lo"], 2 * u + 2)
                        pe.wait_ge(s["q_dup"], 32 * u + 32)
                        pe.wait_ge(s["k_lo"], 4 * u + 4)
                        pe.wait_ge(s["k_dup"], 32 * u + 32)
                    pe.wait_ge(s["scores_taken"], 2 * NK * u + j + 1)
                    o = ps[0:n, SC + j % 3, :]
                    mm(o, k_a[:, st, h, kt * P:kt * P + n], q_a[:, st, h, :], start=True, stop=False)
                    mm(o, k_b[:, st, h, kt * P:kt * P + n], q_b[:, st, h, :],
                       start=False, stop=True).then_inc(s["scores"], 1)

            def pv(u, st, kt):
                n = min(P, KV0 - kt * P)
                if kt == 0:
                    pe.wait_ge(s["v_dve"], u + 1)
                    pe.wait_ge(s["v_act"], 2 * u + 2)
                pe.wait_ge(s["scores_taken"], 3 + 2 * NK * u + 2 * kt + 2)
                for h in range(2):
                    last = mm(ps[DH0 * h:DH0 * h + DH0, PV + st, :], v0[0:n, st, kt, DH0 * h:DH0 * h + DH0],
                              prob[0:n, h, kt, :], start=(kt == 0), stop=(kt == NK - 1))
                if kt == NK - 1:
                    last.then_inc(s["pv_done"], 1)

            def den(u, more):
                if more == 0:
                    pe.wait_ge(s["den_read"], 1 + u)
                pe.wait_ge(s["sum_step"], 2 * (NK - 1) * (u + 1))
                for h in range(2):
                    last = mm(ps[DH0 * h:DH0 * h + DH0, 1, :], ones[:], psums[:, h, :], start=True, stop=True)
                last.then_inc(s["den_done"], 1)

            def wo_proj(c):
                pe.wait_ge(s["head_done"], 1 + PAIRS * B - B + c + 1)
                for t in range(QT * c, QT * c + QT):
                    for j in range(PAIRS):
                        last = mm(ps[:, WO_BANKS[c], (t % QT) * P:(t % QT + 1) * P], big[:, j, t * P:(t + 1) * P],
                                  wo0[:, j, :], start=(j == 0), stop=(j == PAIRS - 1))
                last.then_inc(s["wo_done"], 1)

            def unit(u, i, more):
                st, nst, b1, wp1 = i % 2, (i + 1) % 2, (i + 1) % B, ((i + 1) // B) % 2
                b2, wp2 = (i + 2) % B, ((i + 2) // B) % 2
                w, z = u + 1, u + 2
                steps = max_scores if more > 0 else (lambda *a: None)
                scores(u, st, 1)
                if more > 0:
                    k_proj(w, b1, wp1, 1)
                pv(u, st, 0)
                steps(w, nst, 0)
                scores(u, st, 2, [0])
                if more > 0:
                    v_proj(w, b1, wp1, 0)
                steps(w, nst, 1)
                scores(u, st, 2, [1])
                pv(u, st, 1)
                steps(w, nst, 2)
                scores(u, st, 3)
                if more > 0:
                    v_proj(w, b1, wp1, 1)
                steps(w, nst, 3)
                pv(u, st, 2)
                scores(u, st, 4, [0])
                steps(w, nst, 4)
                scores(u, st, 4, [1])
                pv(u, st, 3)
                steps(w, nst, 5)
                scores(u, st, 5, [0])
                pv(u, st, 4)
                steps(w, nst, 6)
                scores(u, st, 5, [1])
                if more > 1:
                    q_proj(z, b2, wp2)
                steps(w, nst, 7)
                pv(u, st, 5)
                if more > 0:
                    max_rows(w)
                else:
                    pe.wait_ge(s["params_loaded"], 16 * N_PARAMS)
                    wo_proj(0)
                    wo_proj(1)
                den(u, more)
                if more > 1:
                    k_proj(z, b2, wp2, 0)
                if more > 0:
                    scores(w, nst, 0)

            def turn(u0, last_turn):
                for i in range(UNITS):
                    if i == UNITS - 2 and not last_turn:
                        pe.wait_ge(s["pair_even"], pair_count(u0) + 48)
                    if i == B - 2:
                        pe.wait_ge(s["pair_odd"], pair_count(u0))
                    unit(u0 + i, i, min(2, UNITS - 1 - i) if last_turn else 2)

            def pair_count(u0):
                return u0 * (48 // UNITS) + 48

            pe.wait_ge(s["first_params"], 16 * N_FIRST)
            transposes(0)
            pe.wait_ge(s["pair_even"], 48)
            pe.wait_ge(s["kvT_done"], 1)
            q_proj(0, 0, 0)
            k_proj(0, 0, 0, 0)
            k_proj(0, 0, 0, 1)
            v_proj(0, 0, 0, 0)
            transposes(1)
            v_proj(0, 0, 0, 1)
            for j in range(8):
                max_scores(0, 0, j)
                if j == 4:
                    transposes(2)
            pe.wait_ge(s["q_dup"], 32)
            pe.wait_ge(s["k_dup"], 32)
            q_proj(1, 1, 0)
            max_rows(0)
            k_proj(1, 1, 0, 0)
            transposes(3)
            pe.wait_ge(s["pool_step"], 3)
            scores(0, 0, 0)
            pe.wait_ge(s["kvT_done"], B)
            with pe.Fori(0, PAIRS * B - UNITS, UNITS) as u0:
                turn(u0, False)
            turn(PAIRS * B - UNITS, True)

            def transpose_xn(stage, c):
                pe.wait_ge(s["ln_ready"], B * stage + c + 1)
                for t in range(QT):
                    last = nc.tensor.transpose(ps[:, 4 + c, t * P:(t + 1) * P], xn[:, QT * c + t, :], ident)
                last.then_inc(s["xt_done"], 1)

            def router(c, w, copies):
                pe.wait_ge(s["xnT_done"], copies)
                for t in range(QT * c, QT * c + QT):
                    last = mm(ps[:, 1, t * E:(t + 1) * E], xnT[:, t * P:(t + 1) * P], w[:], start=True, stop=True)
                if c == B - 1:
                    last.then_inc(s["logits_done"], 1)

            wo_proj(2)
            transpose_xn(0, 0)
            pe.wait_ge(s["den_read"], 1 + PAIRS * B)
            router(0, wr0, 1)
            transpose_xn(0, 1)
            wo_proj(3)
            router(1, wr0, 2)
            transpose_xn(0, 2)
            router(2, wr0, 3)
            transpose_xn(0, 3)
            router(3, wr0, 4)
            for c in range(B):
                mm(ps[:, 4 + c, :], wd[:].rearrange("p e r -> p (e r)"), xnT[:, c * S:(c + 1) * S],
                   start=True, stop=True).then_inc(s["hT_done"], 1)
            pe.wait_ge(s["w_done"], 1)
            for t in range(NT):
                last = nc.tensor.transpose(ps[0:E, t // QT, (t % QT) * P:(t % QT + 1) * P], wgt[:, t, :], ident)
                if t % QT == QT - 1:
                    last.then_inc(s["wT_tr"], 1)
            for c in range(B):
                pe.wait_ge(s["wT_done"], c + 1)
                mm(ps[:, c, :], expert_of_row, wT[:, c * S:(c + 1) * S], start=True, stop=True).then_inc(s["wb_done"], 1)
            def adapters_up(c):
                pe.wait_ge(s["hw_done"], c + 1)
                pe.wait_ge(s["h_gelu"], B)
                for t in range(QT * c, QT * c + QT):
                    o = ps[:, 4 + c, (t % QT) * P:(t % QT + 1) * P]
                    mm(o, hidden[:, t * P:(t + 1) * P], wu[:], start=True, stop=False)
                    last = mm(o, wT[:, t * P:(t + 1) * P], bu[:], start=False, stop=True)
                last.then_inc(s["up_done"], 1)

            for c in range(3):
                adapters_up(c)
            transpose_xn(1, 0)
            adapters_up(3)
            def q1_proj(z, hz, bz):
                if not (isinstance(z, int) and z < 2):
                    pe.wait_ge(s["q1_max"], z - 1)
                mm(ps[:, 4, :], wq1[:, hz, :], xnT[:, bass.ds(bz * S, S)],
                   start=True, stop=True).then_inc(s["q1_proj"], 1)

            def kv1_proj(z, hz, bz):
                if not (isinstance(z, int) and z == 0):
                    pe.wait_ge(s["k1_split"], 2 * z)
                    pe.wait_ge(s["v1_dve"], 2 * z)
                pe.wait_ge(s["ctx1_ready"], bz + 1)
                mm(ps[:, 5, 0:C], wk1[:, hz, :], ctxT[:, bass.ds(bz, 1), :].rearrange("p b c -> p (b c)"),
                   start=True, stop=False)
                mm(ps[:, 5, 0:C], neg_place[:], neg_row[:, bass.ds(bz, 1), :].rearrange("p b c -> p (b c)"),
                   start=False, stop=True)
                mm(ps[:, 5, 160:160 + D], cT[:, 0:P], wv1h[:, hz, :], start=True, stop=True)
                mm(ps[0:TAILS, 5, 160 + D:160 + 2 * D], cT[:, P:P + TAILS], wv1h[:, hz, :],
                   start=True, stop=True).then_inc(s["kv1_proj"], 1)

            def max1(w, hw, t, bw=None):
                if t == 0:
                    pe.wait_ge(s["q1_slots"], w + 1)
                    pe.wait_ge(s["k1_diag"], 2 * w + 2)
                    if bw is not None:
                        pe.wait_ge(s["x3_done"], 1 + bw)
                first = isinstance(w, int) and w == 0
                bank = 2 * (t % 2) if first else 0
                if not first:
                    pe.wait_ge(s["max1_taken"], QT * w + t)
                elif t > 1:
                    pe.wait_ge(s["max1_taken"], t - 1)
                for c in range(2):
                    last = mm(ps[:, bank + c, 0:2 * C], q_slots[:, hw, t * P:(t + 1) * P], k_diag[:, hw, 2 * c:2 * c + 2, :],
                              start=True, stop=True)
                last.then_inc(s["max1"], 1)

            def rows1(w, splits):
                pe.wait_ge(s["max1_taken"], QT * w + QT)
                pe.wait_ge(s["q1_split"], 2 * splits)
                for t in range(QT):
                    last = mm(ps[:, 4, t * P:(t + 1) * P], nmax1[:, t, :], identb[:], start=True, stop=True)
                last.then_inc(s["rows1"], 1)

            def scores1(u, h, j):
                if j == 0:
                    pe.wait_ge(s["q1_max"], u + 1)
                pe.wait_ge(s["s1_taken"], 5 * u + j + 1)
                n = (5 * h + j) % 2
                k = k_diag[:, h, j, 0:P] if j < G1 else k_tails[:, h, :]
                mm(ps[0:P if j < G1 else TAILS, 2 + n, :], k, q_slots[:, h, :],
                   start=True, stop=True).then_inc(s["s1"], 1)

            def pv1(u, h, bu=None):
                if bu is not None:
                    pe.wait_ge(s["o1_copied"], 2 * bu)
                pe.wait_ge(s["v1_dve"], 2 * u + 2)
                pe.wait_ge(s["s1_taken"], 2 + 5 * u + G1)
                for g in range(G1):
                    mm(ps[32 * g:32 * g + 32, 6, :], vm[:, h, 32 * g:32 * g + 32], probm[:, h % 2, g, :],
                       start=(h == 0), stop=False)

            def den1(h):
                for g in range(G1):
                    mm(ps[32 * g:32 * g + 32, 7, :], dim_in_group[:, h, :], probm[:, h % 2, g, :],
                       start=(h == 0), stop=False)

            def pv1_tail(u, h):
                pe.wait_ge(s["v1_pool"], u + 1)
                pe.wait_ge(s["s1_taken"], 2 + 5 * u + G1 + 1)
                mm(ps[:, 6, :], vt[0:TAILS, h, :], probt[0:TAILS, h % 2, :], start=False, stop=(h == GH - 1))

            def den1_tail(h):
                mm(ps[:, 7, :], tails[0:TAILS, 1 + h, :], probt[0:TAILS, h % 2, :],
                   start=False, stop=(h == GH - 1)).then_inc(s["pv1"], 1)

            def wo1_proj(b):
                pe.wait_ge(s["o1_done"], 1 + b + 1)
                for t in range(QT):
                    last = mm(ps[:, 0, t * P:(t + 1) * P], oT[:, t * P:(t + 1) * P], wo1[:], start=True, stop=True)
                last.then_inc(s["wo1"], 1)

            def unit1(b, i, more):
                u, w, z = GH * b + i, GH * b + i + 1, GH * b + i + 2
                hw, hz, bz = (i + 1) % GH, (i + 2) % GH, b + (i + 2) // GH
                first = isinstance(u, int) and u == 0
                scores1(u, i, 0)
                scores1(u, i, 1)
                if more > 0:
                    max1(w, hw, 0, b if i == 2 and not (isinstance(b, int) and b == 0) else None)
                if more > 1:
                    q1_proj(z, hz, bz)
                scores1(u, i, 2)
                if more > 0:
                    max1(w, hw, 1)
                scores1(u, i, 3)
                if more > 1:
                    kv1_proj(z, hz, bz)
                if more > 0:
                    max1(w, hw, 2)
                scores1(u, i, 4)
                pv1(u, i, b if i == 0 and not first else None)
                if more > 0:
                    max1(w, hw, 3)
                den1(i)
                if i == 1 and not (isinstance(b, int) and b == 0):
                    pe.wait_ge(s["max1_taken"], QT * w + QT)
                    wo1_proj(b - 1)
                pv1_tail(u, i)
                if more > 0:
                    rows1(w, z + 1 if more > 1 else z)
                den1_tail(i)

            pe.wait_ge(s["second_loaded"], 16 * 5)
            transpose_xn(1, 1)
            pe.wait_ge(s["xnT_done"], B + 1)
            q1_proj(0, 0, 0)
            transpose_xn(1, 2)
            pe.wait_ge(s["xnT_done"], B + 2)
            kv1_proj(0, 0, 0)
            transpose_xn(1, 3)
            for t in range(QT):
                max1(0, 0, t)
            pe.wait_ge(s["q1_split"], 2)
            q1_proj(1, 1, 0)
            kv1_proj(1, 1, 0)
            rows1(0, 2)
            pe.wait_ge(s["xnT_done"], 2 * B)
            unit1(0, 0, 2)
            unit1(0, 1, 2)
            with pe.Fori(0, B - 1) as b:
                unit1(b, 2, 2)
                unit1(b, 3, 2)
                unit1(b + 1, 0, 2)
                unit1(b + 1, 1, 2)
            unit1(B - 1, 2, 1)
            unit1(B - 1, 3, 0)

            transpose_xn(2, 0)
            transpose_xn(2, 1)
            pe.wait_ge(s["o1_copied"], 2 * B)
            router(0, wr1, 2 * B + 2)
            router(1, wr1, 2 * B + 4)
            transpose_xn(2, 2)
            wo1_proj(B - 1)
            router(2, wr1, 2 * B + 6)
            transpose_xn(2, 3)
            router(3, wr1, 2 * B + 8)

            def up(m, c, par, j, dist):
                f0, fn = F_TILES[j]
                if not (isinstance(m, int) and m == 0):
                    pe.wait_ge(s["gelu_done"], 1 + NF * m - dist)
                    pe.wait_ge(s["h_done"], 1 + NF * m - dist)
                high, low = xnT_high[:, c * S:(c + 1) * S], xnT_low[:, c * S:(c + 1) * S]
                for k, done in enumerate(["g_done", "v_done"]):
                    o, w = ps[0:fn, NF * k + j, :], we1_split[:, par, :, k, f0:f0 + fn]
                    mm(o, w[:, 0, :], high, start=True, stop=False)
                    mm(o, w[:, 0, :], low, start=False, stop=False)
                    mm(o, w[:, 1, :], high, start=False, stop=True).then_inc(s[done], 1)

            def down(m, i):
                pe.wait_ge(s["h_done"], 1 + NF * m + NF)
                for t in range(QT):
                    for j, (f0, fn) in enumerate(F_TILES):
                        last = mm(ps[:, 6 + i % 2, t * P:(t + 1) * P], hid[0:fn, i % 2, j, t * P:(t + 1) * P],
                                  we2[0:fn, (i // B) % 2, j, :], start=(j == 0), stop=(j == NF - 1))
                last.then_inc(s["down_done"], 1)

            def turn1(m0, last_turn):
                for i in range(UNITS):
                    m, c, par = m0 + i, i % B, i // B
                    up(m, c, par, 1, 0)
                    up(m, c, par, 2, 0)
                    if not (last_turn and i == UNITS - 1):
                        if i == UNITS - 1:
                            pe.wait_ge(s["w_split"], m0 + 12)
                        if i == B - 1:
                            pe.wait_ge(s["w_split"], m0 + 8)
                        up(m + 1, (i + 1) % B, ((i + 1) // B) % 2, 0, NF - 1)
                    down(m, i)

            pe.wait_ge(s["w_split"], 4)
            pe.wait_ge(s["xnT_low_done"], B)
            up(0, 0, 0, 0, 0)
            pe.wait_ge(s["logit_ready"], 2)
            with pe.Fori(0, E * B - UNITS, UNITS) as m0:
                turn1(m0, False)
            turn1(E * B - UNITS, True)

        @block.scalar
        def _(act):
            cp = nc.scalar.copy
            af = nc.scalar.activation
            for n in from_one["act"]:
                act.sem_inc(s[n], 1)

            def roots(n):
                act.wait_ge(s["var_ready"], n + 1)
                af(sd[:], mv[:, :, 1], ACT.Sqrt).then_inc(s["sd_ready"], 1)

            def context(b):
                act.wait_ge(s["tr_done"], b + 1)
                cp(ctxT[:, b, :], ps[:, 6, 160:160 + C]).then_inc(s["ctxT_done"], 1)

            SC, PR = 2, 7
            s_taken = s["scores_taken"]

            def q_hi(w, st):
                act.wait_ge(s["q_proj"], w + 1)
                for h in range(2):
                    cp(q_a[0:DH0, st, h, :], ps[DH0 * h:DH0 * h + DH0, PR, :]).then_inc(s["q_hi"], 1)

            def k_hi(w, st, c):
                n = KV0 // 2
                act.wait_ge(s["k_proj"], 2 * w + c + 1)
                for h in range(2):
                    cp(k_a[0:DH0, st, h, c * n:(c + 1) * n],
                       ps[DH0 * h:DH0 * h + DH0, PR, 0:n]).then_inc(s["k_hi"], 1)

            def v_last(w, st):
                act.wait_ge(s["v_proj"], 2 * w + 2)
                cp(v0[:, st, 4, :], ps[:, PR, 0:P]).then_inc(s["v_act"], 1)
                cp(v0[0:KTAIL, st, 5, :], ps[0:KTAIL, PR, P:2 * P]).then_inc(s["v_act"], 1)

            def max_row(w, st):
                act.wait_ge(s["row_proj"], w + 1)
                for h in range(2):
                    cp(q_b[DH0:DH0 + 1, st, h, :], ps[32 * h:32 * h + 1, 0, :]).then_inc(s["row_copied"], 1)

            def sums_copy(u):
                act.wait_ge(s["den_done"], u + 1)
                act.wait_ge(s["head_done"], 1 + u)
                cp(rden[:], ps[:, 1, :]).then_inc(s["den_read"], 1)

            def exps(u, st, kt, heads=(0, 1)):
                n = min(P, KV0 - kt * P)
                if kt == 0 and not (isinstance(u, int) and u == 0):
                    act.wait_ge(s["sum_step"], 2 * (NK - 1) * (u - 1) + 2)
                for h in heads:
                    j = 2 * kt + h
                    act.wait_ge(s["scores"], 2 * NK * u + j + 1)
                    af(prob[0:n, h, kt, :], ps[0:n, SC + j % 3, :], ACT.Exp,
                       scale=1.0 / DH0 ** 0.5).then_inc(s_taken, 1)

            def unit(u, i, more):
                st, nst, w, z = i % 2, (i + 1) % 2, u + 1, u + 2
                exps(u, st, 1, [0])
                if more > 0:
                    k_hi(w, nst, 1)
                exps(u, st, 1, [1])
                exps(u, st, 2)
                exps(u, st, 3)
                if more > 0:
                    v_last(w, nst)
                exps(u, st, 4)
                exps(u, st, 5)
                if more > 1:
                    q_hi(z, st)
                if more > 0:
                    max_row(w, nst)
                else:
                    roots(2 * B)
                sums_copy(u)
                if more > 1:
                    k_hi(z, st, 0)
                if more > 0:
                    exps(w, nst, 0)

            act.sem_inc(s_taken, 3)
            roots(0)
            roots(1)
            context(0)
            q_hi(0, 0)
            roots(2)
            k_hi(0, 0, 0)
            roots(3)
            k_hi(0, 0, 1)
            context(1)
            v_last(0, 0)
            roots(4)
            roots(5)
            context(2)
            roots(6)
            q_hi(1, 1)
            roots(7)
            max_row(0, 0)
            k_hi(1, 1, 0)
            context(3)
            exps(0, 0, 0)
            with act.Fori(0, PAIRS * B - UNITS, UNITS) as u0:
                for i in range(UNITS):
                    unit(u0 + i, i, 2)
            for i in range(UNITS):
                unit(PAIRS * B - UNITS + i, i, min(2, UNITS - 1 - i))

            def copy_xnT(stage, c):
                act.wait_ge(s["xt_done"], B * stage + c + 1)
                cp(xnT[:, c * S:(c + 1) * S], ps[:, 4 + c, :]).then_inc(s["xnT_done"], 1)

            def gate_exp(stage):
                act.wait_ge(s["logit_ready"], stage + 1)
                af(gate[:], lg[:], ACT.Exp).then_inc(s["gate_exp"], 1)

            act.wait_ge(s["params_loaded"], 16 * N_PARAMS)
            roots(2 * B + 1)
            roots(2 * B + 2)
            copy_xnT(0, 0)
            copy_xnT(0, 1)
            roots(2 * B + 3)
            copy_xnT(0, 2)
            copy_xnT(0, 3)
            gate_exp(0)
            for c in range(B):
                act.wait_ge(s["hT_done"], c + 1)
                af(hidden[:, c * S:(c + 1) * S], ps[:, 4 + c, :], ACT.Gelu_apprx_tanh, bias=cols[:, 4:5]).then_inc(s["h_gelu"], 1)
            for c in range(B):
                act.wait_ge(s["wT_tr"], c + 1)
                cp(wT[:, c * S:(c + 1) * S], ps[0:E, c, :]).then_inc(s["wT_done"], 1)

            roots(3 * B)
            roots(3 * B + 1)
            copy_xnT(1, 0)
            roots(3 * B + 2)
            copy_xnT(1, 1)
            roots(3 * B + 3)
            def q1_split(z, h):
                act.wait_ge(s["q1_proj"], z + 1)
                if not (isinstance(z, int) and z == 0):
                    act.wait_ge(s["q1_slots"], z)
                for o in (q_full, q_high.bitcast(F32R)):
                    af(o, ps[:, 4, :], ACT.Identity, bias=b_slots[:, 0, h:h + 1]).then_inc(s["q1_split"], 1)

            def k1_split(z, h):
                act.wait_ge(s["kv1_proj"], z + 1)
                if not (isinstance(z, int) and z == 0):
                    act.wait_ge(s["k1_slots"], z)
                for o in (k_full, k_high.bitcast(F32R)):
                    af(o, ps[:, 5, 0:C], ACT.Identity, bias=b_slots[:, 1, h:h + 1]).then_inc(s["k1_split"], 1)

            def exps1(u, h, j):
                if j == 0 and not (isinstance(u, int) and u < 2):
                    act.wait_ge(s["pv1"], u - 1)
                act.wait_ge(s["s1"], 5 * u + j + 1)
                n = (5 * h + j) % 2
                if j < G1:
                    af(probm[:, h % 2, j, :], ps[:, 2 + n, :], ACT.Exp, bias=mcol_b[:, 1:2],
                       scale=mcol_b[:, 0:1]).then_inc(s["s1_taken"], 1)
                else:
                    af(probt[0:TAILS, h % 2, :], ps[0:TAILS, 2 + n, :], ACT.Exp, bias=mcol_b[0:TAILS, 3:4],
                       scale=mcol_b[0:TAILS, 2:3]).then_inc(s["s1_taken"], 1)

            def mask_cols(b):
                if not (isinstance(b, int) and b == 0):
                    act.wait_ge(s["s1_taken"], 2 + 5 * GH * b)
                cp(mcol_b[:], mcol[:, bass.ds(b, 1), :].rearrange("p b c -> p (b c)")).then_inc(s["mc_done"], 1)
                act.wait_ge(s["mc_done"], b + 1)

            def results(b):
                act.wait_ge(s["pv1"], GH * b + GH)
                act.wait_ge(s["o1_done"], 1 + b)
                cp(o_raw, ps[:, 6, :]).then_inc(s["o1_copied"], 1)
                cp(rden[:], ps[:, 7, :]).then_inc(s["o1_copied"], 1)

            def unit1(b, i, more):
                u, z, hz = GH * b + i, GH * b + i + 2, (i + 2) % GH
                if i == 0:
                    mask_cols(b)
                exps1(u, i, 0)
                if i == 0 and not (isinstance(b, int) and b == 0):
                    results(b - 1)
                exps1(u, i, 1)
                exps1(u, i, 2)
                exps1(u, i, 3)
                if more > 1:
                    k1_split(z, hz)
                exps1(u, i, 4)
                if more > 1:
                    q1_split(z, hz)

            act.sem_inc(s["s1_taken"], 2)
            act.wait_ge(s["b_slots_done"], 1)
            q1_split(0, 0)
            copy_xnT(1, 2)
            k1_split(0, 0)
            copy_xnT(1, 3)
            q1_split(1, 1)
            k1_split(1, 1)
            unit1(0, 0, 2)
            unit1(0, 1, 2)
            with act.Fori(0, B - 1) as b:
                unit1(b, 2, 2)
                unit1(b, 3, 2)
                unit1(b + 1, 0, 2)
                unit1(b + 1, 1, 2)
            unit1(B - 1, 2, 1)
            unit1(B - 1, 3, 0)
            roots(4 * B)
            results(B - 1)

            for c in range(B):
                if c == B - 1:
                    roots(4 * B + 1)
                act.wait_ge(s["xt_done"], 2 * B + c + 1)
                cp(xnT_high[:, c * S:(c + 1) * S], ps[:, 4 + c, :]).then_inc(s["xnT_done"], 1)
                cp(xnT[:, c * S:(c + 1) * S], ps[:, 4 + c, :]).then_inc(s["xnT_done"], 1)
            gate_exp(1)

            def gelu(m, j):
                fn = F_TILES[j][1]
                act.wait_ge(s["g_done"], NF * m + j + 1)
                if not (isinstance(m, int) and m == 0):
                    act.wait_ge(s["h_done"], 1 + NF * m + j + 1 - NF)
                af(gg[0:fn, j, :], ps[0:fn, j, :], ACT.Gelu).then_inc(s["gelu_done"], 1)

            def gelus(m, last_one):
                for j in (1, 2):
                    fn = F_TILES[j][1]
                    act.wait_ge(s["g_done"], NF * m + j + 1)
                    act.wait_ge(s["h_done"], 1 + NF * m)
                    af(gg[0:fn, j, :], ps[0:fn, j, :], ACT.Gelu).then_inc(s["gelu_done"], 1)
                if not last_one:
                    gelu(m + 1, 0)

            gelu(0, 0)
            with act.Fori(0, E * B - UNITS, UNITS) as m0:
                for i in range(UNITS):
                    gelus(m0 + i, False)
            for i in range(UNITS):
                gelus(E * B - UNITS + i, i == UNITS - 1)

        @block.vector
        def _(dve):
            v = nc.vector
            tt, ts, tc, rd, stt = v.tensor_tensor, v.tensor_scalar, v.tensor_copy, v.tensor_reduce, v.scalar_tensor_tensor
            ln_n = [0]

            def norm_stats(srcs):
                for t, src in enumerate(srcs):
                    ins = v.bn_stats(stats[0:src.shape[0], t, :], src)
                link(dve, ins)
                for t, src in enumerate(srcs):
                    ins = v.bn_aggr(mv[0:src.shape[0], t, :], stats[0:src.shape[0], t, :])
                link(dve, ins)
                n = len(srcs)
                ts(mv[:, 0:n, 1], mv[:, 0:n, 1], EPS, None, ALU.add).then_inc(s["var_ready"], 1)

            def norm_apply(srcs, dsts, per_chunk=None):
                dve.wait_ge(s["sd_ready"], ln_n[0] + 1)
                ln_n[0] += 1
                n = len(srcs)
                link(dve, v.reciprocal(rstd[:, 0:n], sd[:, 0:n]))
                for t, (src, dst) in enumerate(zip(srcs, dsts)):
                    p = src.shape[0]
                    ins = ts(dst, src, mv[0:p, t, 0:1], rstd[0:p, t:t + 1], ALU.subtract, ALU.mult)
                    if per_chunk is not None and t % QT == QT - 1:
                        ins.then_inc(per_chunk, 1)
                return ins

            def x_and_xn(*chunks):
                tiles = [t for c in chunks for t in range(QT * c, QT * c + QT)]
                return [x[:, t, :] for t in tiles], [xn[:, t, :] for t in tiles]

            def norm_x(*chunks):
                norm_stats(x_and_xn(*chunks)[0])
                return norm_apply(*x_and_xn(*chunks), s["ln_ready"])

            for n in from_one["dve"]:
                dve.sem_inc(s[n], 1)

            v.memset(ones[:], 1.0)
            link(dve, v.memset(mv[:], 0.0))

            def first(b):
                tiles = range(QT * b, QT * b + QT)
                return ([x[:, t, :] for t in tiles] + [ctx_in[:, b, 0, :], ctx_in[0:CT, b, 1, :]],
                        [xn[:, t, :] for t in tiles] + [ctxn[:, b, 0, :], ctxn[0:CT, b, 1, :]])

            def second(b):
                return [xn[:, t, :] for t in range(QT * b, QT * b + QT)]

            def masks():
                dve.wait_ge(s["mask_loaded"], 16 * 6)
                tc(valid_m[:, 0, :], mask_i[:])
                tc(valid_m[:, 1, :], mask_t[:])
                link(dve, tc(valid_r, mask_r))
                ts(valid_m[:], valid_m[:], 0.0, None, ALU.not_equal)
                link(dve, ts(valid_r, valid_r, 0.0, None, ALU.not_equal))
                link(dve, rd(any_valid[:], valid_r, AX.X, ALU.max))
                for k in range(2):
                    ts(mcol[:, :, 2 * k], valid_m[:, k, :], 1.0 / DH1 ** 0.5, None, ALU.mult)
                    ts(mcol[:, :, 2 * k + 1], valid_m[:, k, :], -NEG, NEG, ALU.mult, ALU.add)
                link(dve, ts(valid_r[0:1], valid_r[0:1], -NEG, NEG, ALU.mult, ALU.add))
                for k in range(2):
                    tt(mcol[:, :, 2 * k + 1], mcol[:, :, 2 * k + 1], any_valid[:], ALU.mult)
                link(dve, tc(neg_row[:], valid_r[0:1]))

            def kvT_out(b):
                dve.wait_ge(s["tr_done"], b + 1)
                ts(kvT[:, b, C:KV0], ps[:, 5, :], cols[:, 2:3], cols[:, 3:4], ALU.mult, ALU.add)
                dve.wait_ge(s["ctxT_done"], b + 1)
                ts(kvT[:, b, 0:C], ps[:, 6, 0:C], cols[:, 0:1], cols[:, 1:2], ALU.mult, ALU.add).then_inc(s["kvT_done"], 1)

            PV, PR = 5, 7

            def q_lo(w, st):
                for h in range(2):
                    dve.wait_ge(s["q_hi"], 2 * w + h + 1)
                    tt(q_b[0:DH0, st, h, :], ps[DH0 * h:DH0 * h + DH0, PR, :], q_a[0:DH0, st, h, :].bitcast(F32),
                       ALU.subtract).then_inc(s["q_lo"], 1)

            def k_lo(w, st, c):
                n = KV0 // 2
                for h in range(2):
                    dve.wait_ge(s["k_hi"], 4 * w + 2 * c + h + 1)
                    tt(k_a[DH0:P, st, h, c * n:(c + 1) * n], ps[DH0 * h:DH0 * h + DH0, PR, 0:n],
                       k_a[0:DH0, st, h, c * n:(c + 1) * n].bitcast(F32), ALU.subtract).then_inc(s["k_lo"], 1)

            def take_max(w, j):
                h, t = divmod(j, QT)
                dve.wait_ge(s["max_scores"], 8 * w + j + 1)
                bank = 2 * (j % 2) if isinstance(w, int) and w == 0 else 0
                rd(nmax[:, h, t:t + 1], ps[:, bank:bank + 2, 0:KC], AX.XY, ALU.max, negate=True).then_inc(s["max_done"], 1)

            def v_first(w, st):
                dve.wait_ge(s["v_proj"], 2 * w + 1)
                tc(v0[:, st, 0:4, :], ps[:, PR, :].rearrange("p (t d) -> p t d", t=4)).then_inc(s["v_dve"], 1)

            def invert(u, part):
                c = slice(part * P, (part + 1) * P)
                dve.wait_ge(s["den_read"], 1 + u + 1)
                v.reciprocal(rden[:, c], rden[:, c]).then_inc(s["recip"], 1)

            def head_out(u, st, pair, b):
                dve.wait_ge(s["recip"], QT * u + QT)
                dve.wait_ge(s["pv_done"], u + 1)
                o = big[:, bass.ds(pair, 1), b * S:(b + 1) * S].rearrange("p a t -> p (a t)")
                tt(o, ps[:, PV + st, :], rden[:], ALU.mult).then_inc(s["head_done"], 1)

            def add_wo(c):
                dve.wait_ge(s["wo_done"], c + 1)
                tt(x[:, QT * c:QT * (c + 1), :], x[:, QT * c:QT * (c + 1), :],
                   ps[:, WO_BANKS[c], :].rearrange("p (t d) -> p t d", t=QT), ALU.add).then_inc(s["x1_done"], 1)
                dve.wait_ge(s["x1_done"], c + 1)

            def unit(u, i, pair, more):
                st, nst, w, z = i % 2, (i + 1) % 2, u + 1, u + 2
                if more > 0:
                    take_max(w, 7)
                if more > 1:
                    q_lo(z, st)
                if more > 1:
                    k_lo(z, st, 0)
                invert(u, 0)
                invert(u, 1)
                if more > 1:
                    k_lo(z, st, 1)
                    take_max(z, 0)
                    v_first(z, st)
                    take_max(z, 1)
                invert(u, 2)
                if more > 1:
                    take_max(z, 2)
                invert(u, 3)
                if more > 1:
                    take_max(z, 3)
                if more > 1:
                    take_max(z, 4)
                head_out(u, st, pair, i % B)
                if more > 1:
                    take_max(z, 5)
                    take_max(z, 6)

            dve.wait_ge(s["x_first"], 16)
            dve.wait_ge(s["ctx_loaded"], 32)
            norm_stats(first(0)[0])
            link(dve, norm_apply(*first(0)))
            norm_stats(second(0))
            norm_apply(second(0), second(0)).then_inc(s["lat_ready"], 1)
            dve.wait_ge(s["first_params"], 16 * N_FIRST)
            tc(identb[:], ident)
            tc(neg_place[:], consts[0:1, C_PLACE:C_PLACE + P])
            kvT_out(0)
            masks()
            q_lo(0, 0)
            dve.wait_ge(s["x_rest"], 16)
            norm_stats(first(1)[0])
            link(dve, norm_apply(*first(1)))
            k_lo(0, 0, 0)
            norm_stats(second(1))
            k_lo(0, 0, 1)
            norm_apply(second(1), second(1)).then_inc(s["lat_ready"], 1)
            v_first(0, 0)
            kvT_out(1)
            take_max(0, 0)
            norm_stats(first(2)[0])
            take_max(0, 1)
            link(dve, norm_apply(*first(2)))
            take_max(0, 2)
            norm_stats(second(2))
            take_max(0, 3)
            norm_apply(second(2), second(2)).then_inc(s["lat_ready"], 1)
            take_max(0, 4)
            kvT_out(2)
            take_max(0, 5)
            norm_stats(first(3)[0])
            take_max(0, 6)
            link(dve, norm_apply(*first(3)))
            take_max(0, 7)
            q_lo(1, 1)
            norm_stats(second(3))
            k_lo(1, 1, 0)
            norm_apply(second(3), second(3)).then_inc(s["lat_ready"], 1)
            kvT_out(3)
            k_lo(1, 1, 1)
            take_max(1, 0)
            v_first(1, 1)
            for j in range(1, 7):
                take_max(1, j)
            with dve.Fori(0, PAIRS - 2, 2) as p0:
                for i in range(UNITS):
                    unit(p0 * B + i, i, p0 + i // B, 2)
            for i in range(UNITS):
                if i == UNITS - 1:
                    dve.wait_ge(s["params_loaded"], 16 * N_PARAMS)
                    tt(b_slots[:], b_slots[:], fixed_rows.unsqueeze(2).broadcast_to([P, 2, GH]),
                       ALU.add).then_inc(s["b_slots_done"], 1)
                    add_wo(0)
                    dve.wait_ge(s["pv_done"], PAIRS * B)
                    dve.wait_ge(s["sum_step"], 2 * (NK - 1) * PAIRS * B)
                    norm_x(0)
                    add_wo(1)
                unit(PAIRS * B - UNITS + i, i, PAIRS - 2 + i // B, min(2, UNITS - 1 - i))
            norm_x(1)
            for c in (2, 3):
                add_wo(c)
                norm_x(c)

            def wide(col):
                return col[:].unsqueeze(2).broadcast_to([P, NT, E])

            def elements(row):
                return row.unsqueeze(1).broadcast_to([P, NT, E])

            def top2(stage, bias, renormalise):
                dve.wait_ge(s["logits_done"], stage + 1)
                z = ps[:, 1, 0:NT * E].rearrange("p (t e) -> p t e", e=E)
                if bias is not None:
                    link(dve, tt(lg[:], z, elements(bias), ALU.add))
                else:
                    link(dve, tc(lg[:], z))
                link(dve, rd(red[:], lg[:], AX.X, ALU.max))
                tt(lg[:], lg[:], wide(red), ALU.subtract).then_inc(s["logit_ready"], 1)
                dve.wait_ge(s["gate_exp"], stage + 1)
                link(dve, rd(red[:], gate[:], AX.X, ALU.add))
                link(dve, v.reciprocal(red[:], red[:]))
                link(dve, tt(gate[:], gate[:], wide(red), ALU.mult))
                link(dve, tc(g2[:], gate[:]))
                for k in range(2):
                    link(dve, rd(red[:], g2[:], AX.X, ALU.max))
                    link(dve, tt(eq[:], g2[:], wide(red), ALU.is_equal))
                    link(dve, tt(eq[:], eq[:], elements(expert_less_8), ALU.mult))
                    link(dve, rd(red[:], eq[:], AX.X, ALU.min))
                    link(dve, tt(eq[:], elements(expert_less_8), wide(red), ALU.is_equal))
                    if k == 0:
                        link(dve, tc(hot[:], eq[:]))
                        link(dve, stt(g2[:], eq[:], -2.0, g2[:], ALU.mult, ALU.add))
                    else:
                        link(dve, tt(hot[:], hot[:], eq[:], ALU.add))
                if renormalise:
                    link(dve, tt(hot[:], gate[:], hot[:], ALU.mult))
                    link(dve, rd(red[:], hot[:], AX.X, ALU.add))
                    link(dve, v.reciprocal(red[:], red[:]))
                    ins = tt(wgt[:], hot[:], wide(red), ALU.mult)
                else:
                    ins = tt(wgt[:], gate[:], hot[:], ALU.mult)
                ins.then_inc(s["w_done"], 1)
                dve.wait_ge(s["w_done"], stage + 1)

            top2(0, br[:], True)
            link(dve, rd(wsum[:], wgt[:], AX.X, ALU.add))
            for t in range(NT):
                ins = stt(x[:, t, :], xn[:, t, :], wsum[:, t:t + 1], x[:, t, :], ALU.mult, ALU.add)
            link(dve, ins)
            for c in range(B):
                dve.wait_ge(s["wb_done"], c + 1)
                dve.wait_ge(s["h_gelu"], c + 1)
                tt(hidden[:, c * S:(c + 1) * S], hidden[:, c * S:(c + 1) * S], ps[:, c, :], ALU.mult).then_inc(s["hw_done"], 1)
            for c in range(B):
                dve.wait_ge(s["up_done"], c + 1)
                tt(x[:, QT * c:QT * (c + 1), :], x[:, QT * c:QT * (c + 1), :],
                   ps[:, 4 + c, :].rearrange("p (t d) -> p t d", t=QT), ALU.add).then_inc(s["x2_done"], 1)
                dve.wait_ge(s["x2_done"], c + 1)
                norm_x(c)

            def q1_slots(z, h):
                dve.wait_ge(s["q1_split"], 2 * z + 2)
                if not (isinstance(z, int) and z < GH):
                    dve.wait_ge(s["s1"], 5 * (z - GH) + 5)
                stt(q_slots[:, h, :], q_high, low_slots[:, 0:1], q_full, ALU.mult, ALU.add).then_inc(s["q1_slots"], 1)

            def k1_slots(z, h):
                dve.wait_ge(s["k1_split"], 2 * z + 2)
                if not (isinstance(z, int) and z == 0):
                    dve.wait_ge(s["k1_diag"], 2 * z)
                stt(k_slots.bitcast(F32R), k_high, low_slots[:, 1:2], k_full, ALU.mult, ALU.add).then_inc(s["k1_slots"], 1)

            def v1_bias(z, h):
                dve.wait_ge(s["k1_split"], 2 * z + 2)
                if not (isinstance(z, int) and z < GH):
                    dve.wait_ge(s["pv1"], z - GH + 1)
                tt(vm[:, h, :], ps[:, 5, 160:160 + D], bv1[:, h, :], ALU.add).then_inc(s["v1_dve"], 1)
                tt(vt[0:TAILS, h, :], ps[0:TAILS, 5, 160 + D:160 + 2 * D], bv1[0:TAILS, h, :],
                   ALU.add).then_inc(s["v1_dve"], 1)

            def take_max1(w, t):
                dve.wait_ge(s["max1"], QT * w + t + 1)
                bank = 2 * (t % 2) if isinstance(w, int) and w == 0 else 0
                rd(nmax1[:, t, :].rearrange("p (g x) -> p g x", g=G1)[:, :, 0:1].rearrange("p (c g) x -> p c (g x)", c=2),
                   ps[:, bank:bank + 2, 0:2 * C].rearrange("p c (g k) -> p c g k", g=2), AX.X, ALU.max,
                   negate=True).then_inc(s["max1_taken"], 1)

            def q1_max(w, h):
                dve.wait_ge(s["rows1"], w + 1)
                dve.wait_ge(s["q1_slots"], w + 1)
                tt(q_slots[:, h, :], q_slots[:, h, :].bitcast(F32), ps[:, 4, :], ALU.add).then_inc(s["q1_max"], 1)

            def invert1(b, part):
                c = slice(part * P, (part + 1) * P)
                dve.wait_ge(s["o1_copied"], 2 * b + 2)
                v.reciprocal(rden[:, c], rden[:, c]).then_inc(s["recip1"], 1)

            def result1(b):
                dve.wait_ge(s["recip1"], QT * b + QT)
                tt(oT, o_raw, rden[:], ALU.mult).then_inc(s["o1_done"], 1)

            def add1(b):
                dve.wait_ge(s["wo1"], b + 1)
                dve.wait_ge(s["bo_added"], B)
                xb = x[:, bass.ds(b * QT, QT), :]
                tt(xb, xb, ps[:, 0, :].rearrange("p (t d) -> p t d", t=QT), ALU.add).then_inc(s["x3_done"], 1)

            def unit1(b, i, more):
                w, z, hw, hz = GH * b + i + 1, GH * b + i + 2, (i + 1) % GH, (i + 2) % GH
                ends = i < 2 and not (isinstance(b, int) and b == 0)
                for t in range(QT - 1 if more > 0 else 0):
                    take_max1(w, t)
                    if ends and t < 2:
                        invert1(b - 1, 2 * i + t)
                if more > 1:
                    v1_bias(z, hz)
                    k1_slots(z, hz)
                if ends and i == 1:
                    result1(b - 1)
                if more > 0:
                    take_max1(w, QT - 1)
                if more > 1:
                    q1_slots(z, hz)
                if ends and i == 1:
                    add1(b - 1)
                if more > 0:
                    q1_max(w, hw)

            v1_bias(0, 0)
            q1_slots(0, 0)
            k1_slots(0, 0)
            for t in range(QT):
                take_max1(0, t)
            q1_slots(1, 1)
            v1_bias(1, 1)
            q1_max(0, 0)
            k1_slots(1, 1)
            unit1(0, 0, 2)
            unit1(0, 1, 2)
            with dve.Fori(0, B - 1) as b:
                unit1(b, 2, 2)
                unit1(b, 3, 2)
                unit1(b + 1, 0, 2)
                unit1(b + 1, 1, 2)
            unit1(B - 1, 2, 1)
            dve.wait_ge(s["x3_done"], 1 + B - 1)
            norm_x(0, 1, 2)
            for part in range(QT):
                invert1(B - 1, part)
            result1(B - 1)
            add1(B - 1)

            dve.wait_ge(s["x3_done"], 1 + B)
            norm_x(3)
            link(dve, tt(acc, x[:], rows[:, 1:2, :].broadcast_to([P, NT, D]), ALU.add))
            for c in range(B):
                dve.wait_ge(s["xnT_done"], 2 * B + 2 * c + 2)
                tt(xnT_low[:, c * S:(c + 1) * S], ps[:, 4 + c, :], xnT_high[:, c * S:(c + 1) * S].bitcast(F32),
                   ALU.subtract).then_inc(s["xnT_low_done"], 1)
            top2(1, None, False)

            def h_prod(m, i, j):
                fn = F_TILES[j][1]
                dve.wait_ge(s["v_done"], NF * m + j + 1)
                dve.wait_ge(s["gelu_done"], 1 + NF * m + j + 1)
                tt(hid[0:fn, i % 2, j, :], gg[0:fn, j, :], ps[0:fn, 3 + j, :], ALU.mult).then_inc(s["h_done"], 1)

            def turn(m0, e0, last_turn):
                for i in range(UNITS):
                    m, c, par = m0 + i, i % B, i // B
                    h_prod(m, i, 1)
                    h_prod(m, i, 2)
                    if not (last_turn and i == UNITS - 1):
                        h_prod(m + 1, i + 1, 0)
                    if c == 0:
                        tc(wcol[:, par, :], wgt[:, :, bass.ds(e0 + par, 1)].rearrange("p t e -> p (t e)")).then_inc(s["r1_done"], 1)
                        dve.wait_ge(s["r1_done"], e0 + par + 1)
                    dve.wait_ge(s["down_done"], m + 1)
                    dve.wait_ge(s["acc_done"], 1 + m)
                    for t in range(QT):
                        o = acc[:, QT * c + t, :]
                        ins = stt(o, ps[:, 6 + i % 2, t * P:(t + 1) * P], wcol[:, par, QT * c + t:QT * c + t + 1], o,
                                  ALU.mult, ALU.add)
                    ins.then_inc(s["acc_done"], 1)

            h_prod(0, 0, 0)
            with dve.Fori(0, E - 2, 2) as e0:
                turn(e0 * B, e0, False)
            turn(E * B - UNITS, E - 2, True)

        @block.gpsimd
        def _(pool):
            g = nc.gpsimd
            g.memset(mask_t[:], 0).then_inc(s["pool_step"], 1)
            pool.wait_ge(s["pool_step"], 1)
            g.memset(k_b[DH0:DH0 + 1, :, :, :].bitcast(F32), 1.0).then_inc(s["pool_step"], 1)
            pool.wait_ge(s["pool_step"], 2)
            g.memset(nmax1[:], 0.0).then_inc(s["pool_step"], 1)

            def sums(u, st, kt):
                n = min(P, KV0 - kt * P)
                for h in range(2):
                    pool.wait_ge(s["scores_taken"], 3 + 2 * NK * u + 2 * kt + h + 1)
                    if kt > 1:
                        pool.wait_ge(s["sum_step"], 2 * (NK - 1) * u + 2 * (kt - 2) + h + 1)
                    first = prob[0:n, h, 0, :] if kt == 1 else psums[0:n, h, :]
                    ins = g.tensor_tensor(psums[0:n, h, :], first, prob[0:n, h, kt, :], ALU.add)
                    ins.then_inc(s["sum_step"], 1)

            def unit(u, i):
                for kt in range(1, NK):
                    sums(u, i % 2, kt)

            with pool.Fori(0, PAIRS * B, UNITS) as u0:
                for i in range(UNITS):
                    unit(u0 + i, i)

            def context1(b):
                if not (isinstance(b, int) and b == 0):
                    pool.wait_ge(s["kv1_proj"], GH * b)
                src = ctxT[:, bass.ds(b, 1), :].rearrange("p b c -> p (b c)")
                g.tensor_copy(cT[:, 0:P], src[:, 0:P])
                g.tensor_copy(cT[:, P:P + TAILS].rearrange("p (g c) -> p g c", g=G1),
                              src[:, P:C].unsqueeze(1).broadcast_to([P, G1, CT])).then_inc(s["ctx1_ready"], 1)

            def spread(z, h):
                pool.wait_ge(s["v1_dve"], 2 * z + 2)
                g.tensor_tensor(vt[0:TAILS, h, :], vt[0:TAILS, h, :], tails[0:TAILS, 0, :],
                                ALU.mult).then_inc(s["v1_pool"], 1)
                pool.wait_ge(s["k1_slots"], z + 1)
                if not (isinstance(z, int) and z < GH):
                    pool.wait_ge(s["s1"], 5 * (z - GH) + 5)
                g.tensor_tensor(k_diag[:, h, :, :], k_slots.unsqueeze(1).broadcast_to([P, G1, C]),
                                group_of_row.unsqueeze(2).broadcast_to([P, G1, C]), ALU.mult).then_inc(s["k1_diag"], 1)
                g.tensor_tensor(k_tails[:, h, :].rearrange("p (g c) -> p g c", g=G1),
                                k_slots[:, P:C].unsqueeze(1).broadcast_to([P, G1, CT]),
                                group_of_row.unsqueeze(2).broadcast_to([P, G1, CT]), ALU.mult).then_inc(s["k1_diag"], 1)

            pool.wait_ge(s["x2_done"], B)
            pool.wait_ge(s["second_loaded"], 16 * 5)
            context1(0)
            for z in range(GH):
                spread(z, z)
            pool.wait_ge(s["ln_ready"], 2 * B)
            for c in range(B):
                g.tensor_tensor(x[:, QT * c:QT * (c + 1), :], x[:, QT * c:QT * (c + 1), :],
                                rows[:, 0:1, :].broadcast_to([P, QT, D]), ALU.add).then_inc(s["bo_added"], 1)
            with pool.Fori(1, B) as b:
                context1(b)
                for h in range(GH):
                    spread(b * GH + h, h)

            def split(par):
                g.tensor_copy(we1_split[:, par, 0, :, :], we1[:, par, :, :]).then_inc(s["w_split"], 2)

            def split_low(e, par):
                pool.wait_ge(s["w_split"], 4 * e + 2)
                g.tensor_tensor(we1_split[:, par, 1, :, :], we1[:, par, :, :], we1_split[:, par, 0, :, :].bitcast(F32),
                                ALU.subtract).then_inc(s["w_split"], 2)

            for e, name in enumerate(["expert_even", "expert_odd"]):
                pool.wait_ge(s[name], 80)
                split(e)
                split_low(e, e)
            with pool.Fori(1, E // 2) as k:
                for par, name in enumerate(["expert_even", "expert_odd"]):
                    pool.wait_ge(s[name], k * 80 + 80)
                    pool.wait_ge(s["v_done"], k * (2 * NF * B) - (1 - par) * NF * B)
                    split(par)
                    split_low(k * 2 + par, par)


_INS = ["x", "ctx_1024", "mask_Bx1x1xS2_ik0", "L0_xattn_ln1_w", "L0_xattn_ln1_b", "L0_xattn_ln2_w", "L0_xattn_ln2_b",
        "L0_xattn_Wq", "L0_xattn_Wkv", "L0_xattn_Wo", "L0_ffn_Wr", "L0_ffn_br", "L0_ffn_Wd", "L0_ffn_bd", "L0_ffn_Wu",
        "L0_ffn_bu", "L1_xattn_Wo", "L1_xattn_bo", "L1_ffn_router_w", "L1_ffn_w1", "L1_ffn_v1", "L1_ffn_w2", "L1_ffn_bias"]


def in_slots(w):
    v = w.reshape(len(w), G1, GH, DH1).transpose(0, 2, 1, 3)[:, :, :, None, :]
    return np.concatenate([np.zeros_like(v), v, v, v], 3).reshape(len(w), GH, P)


def by_head(w):
    v = w.reshape(len(w), G1, GH, DH1)
    r = np.zeros((len(w), GH) + v.shape[1:], w.dtype)
    for h in range(GH):
        r[:, h, :, h, :] = v[:, :, h, :]
    return r.reshape(len(w), GH, P)


def kernel(**inputs):
    import concourse.bacc as _bacc
    from concourse.bass_utils import run_bass_kernel_spmd as _run

    nc = _bacc.Bacc("TRN2", target_bir_lowering=False, num_devices=1)
    arrays = {f"in_{n}_dram": np.ascontiguousarray(inputs[n]) for n in _INS}
    arrays["in_shape_consts_dram"] = constants()
    arrays["in_tail_consts_dram"] = tail_constants()
    wq, wk, wv, bq, bk, bv = (np.asarray(inputs["L1_xattn_" + n]) for n in ("Wq", "Wk", "Wv", "bq", "bk", "bv"))
    arrays["in_Wq_slots_dram"], arrays["in_Wk_slots_dram"] = in_slots(wq), in_slots(wk)
    arrays["in_b_slots_dram"] = np.ascontiguousarray(in_slots(np.stack([bq, bk])).transpose(2, 0, 1))
    arrays["in_Wv_heads_dram"] = by_head(wv)
    arrays["in_bv_heads_dram"] = by_head(bv[None]).reshape(-1)
    arrays["in_mask_by_key_dram"] = np.ascontiguousarray(np.asarray(inputs["mask_Bx1x1xS2_ik0"]).reshape(B, C).T)
    args = {n[3:-5]: nc.dram_tensor(n, v.shape, mybir.dt.from_np(v.dtype), kind="ExternalInput").ap()
            for n, v in arrays.items()}
    out = nc.dram_tensor("out_0_dram", (B, S, D), F32, kind="ExternalOutput").ap()
    build(nc, args, out)
    r = _run(nc, [arrays], core_ids=[0])
    return r.results[0]["out_0_dram"]
```
